# Optimizing a Trainium2 kernel written in Bass

```python
import numpy as np
import jax
import jax.numpy as jnp

def _softmax(x, axis=-1):
    return jax.nn.softmax(x, axis=axis)

def _gelu(x):
    return jax.nn.gelu(x, approximate=True)

def _silu(x):
    return jax.nn.silu(x)

def _sigmoid(x):
    return jax.nn.sigmoid(x)

def _layernorm(x, axis=-1, eps=1e-05):
    m = jnp.mean(x, axis=axis, keepdims=True)
    v = jnp.var(x, axis=axis, keepdims=True)
    return (x - m) / jnp.sqrt(v + eps)

def _scatter_add(tgt, idx, src, axis=0):
    return tgt.at[idx].add(src)

def _segment_sum(src, seg, n):
    return jax.ops.segment_sum(src, seg, n)
kernel_name = 'mk_seq_postln_d2_jaxref_r4_bf893b'

def setup_inputs(seed: int=0):
    np.random.seed(seed)
    _w = jnp.asarray

    def _L0_attn_setup():
        import jax, jax.numpy as jnp
        import numpy as np
        from jax import lax
        B, L, DM = (4, 128, 256)
        N_STATE = 16
        K_CONV = 4
        D_INNER = 2 * DM
        DT_RANK = (DM + 15) // 16
        DT_MIN, DT_MAX = (0.001, 0.1)
        key = jax.random.key(seed)
        ks = jax.random.split(key, 10)
        x = jax.random.normal(ks[0], (B, L, DM), dtype=jnp.float32)
        s = 0.02
        W_in = jax.random.normal(ks[1], (2 * D_INNER, DM), dtype=jnp.float32) * s
        conv_w = jax.random.normal(ks[2], (D_INNER, 1, K_CONV), dtype=jnp.float32) * 0.3
        conv_b = jnp.zeros((D_INNER,), dtype=jnp.float32)
        W_x = jax.random.normal(ks[3], (DT_RANK + 2 * N_STATE, D_INNER), dtype=jnp.float32) * s
        W_dt = jax.random.normal(ks[4], (D_INNER, DT_RANK), dtype=jnp.float32) * DT_RANK ** (-0.5)
        dt = jnp.exp(jax.random.uniform(ks[5], (D_INNER,), dtype=jnp.float32) * (np.log(DT_MAX) - np.log(DT_MIN)) + np.log(DT_MIN))
        dt = jnp.clip(dt, DT_MIN, None)
        b_dt = dt + jnp.log(-jnp.expm1(-dt))
        A_log = jnp.broadcast_to(jnp.log(jnp.arange(1, N_STATE + 1, dtype=jnp.float32)), (D_INNER, N_STATE)).copy()
        D_param = jnp.ones((D_INNER,), dtype=jnp.float32)
        W_out = jax.random.normal(ks[6], (DM, D_INNER), dtype=jnp.float32) * s
        return {'x': x, 'W_in': W_in, 'conv_w': conv_w, 'conv_b': conv_b, 'W_x': W_x, 'W_dt': W_dt, 'b_dt': b_dt, 'A_log': A_log, 'D_param': D_param, 'W_out': W_out}
    _L0_attn_in = _L0_attn_setup()

    def _L0_ffn_setup():
        import jax, jax.numpy as jnp
        import numpy as np
        B, T, D, R, E = (32, 256, 256, 64, 8)
        key = jax.random.key(seed)
        ks = jax.random.split(key, 12)
        inp = {}
        inp['x'] = jax.random.normal(ks[0], (B, T, D), dtype=jnp.float32)
        inp['base_W'] = jax.random.normal(ks[1], (D, D), dtype=jnp.float32) * (1.0 / np.sqrt(D))
        inp['base_b'] = jax.random.normal(ks[2], (D,), dtype=jnp.float32) * 0.01
        inp['disc_mu'] = jax.random.normal(ks[3], (E, D), dtype=jnp.float32) * 0.5
        inp['disc_sigma'] = jax.random.uniform(ks[4], (E, D), dtype=jnp.float32, minval=0.5, maxval=1.5)
        inp['down_W'] = jax.random.normal(ks[5], (E, D, R), dtype=jnp.float32) * (1.0 / np.sqrt(D))
        inp['down_b'] = jax.random.normal(ks[6], (E, R), dtype=jnp.float32) * 0.01
        inp['up_W'] = jax.random.normal(ks[7], (E, R, D), dtype=jnp.float32) * (1.0 / np.sqrt(R))
        inp['up_b'] = jax.random.normal(ks[8], (E, D), dtype=jnp.float32) * 0.01
        inp['conv_W'] = jax.random.normal(ks[9], (E, D, D), dtype=jnp.float32) * 0.02
        inp['conv_b'] = jax.random.normal(ks[10], (E, D), dtype=jnp.float32) * 0.01
        return inp
    _L0_ffn_in = _L0_ffn_setup()

    def _L1_attn_setup():
        import jax, jax.numpy as jnp
        import numpy as np
        D_MODEL = 256
        NUM_HEADS = 16
        B, S = (1, 1024)
        key = jax.random.key(seed)
        kx, kq, kk, kv, ko = jax.random.split(key, 5)
        std = (1.0 / D_MODEL) ** 0.5

        def trunc(k):
            return std * jax.random.truncated_normal(k, -3.0, 3.0, (D_MODEL, D_MODEL), dtype=jnp.float32)
        return {'x': jax.random.normal(kx, (B, S, D_MODEL), dtype=jnp.float32), 'W_Q': trunc(kq), 'W_K': trunc(kk), 'W_V': trunc(kv), 'W_O': trunc(ko)}
    _L1_attn_in = _L1_attn_setup()

    def _L1_ffn_setup():
        import jax, jax.numpy as jnp
        import numpy as np
        E, D, F = (8, 256, 1024)
        B, S = (4, 512)

        def _layernorm(x, g, b, eps=1e-05):
            mu = jnp.mean(x, axis=-1, keepdims=True)
            var = jnp.var(x, axis=-1, keepdims=True)
            return (x - mu) * jax.lax.rsqrt(var + eps) * g + b
        key = jax.random.key(seed)
        ks = jax.random.split(key, 5)
        return {'input_features': jax.random.normal(ks[0], (B, S, D), jnp.float32), 'centroids': jax.random.normal(ks[1], (E, D), jnp.float32) * 0.1, 'ln_g': jnp.ones((E, D), jnp.float32), 'ln_b': jnp.zeros((E, D), jnp.float32), 'w1': jax.random.normal(ks[2], (E, F, D), jnp.float32) * (1.0 / np.sqrt(D).astype(np.float32)), 'b1': jnp.zeros((E, F), jnp.float32), 'w2': jax.random.normal(ks[3], (E, D, F), jnp.float32) * (1.0 / np.sqrt(F).astype(np.float32)), 'b2': jnp.zeros((E, D), jnp.float32)}
    _L1_ffn_in = _L1_ffn_setup()
    _d = {'L0_attn_x': _L0_attn_in['x'], 'L0_attn_W_in': _L0_attn_in['W_in'], 'L0_attn_conv_w': _L0_attn_in['conv_w'], 'L0_attn_conv_b': _L0_attn_in['conv_b'], 'L0_attn_W_x': _L0_attn_in['W_x'], 'L0_attn_W_dt': _L0_attn_in['W_dt'], 'L0_attn_b_dt': _L0_attn_in['b_dt'], 'L0_attn_A_log': _L0_attn_in['A_log'], 'L0_attn_D_param': _L0_attn_in['D_param'], 'L0_attn_W_out': _L0_attn_in['W_out'], 'L0_ffn_base_W': _L0_ffn_in['base_W'], 'L0_ffn_base_b': _L0_ffn_in['base_b'], 'L0_ffn_disc_mu': _L0_ffn_in['disc_mu'], 'L0_ffn_disc_sigma': _L0_ffn_in['disc_sigma'], 'L0_ffn_down_W': _L0_ffn_in['down_W'], 'L0_ffn_down_b': _L0_ffn_in['down_b'], 'L0_ffn_up_W': _L0_ffn_in['up_W'], 'L0_ffn_up_b': _L0_ffn_in['up_b'], 'L0_ffn_conv_W': _L0_ffn_in['conv_W'], 'L0_ffn_conv_b': _L0_ffn_in['conv_b'], 'L1_attn_W_Q': _L1_attn_in['W_Q'], 'L1_attn_W_K': _L1_attn_in['W_K'], 'L1_attn_W_V': _L1_attn_in['W_V'], 'L1_attn_W_O': _L1_attn_in['W_O'], 'L1_ffn_centroids': _L1_ffn_in['centroids'], 'L1_ffn_ln_g': _L1_ffn_in['ln_g'], 'L1_ffn_ln_b': _L1_ffn_in['ln_b'], 'L1_ffn_w1': _L1_ffn_in['w1'], 'L1_ffn_b1': _L1_ffn_in['b1'], 'L1_ffn_w2': _L1_ffn_in['w2'], 'L1_ffn_b2': _L1_ffn_in['b2']}
    _x0 = _d['L0_attn_x']
    _d['L0_attn_x'] = jax.random.normal(jax.random.fold_in(jax.random.key(seed), 1), (1, 4096, 256), dtype=_x0.dtype)
    del _x0
    return _d

def reference(L0_attn_x, L0_attn_W_in, L0_attn_conv_w, L0_attn_conv_b, L0_attn_W_x, L0_attn_W_dt, L0_attn_b_dt, L0_attn_A_log, L0_attn_D_param, L0_attn_W_out, L0_ffn_base_W, L0_ffn_base_b, L0_ffn_disc_mu, L0_ffn_disc_sigma, L0_ffn_down_W, L0_ffn_down_b, L0_ffn_up_W, L0_ffn_up_b, L0_ffn_conv_W, L0_ffn_conv_b, L1_attn_W_Q, L1_attn_W_K, L1_attn_W_V, L1_attn_W_O, L1_ffn_centroids, L1_ffn_ln_g, L1_ffn_ln_b, L1_ffn_w1, L1_ffn_b1, L1_ffn_w2, L1_ffn_b2):

    def _L0_attn_ref(x, W_in, conv_w, conv_b, W_x, W_dt, b_dt, A_log, D_param, W_out):
        import jax, jax.numpy as jnp
        import numpy as np
        from jax import lax
        B, L, DM = (4, 128, 256)
        N_STATE = 16
        K_CONV = 4
        D_INNER = 2 * DM
        DT_RANK = (DM + 15) // 16
        DT_MIN, DT_MAX = (0.001, 0.1)
        Bb, Ll, Dm = x.shape
        d_inner = conv_b.shape[0]
        k = conv_w.shape[-1]
        n = A_log.shape[1]
        dt_rank = W_dt.shape[1]
        xz = x @ W_in.T
        xp, z = jnp.split(xz, 2, axis=-1)
        u = xp.transpose(0, 2, 1)
        u = lax.conv_general_dilated(u, conv_w, window_strides=(1,), padding=[(k - 1, 0)], dimension_numbers=('NCH', 'OIH', 'NCH'), feature_group_count=d_inner)
        u = u + conv_b[None, :, None]
        u = jax.nn.silu(u.transpose(0, 2, 1))
        x_dbl = u @ W_x.T
        dlt, Bm, Cm = jnp.split(x_dbl, [dt_rank, dt_rank + n], axis=-1)
        delta = jax.nn.softplus(dlt @ W_dt.T + b_dt)
        A = -jnp.exp(A_log)
        deltaA = jnp.exp(jnp.einsum('bld,dn->bldn', delta, A))
        dBu = jnp.einsum('bld,bln,bld->bldn', delta, Bm, u)

        def step(state, inp):
            dA_t, dBu_t, C_t = inp
            state = dA_t * state + dBu_t
            y_t = jnp.einsum('bdn,bn->bd', state, C_t)
            return (state, y_t)
        init = jnp.zeros((Bb, d_inner, n), dtype=x.dtype)
        _, ys = lax.scan(step, init, (deltaA.transpose(1, 0, 2, 3), dBu.transpose(1, 0, 2, 3), Cm.transpose(1, 0, 2)))
        y = ys.transpose(1, 0, 2) + u * D_param
        y = y * jax.nn.silu(z)
        return y @ W_out.T

    def _L0_ffn_ref(x, base_W, base_b, disc_mu, disc_sigma, down_W, down_b, up_W, up_b, conv_W, conv_b):
        import jax, jax.numpy as jnp
        import numpy as np
        B, T, D, R, E = (32, 256, 256, 64, 8)
        base = jnp.einsum('btd,od->bto', x, base_W) + base_b
        m1 = x.mean(axis=1)
        m2 = (x * x).mean(axis=1)
        inv_var = 1.0 / (disc_sigma * disc_sigma)
        losses = (jnp.einsum('bd,ed->eb', m2, inv_var) - 2.0 * jnp.einsum('bd,ed->eb', m1, disc_mu * inv_var) + jnp.sum(disc_mu * disc_mu * inv_var, axis=1)[:, None]) / D
        idx = jnp.argmin(losses, axis=0)
        Wd, bd = (down_W[idx], down_b[idx])
        Wu, bu = (up_W[idx], up_b[idx])
        Wc, bc = (conv_W[idx], conv_b[idx])
        h = jax.nn.relu(jnp.einsum('btd,bdr->btr', x, Wd) + bd[:, None, :])
        a = jnp.einsum('btr,brd->btd', h, Wu) + bu[:, None, :]
        y = jnp.einsum('btd,bod->bto', a, Wc) + bc[:, None, :]
        return base + y

    def _L1_attn_ref(x, W_Q, W_K, W_V, W_O):
        import jax, jax.numpy as jnp
        import numpy as np
        D_MODEL = 256
        NUM_HEADS = 16
        B, S = (1, 1024)
        Bx, Sx, Dm = x.shape
        H = NUM_HEADS
        d_attn = Dm // H
        Q = x @ W_Q.T
        K = x @ W_K.T
        V = x @ W_V.T
        Q = Q.reshape(Bx, Sx, H, d_attn).transpose(0, 2, 1, 3)
        K = K.reshape(Bx, Sx, H, d_attn).transpose(0, 2, 1, 3)
        V = V.reshape(Bx, Sx, H, d_attn).transpose(0, 2, 1, 3)
        scale = 1.0 / jnp.sqrt(jnp.asarray(d_attn, dtype=x.dtype))
        attn = jnp.einsum('bhqd,bhkd->bhqk', Q, K) * scale
        causal = jnp.tril(jnp.ones((Sx, Sx), dtype=bool))
        attn = jnp.where(causal, attn, jnp.asarray(-jnp.inf, dtype=attn.dtype))
        probs = jax.nn.softmax(attn, axis=-1)
        y = jnp.einsum('bhqk,bhkd->bhqd', probs, V)
        y = y.transpose(0, 2, 1, 3).reshape(Bx, Sx, Dm)
        return y @ W_O.T

    def _L1_ffn_ref(input_features, centroids, ln_g, ln_b, w1, b1, w2, b2):
        import jax, jax.numpy as jnp
        import numpy as np
        E, D, F = (8, 256, 1024)
        B, S = (4, 512)

        def _layernorm(x, g, b, eps=1e-05):
            mu = jnp.mean(x, axis=-1, keepdims=True)
            var = jnp.var(x, axis=-1, keepdims=True)
            return (x - mu) * jax.lax.rsqrt(var + eps) * g + b
        Bf, Sf, Df = input_features.shape
        x = input_features.reshape(-1, Df)
        aff = x @ centroids.T
        assign = jnp.argmax(aff, axis=1)
        order = jnp.argsort(assign)
        xs = x[order]
        es = assign[order]
        alpha = jax.nn.sigmoid(jnp.take_along_axis(aff[order], es[:, None], axis=1))
        nE = centroids.shape[0]
        y = jnp.zeros_like(xs)
        for e in range(nE):
            h = _layernorm(xs, ln_g[e], ln_b[e])
            h = jax.nn.relu(h @ w1[e].T + b1[e])
            ye = xs + h @ w2[e].T + b2[e]
            y = y + jnp.where((es == e)[:, None], ye, 0.0)
        out_sorted = alpha * y + (1.0 - alpha) * xs
        inv = jnp.argsort(order)
        return out_sorted[inv].reshape(Bf, Sf, Df)
    x = L0_attn_x
    x = _layernorm(x + _L0_attn_ref(x, L0_attn_W_in, L0_attn_conv_w, L0_attn_conv_b, L0_attn_W_x, L0_attn_W_dt, L0_attn_b_dt, L0_attn_A_log, L0_attn_D_param, L0_attn_W_out), axis=-1)
    x = _layernorm(x + _L0_ffn_ref(x, L0_ffn_base_W, L0_ffn_base_b, L0_ffn_disc_mu, L0_ffn_disc_sigma, L0_ffn_down_W, L0_ffn_down_b, L0_ffn_up_W, L0_ffn_up_b, L0_ffn_conv_W, L0_ffn_conv_b), axis=-1)
    x = _layernorm(x + _L1_attn_ref(x, L1_attn_W_Q, L1_attn_W_K, L1_attn_W_V, L1_attn_W_O), axis=-1)
    x = _layernorm(x + _L1_ffn_ref(x, L1_ffn_centroids, L1_ffn_ln_g, L1_ffn_ln_b, L1_ffn_w1, L1_ffn_b1, L1_ffn_w2, L1_ffn_b2), axis=-1)
    return x

_drawn_inputs = setup_inputs


def setup_inputs(seed=0):
    import zlib

    import numpy as np

    out = dict(_drawn_inputs(seed))
    spreads = {'L0_attn_conv_b': (0.0, 0.352),
     'L0_attn_D_param': (1.0, 0.6),
     'L1_ffn_ln_g': (1.0, 0.2),
     'L1_ffn_ln_b': (0.0, 0.272),
     'L1_ffn_b1': (0.0, 0.267),
     'L1_ffn_b2': (0.0, 0.1)}
    factors = {'L0_attn_W_x': 31.848,
     'L0_attn_W_dt': 8.0,
     'L0_attn_b_dt': 38.242,
     'L0_attn_A_log': 28.063,
     'L0_ffn_down_b': 4.99,
     'L0_ffn_up_b': 3.128}
    for name, (base, spread) in spreads.items():
        noise = np.random.default_rng([zlib.crc32(name.encode()), seed]).standard_normal(out[name].shape)
        drawn = base * np.exp(spread * noise) if base else spread * noise
        out[name] = jnp.asarray(drawn.astype(out[name].dtype))
    for name, factor in factors.items():
        out[name] = (out[name] * factor).astype(out[name].dtype)
    return out
```

```python
from contextlib import ExitStack

import concourse.bass as bass
from concourse import mybir

F32 = mybir.dt.float32
BF16 = mybir.dt.bfloat16
I32 = mybir.dt.int32
U32 = mybir.dt.uint32
ALU = mybir.AluOpType
ACT = mybir.ActivationFunctionType
AXX = mybir.AxisListType.X

P = 128
L = 4096
DM = 256
KD = DM // P
DI = 512
ND = DI // P
NS = 16
RK = 16
KC = 4
TC = 512
NC = L // TC
TT = L // P
JT = TC // P
EPS = 1e-5


PRIMED = 1


def prime(sp, sems):
    for sem in sems:
        sp.sem_inc(sem, PRIMED)


class Mem:

    def __init__(self, nc):
        self.nc, self.stack, self.sems = nc, ExitStack(), []

    def __enter__(self):
        self.stack.__enter__()
        return self

    def __exit__(self, *a):
        return self.stack.__exit__(*a)

    def sb(self, name, shape, dt=F32):
        return self.stack.enter_context(self.nc.sbuf_tensor(name, shape, dt))

    def ps(self, name, shape, dt=F32):
        return self.stack.enter_context(self.nc.psum_tensor(name, shape, dt))

    def sem(self, name):
        self.sems.append(self.stack.enter_context(self.nc.semaphore(name)))
        return self.sems[-1]

    def clear_sems(self):
        with self.nc.Block() as block:
            @block.gpsimd
            def _(pool):
                pool.sem_clear(range(self.sems[0].num, self.sems[-1].num + 1))


def mixer_front(nc, S, D, keep):
    bc_parts = keep["bc_parts"]
    with Mem(nc) as m:
        xT = m.sb("s1_xT", [P, KD, L])
        w_in = m.sb("s1_w_in", [P, KD, 2 * DI])
        w_x = m.sb("s1_w_x", [P, ND, RK + 2 * NS])
        w_dt = m.sb("s1_w_dt", [RK, DI])
        vecs = m.sb("s1_vecs", [P, ND, KC + 2])
        xp = m.sb("s1_xp", [P, ND, KC - 1 + TC])
        conv = m.sb("s1_conv", [P, ND, TC])
        u = m.sb("s1_u", [P, ND, TC])
        sz = m.sb("s1_sz", [P, ND, TC])
        dlt = m.sb("s1_dlt", [RK, TC])
        bc_rest = m.sb("s1_bc_rest", [2 * NS, TC])
        bc_mid = m.sb("s1_bc_mid", [2 * NS, TC], BF16)
        absv = m.sb("s1_absv", [P, ND, TC])
        ex = m.sb("s1_ex", [P, ND, TC])
        ex1 = m.sb("s1_ex1", [P, ND, TC])
        lost = m.sb("s1_lost", [P, ND, TC])
        lnv = m.sb("s1_lnv", [P, ND, TC])
        relu = m.sb("s1_relu", [P, ND, TC])
        delta = m.sb("s1_delta", [P, ND, TC])
        p_proj = [m.ps(f"s1_p_proj{i}", [P, TC]) for i in range(4)]
        p_x = m.ps("s1_p_x", [P, TC])
        p_dt = [m.ps(f"s1_p_dt{i}", [P, TC]) for i in range(2)]

        loaded, rest_loaded, zeroed = S("loaded"), S("rest_loaded"), S("history_zeroed")
        xp_shifted = S("xp_shifted")
        proj_ready, xp_ready, conv_step, conv_ready = S("proj_ready"), S("xp_ready"), S("conv_step"), S("conv_ready")
        z_ready, u_ready, xdbl_ready = S("z_ready"), S("u_ready"), S("xdbl_ready")
        hi_ready, rest_ready, mid_ready, low_ready = S("hi_ready"), S("rest_ready"), S("mid_ready"), S("low_ready")
        dlt_ready, dt_ready, abs_ready, relu_ready = S("dlt_ready"), S("dt_ready"), S("abs_ready"), S("relu_ready")
        ex_ready, ex1_ready, lost_ready, ln_ready = S("ex_ready"), S("ex1_ready"), S("lost_ready"), S("ln_ready")
        log1p_ready, delta_ready = S("log1p_ready"), S("delta_ready")
        z_out = [S(f"z_out{d}") for d in range(ND)]
        u_out = [S(f"u_out{d}") for d in range(ND)]
        delta_out = [S(f"delta_out{d}") for d in range(ND)]
        LOADS = 5
        Z0, U0, CONV0, RELU0 = ND, ND, ND, 2

        with nc.Block() as block:
            @block.sync
            def _(sp):
                prime(sp, [dlt_ready, rest_ready, xdbl_ready, dt_ready, low_ready, delta_ready, *z_out, *u_out, *delta_out])
                x_from = D["xT"].rearrange("(k p) n -> p k n", p=P)
                sp.dma_start(w_in[:], D["w_in"].rearrange("(k p) n -> p k n", p=P)).then_inc(loaded, 16)
                sp.dma_start(xT[:, :, 0:TC], x_from[:, :, 0:TC]).then_inc(loaded, 16)
                sp.dma_start(vecs[:], D["mixer_vecs"].rearrange("(k p) n -> p k n", p=P)).then_inc(loaded, 16)
                sp.dma_start(w_x[:], D["w_x"].rearrange("(k p) n -> p k n", p=P)).then_inc(loaded, 16)
                sp.dma_start(w_dt[:], D["w_dt"]).then_inc(loaded, 16)
                sp.dma_start(xT[:, :, TC:L], x_from[:, :, TC:L]).then_inc(rest_loaded, 16)
                with sp.Fori(0, NC) as c:
                    for d in range(ND):
                        sp.wait_ge(z_ready, c * ND + (Z0 + d + 1))
                        sp.dma_start(D["sz"][d * P:(d + 1) * P, bass.ds(c * TC, TC)], sz[:, d, :]).then_inc(z_out[d], 16)
                        sp.wait_ge(u_ready, c * ND + (U0 + d + 1))
                        sp.dma_start(D["u"][d * P:(d + 1) * P, bass.ds(c * TC, TC)], u[:, d, :]).then_inc(u_out[d], 16)
                    for d in range(ND):
                        sp.wait_ge(delta_ready, PRIMED + c * ND + (d + 1))
                        sp.dma_start(D["delta"][d * P:(d + 1) * P, bass.ds(c * TC, TC)],
                                     delta[:, d, :]).then_inc(delta_out[d], 16)
                for d in range(ND):
                    sp.wait_ge(z_out[d], PRIMED + 16 * NC)
                    sp.wait_ge(u_out[d], PRIMED + 16 * NC)
                    sp.wait_ge(delta_out[d], PRIMED + 16 * NC)

            @block.tensor
            def _(pe):
                pe.wait_ge(loaded, 16 * LOADS)
                with pe.Fori(0, NC) as c:
                    for n in range(2 * ND):
                        if n < ND:
                            pe.wait_ge(z_ready, c * ND + (n + 1))
                        else:
                            pe.wait_ge(xp_ready, c * ND + (n - ND + 1))
                        for k in range(KD):
                            mm = nc.tensor.matmul(p_proj[n % ND][:], w_in[:, k, n * P:(n + 1) * P],
                                                  xT[:, k, bass.ds(c * TC, TC)], start=k == 0, stop=k == KD - 1)
                        mm.then_inc(proj_ready, 1)
                    pe.wait_ge(rest_loaded, 16)
                    pe.wait_ge(dlt_ready, PRIMED + c)
                    pe.wait_ge(rest_ready, PRIMED + c)
                    for k in range(ND):
                        pe.wait_ge(u_ready, c * ND + (U0 + k + 1))
                        mm = nc.tensor.matmul(p_x[0:RK + 2 * NS, :], w_x[:, k, :], u[:, k, :],
                                              start=k == 0, stop=k == ND - 1)
                    mm.then_inc(xdbl_ready, 1)
                    pe.wait_ge(dlt_ready, PRIMED + c + 1)
                    for d in range(ND):
                        pe.wait_ge(relu_ready, c * ND + (d + 1))
                        nc.tensor.matmul(p_dt[d % 2][:], w_dt[:, d * P:(d + 1) * P], dlt[:],
                                         start=True, stop=True).then_inc(dt_ready, 1)

            @block.scalar
            def _(act):
                act.sem_inc(z_ready, Z0)
                act.sem_inc(u_ready, U0)
                act.sem_inc(relu_ready, RELU0)
                act.wait_ge(loaded, 16 * LOADS)
                act.wait_ge(zeroed, 1)
                with act.Fori(0, NC) as c:
                    for d in range(ND):
                        act.wait_ge(conv_ready, c * ND + (d + 1))
                        nc.scalar.copy(xp[:, d, 0:KC - 1], xp[:, d, TC:TC + KC - 1]).then_inc(xp_shifted, 1)
                        act.wait_ge(proj_ready, c * (2 * ND) + (d + 1))
                        act.wait_ge(xp_shifted, c * ND + (d + 1))
                        nc.scalar.copy(xp[:, d, KC - 1:], p_proj[d][:]).then_inc(xp_ready, 1)
                    act.wait_ge(xdbl_ready, PRIMED + c)
                    for d in range(ND):
                        act.wait_ge(proj_ready, c * (2 * ND) + (ND + d + 1))
                        act.wait_ge(z_out[d], PRIMED + c * 16)
                        nc.scalar.activation(sz[:, d, :], p_proj[d][:], ACT.Silu).then_inc(z_ready, 1)
                        act.wait_ge(conv_ready, c * ND + (CONV0 + d + 1))
                        act.wait_ge(u_out[d], PRIMED + c * 16)
                        nc.scalar.activation(u[:, d, :], conv[:, d, :], ACT.Silu,
                                             bias=vecs[:, d, KC:KC + 1]).then_inc(u_ready, 1)
                    act.wait_ge(xdbl_ready, PRIMED + c + 1)
                    act.wait_ge(dt_ready, PRIMED + c * ND)
                    nc.scalar.copy(bc_parts[0:2 * NS, bass.ds(c * TC, TC)], p_x[0:2 * NS, :]).then_inc(hi_ready, 1)
                    nc.scalar.copy(dlt[:], p_x[2 * NS:2 * NS + RK, :]).then_inc(dlt_ready, 1)
                    act.wait_ge(rest_ready, PRIMED + c + 1)
                    act.wait_ge(low_ready, PRIMED + c)
                    nc.scalar.copy(bc_mid[:], bc_rest[:]).then_inc(mid_ready, 1)
                    act.wait_ge(mid_ready, c + 1)
                    nc.scalar.copy(bc_parts[2 * NS:4 * NS, bass.ds(c * TC, TC)], bc_mid[:])
                    act.wait_ge(delta_ready, PRIMED + c * ND)
                    for d in range(ND):
                        act.wait_ge(dt_ready, PRIMED + c * ND + (d + 1))
                        nc.scalar.activation(absv[:, d, :], p_dt[d % 2][:], ACT.Abs,
                                             bias=vecs[:, d, KC + 1:KC + 2]).then_inc(abs_ready, 1)
                        nc.scalar.activation(relu[:, d, :], p_dt[d % 2][:], ACT.Relu,
                                             bias=vecs[:, d, KC + 1:KC + 2]).then_inc(relu_ready, 1)
                        act.wait_ge(abs_ready, c * ND + (d + 1))
                        nc.scalar.activation(ex[:, d, :], absv[:, d, :], ACT.Exp, scale=-1.0).then_inc(ex_ready, 1)
                    for d in range(ND):
                        act.wait_ge(ex1_ready, c * ND + (d + 1))
                        nc.scalar.activation(lnv[:, d, :], ex1[:, d, :], ACT.Ln).then_inc(ln_ready, 1)

            @block.vector
            def _(dve):
                dve.sem_inc(conv_ready, CONV0)
                nc.vector.memset(xp[:], 0.0).then_inc(zeroed, 1)
                dve.wait_ge(loaded, 16 * LOADS)
                with dve.Fori(0, NC) as c:
                    for d in range(ND):
                        dve.wait_ge(xp_ready, c * ND + (d + 1))
                        dve.wait_ge(u_ready, c * ND + (d + 1))
                        nc.vector.tensor_scalar(conv[:, d, :], xp[:, d, 0:TC], vecs[:, d, 0:1], None,
                                                ALU.mult).then_inc(conv_step, 1)
                        for k in range(1, KC):
                            dve.wait_ge(conv_step, (c * ND + d) * (KC - 1) + k)
                            nc.vector.scalar_tensor_tensor(
                                out=conv[:, d, :], in0=xp[:, d, k:k + TC], scalar=vecs[:, d, k:k + 1],
                                in1=conv[:, d, :], op0=ALU.mult, op1=ALU.add,
                            ).then_inc(conv_step if k < KC - 1 else conv_ready, 1)
                    dve.wait_ge(hi_ready, c + 1)
                    nc.vector.tensor_tensor(bc_rest[:], p_x[0:2 * NS, :], bc_parts[0:2 * NS, bass.ds(c * TC, TC)],
                                            ALU.subtract).then_inc(rest_ready, 1)
                    dve.wait_ge(mid_ready, c + 1)
                    nc.vector.tensor_tensor(bc_parts[4 * NS:6 * NS, bass.ds(c * TC, TC)], bc_rest[:], bc_mid[:],
                                            ALU.subtract).then_inc(low_ready, 1)
                    for d in range(ND):
                        dve.wait_ge(ex_ready, c * ND + (d + 1))
                        nc.vector.tensor_scalar(ex1[:, d, :], ex[:, d, :], 1.0, None, ALU.add).then_inc(ex1_ready, 1)
                        dve.wait_ge(ex1_ready, c * ND + (d + 1))
                        nc.vector.scalar_tensor_tensor(out=lost[:, d, :], in0=ex1[:, d, :], scalar=-1.0,
                                                       in1=ex[:, d, :], op0=ALU.add,
                                                       op1=ALU.subtract).then_inc(lost_ready, 1)
                    for d in range(ND):
                        dve.wait_ge(ln_ready, c * ND + (d + 1))
                        dve.wait_ge(lost_ready, c * ND + (d + 1))
                        nc.vector.tensor_tensor(lost[:, d, :], lnv[:, d, :], lost[:, d, :],
                                                ALU.subtract).then_inc(log1p_ready, 1)
                        dve.wait_ge(log1p_ready, c * ND + (d + 1))
                        dve.wait_ge(delta_out[d], PRIMED + c * 16)
                        nc.vector.tensor_tensor(delta[:, d, :], lost[:, d, :], relu[:, d, :],
                                                ALU.add).then_inc(delta_ready, 1)


def set_identity(pool, tile, cleared, done):
    n = tile.shape[0]
    nc_pool = pool
    nc_pool.memset(tile[:], 0.0).then_inc(cleared, 1)
    pool.wait_ge(cleared, 1)
    nc_pool.affine_select(out=tile[:], in_=tile[:], compare_op=ALU.not_equal, fill=1.0, base=0,
                          pattern=[[-1, n]], channel_multiplier=1).then_inc(done, 1)


def mixer_scan(nc, S, D, keep):
    bc_parts = keep["bc_parts"]
    GN = 4
    NG = NS // GN
    Q = ND * NG
    RH, RA, RP = 4, 2, 4
    with Mem(nc) as m:
        rep = m.sb("s2_rep", [P, 2, NS, TC])
        dA = [m.sb(f"s2_dA{i}", [P, GN, TC]) for i in range(RA)]
        h = [m.sb(f"s2_h{i}", [P, GN, TC]) for i in range(RH)]
        hC = [m.sb(f"s2_hC{i}", [P, GN, TC]) for i in range(RA)]
        delta = m.sb("s2_delta", [P, ND, TC])
        u = m.sb("s2_u", [P, ND, TC])
        sz = m.sb("s2_sz", [P, ND, TC])
        du = m.sb("s2_du", [P, ND, TC])
        yz = m.sb("s2_yz", [P, ND, TC])
        state = m.sb("s2_state", [P, ND, NS])
        scanv = m.sb("s2_scanv", [P, ND, NS + 1])
        A = m.sb("s2_A", [P, ND, NS])
        sel = m.sb("s2_sel", [3 * 2 * NS, 2 * NS, P], BF16)
        ident = m.sb("s2_ident", [P, P])
        diag = m.sb("s2_diag", [P, ND, P])
        p_rep = [m.ps(f"s2_p_rep{i}", [P, TC]) for i in range(RP)]
        p_y = [m.ps(f"s2_p_y{i}", [P, TC]) for i in range(2)]

        cleared, ident_ready, sel_cleared, sel_step = S("cleared"), S("ident_ready"), S("sel_cleared"), S("sel_step")
        vec_in, exp_a, a_ready, state_ready = S("vec_in"), S("exp_a"), S("a_ready"), S("state_ready")
        chunk_in = [S(f"chunk_in{d}") for d in range(ND)]
        rep_mm, rep_ready = S("rep_mm"), S("rep_ready")
        da_ready, du_ready, dbu_ready, scan_ready = S("da_ready"), S("du_ready"), S("dbu_ready"), S("scan_ready")
        hc_ready, sum_done, diag_ready, yz_ready = S("hc_ready"), S("sum_done"), S("diag_ready"), S("yz_ready")
        yz_out = [S(f"yz_out{d}") for d in range(ND)]
        STATE0, SCAN0, REP0, SUM0, YZ0 = Q, RA, RP, RA, 2

        with nc.Block() as block:
            @block.sync
            def _(sp):
                prime(sp, yz_out)
                def load(c, d):
                    at = (slice(d * P, (d + 1) * P), bass.ds(c * TC, TC))
                    sp.dma_start(delta[:, d, :], D["delta"][at]).then_inc(chunk_in[d], 16)
                    sp.dma_start(u[:, d, :], D["u"][at]).then_inc(chunk_in[d], 16)
                    sp.dma_start(sz[:, d, :], D["sz"][at]).then_inc(chunk_in[d], 16)

                def store(c, d):
                    sp.dma_start(D["yz"][d * P:(d + 1) * P, bass.ds(c * TC, TC)], yz[:, d, :]).then_inc(yz_out[d], 16)

                sp.dma_start(scanv[:], D["scan_vecs"].rearrange("(k p) n -> p k n", p=P)).then_inc(vec_in, 16)
                for d in range(ND):
                    load(0, d)
                with sp.Fori(1, NC) as c:
                    for d in range(ND):
                        sp.wait_ge(yz_ready, c * ND + (YZ0 - ND + d + 1))
                        store(c - 1, d)
                        load(c, d)
                for d in range(ND):
                    sp.wait_ge(yz_ready, (NC - 1) * ND + YZ0 + d + 1)
                    store(NC - 1, d)
                for d in range(ND):
                    sp.wait_ge(yz_out[d], PRIMED + 16 * NC)

            @block.gpsimd
            def _(pool):
                set_identity(pool, ident, cleared, ident_ready)
                pool.memset(sel[:], 0.0).then_inc(sel_cleared, 1)
                pool.wait_ge(sel_cleared, 1)
                for part in range(3):
                    pool.wait_ge(sel_step, part)
                    pool.affine_select(out=sel[:], in_=sel[:], compare_op=ALU.not_equal, fill=1.0,
                                       base=-2 * NS * part, pattern=[[-1, 2 * NS], [0, P]],
                                       channel_multiplier=1).then_inc(sel_step, 1)
                def delta_u(c, d):
                    pool.wait_ge(chunk_in[d], c * 48 + 48)
                    pool.tensor_tensor(du[:, d, :], delta[:, d, :], u[:, d, :], ALU.mult).then_inc(du_ready, 1)

                def chunk(c, last):
                    for q in range(Q):
                        d, g = divmod(q, NG)
                        pool.wait_ge(scan_ready, c * Q + (SCAN0 + q + 1))
                        pool.wait_ge(sum_done, c * Q + (q + 1))
                        pool.tensor_tensor(hC[q % RA][:], h[q % RH][:], rep[:, 1, g * GN:(g + 1) * GN, :],
                                           ALU.mult).then_inc(hc_ready, 1)
                        pool.tensor_copy(state[:, d, g * GN:(g + 1) * GN],
                                         h[q % RH][:, :, TC - 1]).then_inc(state_ready, 1)
                        if g == 1 and d < ND - 1:
                            delta_u(c, d + 1)
                        elif g == 1 and not last:
                            delta_u(c + 1, 0)

                delta_u(0, 0)
                with pool.Fori(0, NC - 1) as c:
                    chunk(c, False)
                chunk(NC - 1, True)

            @block.scalar
            def _(act):
                act.sem_inc(rep_ready, REP0)
                act.wait_ge(vec_in, 16)
                nc.scalar.activation(A[:], scanv[:, :, 0:NS], ACT.Exp).then_inc(exp_a, 1)
                act.wait_ge(exp_a, 1)
                nc.scalar.mul(A[:], A[:], -1.0).then_inc(a_ready, 1)
                act.wait_ge(a_ready, 1)
                with act.Fori(0, NC) as c:
                    for q in range(Q):
                        d, g = divmod(q, NG)
                        if q < NG:
                            act.wait_ge(state_ready, c * Q + (STATE0 - NG + q + 1))
                            for j in range(2 * GN):
                                k = q * 2 * GN + j
                                act.wait_ge(rep_mm, c * (2 * NS) + (k + 1))
                                nc.scalar.copy(rep[:, j // GN, g * GN + j % GN, :], p_rep[k % RP][:]).then_inc(rep_ready, 1)
                        if g == 0:
                            act.wait_ge(chunk_in[d], c * 48 + 48)
                        act.wait_ge(scan_ready, c * Q + (q + 1))
                        for n in range(GN):
                            ex = nc.scalar.activation(dA[q % RA][:, n, :], delta[:, d, :], ACT.Exp,
                                                      scale=A[:, d, g * GN + n:g * GN + n + 1])
                        ex.then_inc(da_ready, 1)

            @block.vector
            def _(dve):
                def chunk(c, first):
                    for q in range(Q):
                        d, g = divmod(q, NG)
                        hb = h[q % RH]
                        if g == 0:
                            dve.wait_ge(du_ready, c * ND + (d + 1))
                        if d == 0:
                            dve.wait_ge(rep_ready, c * (2 * NS) + (REP0 + (g + 1) * 2 * GN))
                        dve.wait_ge(state_ready, c * Q + (STATE0 - RH + q + 1))
                        nc.vector.tensor_tensor(hb[:], du[:, d:d + 1, :].to_broadcast([P, GN, TC]),
                                                rep[:, 0, g * GN:(g + 1) * GN, :], ALU.mult).then_inc(dbu_ready, 1)
                        dve.wait_ge(dbu_ready, c * Q + (q + 1))
                        dve.wait_ge(da_ready, c * Q + (q + 1))
                        for n in range(GN):
                            at = g * GN + n
                            sc = nc.vector.tensor_tensor_scan(hb[:, n, :], dA[q % RA][:, n, :], hb[:, n, :],
                                                              state[:, d, at:at + 1], ALU.mult, ALU.add)
                        sc.then_inc(scan_ready, 1)
                        if q % NG == 2 and not (first and d == 0):
                            epilogue(c, d - 1) if d else epilogue(c - 1, ND - 1)

                def epilogue(c, d):
                    dve.wait_ge(sum_done, c * Q + (SUM0 + (d + 1) * NG))
                    dve.wait_ge(chunk_in[d], c * 48 + 48)
                    dve.wait_ge(yz_out[d], PRIMED + c * 16)
                    nc.vector.tensor_tensor(yz[:, d, :], p_y[d % 2][:], sz[:, d, :], ALU.mult).then_inc(yz_ready, 1)

                dve.sem_inc(scan_ready, SCAN0)
                dve.sem_inc(yz_ready, YZ0)
                nc.vector.memset(state[:], 0.0).then_inc(state_ready, STATE0)
                dve.wait_ge(vec_in, 16)
                dve.wait_ge(ident_ready, 1)
                for d in range(ND):
                    nc.vector.tensor_scalar(diag[:, d, :], ident[:], scanv[:, d, NS:NS + 1], None,
                                            ALU.mult).then_inc(diag_ready, 1)
                chunk(0, True)
                with dve.Fori(1, NC) as c:
                    chunk(c, False)
                epilogue(NC - 1, ND - 1)

            @block.tensor
            def _(pe):
                def spread(c, g):
                    for j in range(2 * GN):
                        k = g * 2 * GN + j
                        row = (j // GN) * NS + g * GN + j % GN
                        pe.wait_ge(rep_ready, c * (2 * NS) + (k + 1))
                        nc.tensor.matmul(p_rep[k % RP][:], sel[:, row, :], bc_parts[:, bass.ds(c * TC, TC)],
                                         start=True, stop=True).then_inc(rep_mm, 1)

                def add_states(c, q):
                    d, g = divmod(q, NG)
                    if g == 0:
                        pe.wait_ge(yz_ready, c * ND + (d + 1))
                        pe.wait_ge(chunk_in[d], c * 48 + 48)
                        nc.tensor.matmul(p_y[d % 2][:], diag[:, d, :], u[:, d, :], start=True, stop=False)
                    pe.wait_ge(hc_ready, c * Q + (q + 1))
                    for n in range(GN):
                        mm = nc.tensor.matmul(p_y[d % 2][:], ident[:], hC[q % RA][:, n, :],
                                              start=False, stop=g == NG - 1 and n == GN - 1)
                    mm.then_inc(sum_done, 1)

                def chunk(c, first):
                    for g in range(NG):
                        spread(c, g)
                        if not first:
                            add_states(c - 1, Q - NG + g)
                    for q in range(Q - NG):
                        add_states(c, q)

                pe.sem_inc(sum_done, SUM0)
                pe.wait_ge(ident_ready, 1)
                pe.wait_ge(sel_step, 3)
                pe.wait_ge(diag_ready, ND)
                chunk(0, True)
                with pe.Fori(1, NC) as c:
                    chunk(c, False)
                for q in range(Q - NG, Q):
                    add_states(NC - 1, q)


class NormRing:

    def __init__(self, m, S, tag, of=None):
        self.s = of.y if of else [m.sb(f"{tag}_sum{i}", [P, JT, DM]) for i in range(2)]
        self.y = [m.sb(f"{tag}_norm{i}", [P, JT, DM]) for i in range(2)]
        self.bst = m.sb(f"{tag}_bst", [P, 2 * JT, 6])
        self.mv = m.sb(f"{tag}_mv", [P, 2 * JT, 2])
        self.std = m.sb(f"{tag}_std", [P, 2 * JT])
        self.rs = m.sb(f"{tag}_rs", [P, 2 * JT])
        self.eps = m.sb(f"{tag}_eps", [P, 1])
        self.gate = S(f"{tag}_gate")
        self.sum_ready = of.norm_ready if of else S(f"{tag}_sum_ready")
        self.eps_ready, self.stat_ready, self.mv_ready = (
            S(f"{tag}_eps_ready"), S(f"{tag}_stat_ready"), S(f"{tag}_mv_ready"))
        self.std_ready, self.rs_ready, self.norm_ready = (
            S(f"{tag}_std_ready"), S(f"{tag}_rs_ready"), S(f"{tag}_norm_ready"))
        self.primed = [self.norm_ready] if of else [self.sum_ready, self.norm_ready]

    def vector_setup(self, dve):
        dve.memset(self.eps[:], EPS).then_inc(self.eps_ready, 1)

    def vector_stats(self, dve, c, par):
        for j in range(JT):
            T, k = c * JT + par * JT + j, par * JT + j
            dve.wait_ge(self.sum_ready, PRIMED + T + 1)
            dve.bn_stats(self.bst[:, k, :], self.s[par][:, j, :]).then_inc(self.stat_ready, 1)
        for j in range(JT):
            T, k = c * JT + par * JT + j, par * JT + j
            dve.wait_ge(self.stat_ready, T + 1)
            dve.sem_inc(self.gate, 1)
            dve.bn_aggr(self.mv[:, k, :], self.bst[:, k, :]).then_inc(self.mv_ready, 1)

    def scalar_std(self, act, c, par):
        k = par * JT
        act.wait_ge(self.mv_ready, c * JT + (k + JT))
        act.activation(self.std[:, k:k + JT], self.mv[:, k:k + JT, 1], ACT.Sqrt,
                       bias=self.eps[:, 0:1]).then_inc(self.std_ready, 1)

    def vector_norm(self, dve, c, par):
        k0 = par * JT
        dve.wait_ge(self.std_ready, c + (par + 1))
        dve.reciprocal(self.rs[:, k0:k0 + JT], self.std[:, k0:k0 + JT]).then_inc(self.rs_ready, 1)
        dve.wait_ge(self.rs_ready, c + (par + 1))
        for j in range(JT):
            k = k0 + j
            dve.tensor_scalar(self.y[par][:, j, :], self.s[par][:, j, :], self.mv[:, k, 0:1],
                              self.rs[:, k:k + 1], ALU.subtract, ALU.mult).then_inc(self.norm_ready, 1)


def mixer_out(nc, S, D, keep):
    xn, xt = keep["xn"], keep["xt"]
    with Mem(nc) as m:
        w_out = m.sb("s3_w_out", [P, ND, DM])
        yz = [m.sb(f"s3_yz{i}", [P, ND, TC]) for i in range(2)]
        xin = [m.sb(f"s3_xin{i}", [P, JT, DM]) for i in range(2)]
        ident = m.sb("s3_ident", [P, P])
        p_o = [m.ps(f"s3_p_o{i}", [P, TC]) for i in range(4)]
        p_t = [m.ps(f"s3_p_t{i}", [P, TC]) for i in range(2)]
        R = NormRing(m, S, "s3")
        cleared, ident_ready, w_loaded = S("cleared"), S("ident_ready"), S("w_loaded")
        chunk_in = [S(f"chunk_in{i}") for i in range(2)]
        out_ready, turned, turn_taken, kept = S("out_ready"), S("turned"), S("turn_taken"), S("kept")

        with nc.Block() as block:
            @block.sync
            def _(sp):
                prime(sp, [out_ready, kept, turned, *R.primed])
                sp.dma_start(w_out[:], D["w_out"].rearrange("(k p) n -> p k n", p=P)).then_inc(w_loaded, 16)
                with sp.Fori(0, NC - 1, 2) as c:
                    for par in range(2):
                        sp.wait_ge(R.sum_ready, PRIMED + c * JT)
                        sp.wait_ge(out_ready, PRIMED + c * JT)
                        sp.dma_start(yz[par][:], D["yz"].rearrange("(k p) n -> p k n", p=P)[
                            :, :, bass.ds((c + par) * TC, TC)]).then_inc(chunk_in[par], 16)
                        sp.dma_start(xin[par][:], D["x"][bass.ds((c + par) * TC, TC), :].rearrange(
                            "(j p) n -> p j n", p=P)).then_inc(chunk_in[par], 16)

            @block.gpsimd
            def _(pool):
                set_identity(pool, ident, cleared, ident_ready)
                with pool.Fori(0, NC - 1, 2) as c:
                    for par in range(2):
                        pool.wait_ge(R.norm_ready, PRIMED + c * JT + (par + 1) * JT)
                        pool.tensor_copy(xn[:, bass.ds((c + par) * JT, JT), :], R.y[par][:]).then_inc(kept, 1)

            @block.tensor
            def _(pe):
                pe.wait_ge(w_loaded, 16)
                pe.wait_ge(ident_ready, 1)
                with pe.Fori(0, NC - 1, 2) as c:
                    for par in range(2):
                        pe.wait_ge(chunk_in[par], c * 16 + 32)
                        for j in range(JT):
                            k = par * JT + j
                            if k < 4:
                                pe.wait_ge(R.sum_ready, PRIMED + c * JT)
                            else:
                                pe.wait_ge(R.sum_ready, PRIMED + c * JT + (k - 3))
                            for d in range(ND):
                                mm = nc.tensor.matmul(p_o[j][:, 0:DM], yz[par][:, d, j * P:(j + 1) * P],
                                                      w_out[:, d, :], start=d == 0, stop=d == ND - 1)
                            mm.then_inc(out_ready, 1)
                    for par in range(2):
                        turn_tiles(pe, c, par, R, p_t, ident, turned, turn_taken)

            @block.scalar
            def _(act):
                act.sem_inc(turn_taken, 2)
                act.wait_ge(R.eps_ready, 1)
                with act.Fori(0, NC - 1, 2) as c:
                    R.scalar_std(act, c, 0)
                    R.scalar_std(act, c, 1)
                    for par in range(2):
                        take_turned(act, c, par, xt, p_t, turned, turn_taken)

            @block.vector
            def _(dve):
                R.vector_setup(dve)
                with dve.Fori(0, NC - 1, 2) as c:
                    dve.wait_ge(R.norm_ready, PRIMED + c * JT)
                    for par in range(2):
                        dve.wait_ge(chunk_in[par], c * 16 + 32)
                        for j in range(JT):
                            dve.wait_ge(out_ready, PRIMED + c * JT + (par * JT + j + 1))
                            nc.vector.tensor_tensor(R.s[par][:, j, :], p_o[j][:, 0:DM], xin[par][:, j, :],
                                                    ALU.add).then_inc(R.sum_ready, 1)
                        R.vector_stats(dve, c, par)
                    for par in range(2):
                        dve.wait_ge(kept, PRIMED + c + par)
                        dve.wait_ge(turned, PRIMED + c * JT)
                        R.vector_norm(dve, c, par)


def turn_tiles(pe, c, par, R, p_t, ident, turned, turn_taken):
    for j in range(JT):
        k = par * JT + j
        pe.wait_ge(R.norm_ready, PRIMED + c * JT + (k + 1))
        pe.wait_ge(turn_taken, c * JT + (k + 1))
        for half in range(KD):
            tr = pe.transpose(p_t[k % 2][:, half * P:(half + 1) * P], R.y[par][:, j, half * P:(half + 1) * P],
                              ident[:])
        tr.then_inc(turned, 1)


def take_turned(act, c, par, xt, p_t, turned, turn_taken):
    for j in range(JT):
        k = par * JT + j
        act.wait_ge(turned, PRIMED + c * JT + (k + 1))
        act.copy(xt[:, :, bass.ds((c * JT + k) * P, P)],
                 p_t[k % 2][:, 0:DM].rearrange("p (h t) -> p h t", h=KD)).then_inc(turn_taken, 1)


R1 = 64
E0 = 8


def adapter(nc, S, D, keep):
    xn, xt = keep["xn"], keep["xt"]
    with Mem(nc) as m:
        base = m.sb("s4_base", [P, KD, DM])
        disc = m.sb("s4_disc", [P, KD, 2 * E0])
        bias = m.sb("s4_bias", [R1 + 1, 2, DM])
        down = m.sb("s4_down", [P, KD, R1])
        down_b = m.sb("s4_down_b", [R1, 1])
        up = m.sb("s4_up", [P, KD, R1 + 1])
        outm = m.sb("s4_outm", [P, KD, DM])
        fused = m.sb("s4_fused", [R1 + 1, DM])
        bst = m.sb("s4_bstT", [P, KD, NC, 6])
        mv = m.sb("s4_mvT", [P, KD, 2])
        vec = m.sb("s4_vec", [P, KD, 4])
        iv = m.sb("s4_iv", [P, KD, E0])
        t = m.sb("s4_t", [P, KD, E0])
        ones = m.sb("s4_ones", [P, 1])
        loss = m.sb("s4_loss", [1, 3, E0])
        choice = m.sb("s4_choice", [1, E0], U32)
        xs = [m.sb(f"s4_xs{i}", [P, KD, TC]) for i in range(2)]
        hid = [m.sb(f"s4_hid{i}", [R1 + 1, TC]) for i in range(2)]
        ident = m.sb("s4_ident", [P, P])
        p_m = m.ps("s4_p_m", [P, TC])
        p_h = m.ps("s4_p_h", [P, TC])
        p_o = [m.ps(f"s4_p_o{i}", [P, TC]) for i in range(4)]
        p_t = [m.ps(f"s4_p_t{i}", [P, TC]) for i in range(2)]
        R = NormRing(m, S, "s4")
        cleared, ident_ready, w_loaded, e_loaded = S("cleared"), S("ident_ready"), S("w_loaded"), S("e_loaded")
        ones_ready, step, loss_mm, chosen = S("ones_ready"), S("step"), S("loss_mm"), S("chosen")
        fuse_mm, fused_ready, x_taken, hid_mm, hid_ready = (
            S("fuse_mm"), S("fused_ready"), S("x_taken"), S("hid_mm"), S("hid_ready"))
        out_ready, turned, turn_taken, kept = S("out_ready"), S("turned"), S("turn_taken"), S("kept")

        with nc.Block() as block:
            @block.sync
            def _(sp):
                prime(sp, [out_ready, kept, turned, *R.primed])
                sp.dma_start(disc[:], D["disc"].rearrange("(k p) n -> p k n", p=P)).then_inc(w_loaded, 16)
                sp.dma_start(base[:], D["base"].rearrange("(k p) n -> p k n", p=P)).then_inc(w_loaded, 16)
                sp.dma_start(bias[R1:R1 + 1, 0, :], D["base_b"]).then_inc(w_loaded, 16)
                sp.wait_ge(chosen, 1)
                e = sp.value_load(choice[0:1, 0:1], min_val=0, max_val=E0 - 1)
                sp.dma_start(down[:], D["down"].rearrange("e (k p) n -> p (e k) n", p=P)[
                    :, bass.ds(e * KD, KD), :]).then_inc(e_loaded, 16)
                sp.dma_start(up[:], D["up"].rearrange("e (k p) n -> p (e k) n", p=P)[
                    :, bass.ds(e * KD, KD), :]).then_inc(e_loaded, 16)
                sp.dma_start(outm[:], D["outm"].rearrange("e (k p) n -> p (e k) n", p=P)[
                    :, bass.ds(e * KD, KD), :]).then_inc(e_loaded, 16)
                sp.dma_start(down_b[:], D["down_b"][bass.ds(e * R1, R1), :]).then_inc(e_loaded, 16)
                sp.dma_start(bias[R1:R1 + 1, 1, :], D["outm_b"][bass.ds(e, 1), :]).then_inc(e_loaded, 16)

            @block.gpsimd
            def _(pool):
                set_identity(pool, ident, cleared, ident_ready)
                with pool.Fori(0, NC - 1, 2) as c:
                    for par in range(2):
                        pool.wait_ge(out_ready, PRIMED + c * JT)
                        pool.tensor_copy(xs[par][:], xt[:, :, bass.ds((c + par) * TC, TC)]).then_inc(x_taken, 1)
                    for par in range(2):
                        pool.wait_ge(R.norm_ready, PRIMED + c * JT + (par + 1) * JT)
                        pool.tensor_copy(xn[:, bass.ds((c + par) * JT, JT), :], R.y[par][:]).then_inc(kept, 1)

            @block.tensor
            def _(pe):
                pe.wait_ge(ones_ready, 1)
                pe.wait_ge(step, 7)
                for k in range(KD):
                    mm = nc.tensor.matmul(p_m[0:1, 0:E0], ones[:], t[:, k, :], start=k == 0, stop=k == KD - 1)
                mm.then_inc(loss_mm, 1)
                pe.wait_ge(e_loaded, 16 * 5)
                pe.wait_ge(step, 8)
                for k in range(KD):
                    mm = nc.tensor.matmul(p_m[0:R1 + 1, 0:DM], up[:, k, :], outm[:, k, :],
                                          start=k == 0, stop=k == KD - 1)
                mm.then_inc(fuse_mm, 1)
                pe.wait_ge(w_loaded, 48)
                pe.wait_ge(ident_ready, 1)
                pe.wait_ge(fused_ready, 2)
                with pe.Fori(0, NC - 1, 2) as c:
                    for par in range(2):
                        pe.wait_ge(x_taken, c + (par + 1))
                        pe.wait_ge(hid_ready, c + (par + 1))
                        for k in range(KD):
                            mm = nc.tensor.matmul(p_h[0:R1, :], down[:, k, :], xs[par][:, k, :],
                                                  start=k == 0, stop=k == KD - 1)
                        mm.then_inc(hid_mm, 1)
                    for par in range(2):
                        pe.wait_ge(hid_ready, c + (par + 2))
                        for j in range(JT):
                            i = par * JT + j
                            pe.wait_ge(R.sum_ready, PRIMED + c * JT + (max(i - 3, 0)))
                            for k in range(KD):
                                nc.tensor.matmul(p_o[j][:, 0:DM], xs[par][:, k, j * P:(j + 1) * P], base[:, k, :],
                                                 start=k == 0, stop=False)
                            nc.tensor.matmul(p_o[j][:, 0:DM], hid[par][:, j * P:(j + 1) * P], fused[:],
                                             start=False, stop=True).then_inc(out_ready, 1)
                    for par in range(2):
                        turn_tiles(pe, c, par, R, p_t, ident, turned, turn_taken)

            @block.scalar
            def _(act):
                act.sem_inc(turn_taken, 2)
                act.wait_ge(R.eps_ready, 1)
                act.wait_ge(e_loaded, 16 * 5)
                act.wait_ge(ones_ready, 3)
                act.sem_inc(hid_ready, 1)
                with act.Fori(0, NC - 1, 2) as c:
                    for par in range(2):
                        act.wait_ge(hid_mm, c + (par + 1))
                        act.wait_ge(out_ready, PRIMED + c * JT)
                        nc.scalar.activation(hid[par][0:R1, :], p_h[0:R1, :], ACT.Relu,
                                             bias=down_b[:, 0:1]).then_inc(hid_ready, 1)
                    R.scalar_std(act, c, 0)
                    R.scalar_std(act, c, 1)
                    for par in range(2):
                        act.wait_ge(x_taken, c + (par + 1))
                        take_turned(act, c, par, xt, p_t, turned, turn_taken)

            @block.vector
            def _(dve):
                R.vector_setup(dve)
                nc.vector.memset(ones[:], 1.0).then_inc(ones_ready, 1)
                for i in range(2):
                    nc.vector.memset(hid[i][:], 1.0).then_inc(ones_ready, 1)
                for k in range(KD):
                    for c in range(NC):
                        st = nc.vector.bn_stats(bst[:, k, c, :], xt[:, k, c * TC:(c + 1) * TC])
                st.then_inc(step, 1)
                dve.wait_ge(step, 1)
                for k in range(KD):
                    st = nc.vector.bn_aggr(mv[:, k, :], bst[:, k, :, :].rearrange("p c s -> p (c s)"))
                st.then_inc(step, 1)
                dve.wait_ge(step, 2)
                dve.wait_ge(w_loaded, 48)
                for k in range(KD):
                    nc.vector.tensor_scalar(vec[:, k, 0:1], mv[:, k, 0:1], -2.0, None, ALU.mult)
                    nc.vector.scalar_tensor_tensor(out=vec[:, k, 1:2], in0=mv[:, k, 0:1], scalar=mv[:, k, 0:1],
                                                   in1=mv[:, k, 1:2], op0=ALU.mult, op1=ALU.add)
                    st = nc.vector.tensor_tensor(iv[:, k, :], disc[:, k, E0:2 * E0], disc[:, k, E0:2 * E0], ALU.mult)
                st.then_inc(step, 1)
                dve.wait_ge(step, 3)
                nc.vector.reciprocal(iv[:], iv[:]).then_inc(step, 1)
                for k in range(KD):
                    st = nc.vector.scalar_tensor_tensor(out=t[:, k, :], in0=disc[:, k, 0:E0], scalar=vec[:, k, 0:1],
                                                        in1=disc[:, k, 0:E0], op0=ALU.add, op1=ALU.mult)
                st.then_inc(step, 1)
                dve.wait_ge(step, 5)
                for k in range(KD):
                    st = nc.vector.tensor_scalar(t[:, k, :], t[:, k, :], vec[:, k, 1:2], None, ALU.add)
                st.then_inc(step, 1)
                dve.wait_ge(step, 6)
                nc.vector.tensor_tensor(t[:], t[:], iv[:], ALU.mult).then_inc(step, 1)
                dve.wait_ge(loss_mm, 1)
                nc.vector.tensor_scalar(loss[:, 0, :], p_m[0:1, 0:E0], -1.0 / DM, None, ALU.mult).then_inc(step, 1)
                dve.wait_ge(step, 8)
                nc.vector.max(loss[:, 1, :], loss[:, 0, :]).then_inc(step, 1)
                dve.wait_ge(step, 9)
                nc.vector.max_index(choice[:], loss[:, 1, :], loss[:, 0, :]).then_inc(chosen, 1)
                dve.wait_ge(fuse_mm, 1)
                dve.wait_ge(e_loaded, 16 * 5)
                nc.vector.tensor_copy(fused[0:R1, :], p_m[0:R1, 0:DM]).then_inc(fused_ready, 1)
                nc.vector.tensor_tensor(bias[R1:R1 + 1, 0, :], bias[R1:R1 + 1, 0, :], bias[R1:R1 + 1, 1, :],
                                        ALU.add).then_inc(step, 1)
                dve.wait_ge(step, 10)
                nc.vector.tensor_tensor(fused[R1:R1 + 1, :], p_m[R1:R1 + 1, 0:DM], bias[R1:R1 + 1, 0, :],
                                        ALU.add).then_inc(fused_ready, 1)
                with dve.Fori(0, NC - 1, 2) as c:
                    dve.wait_ge(R.norm_ready, PRIMED + c * JT)
                    for par in range(2):
                        for j in range(JT):
                            i = par * JT + j
                            dve.wait_ge(out_ready, PRIMED + c * JT + (i + 1))
                            nc.vector.tensor_tensor(R.s[par][:, j, :], p_o[j][:, 0:DM], xn[:, c * JT + i, :],
                                                    ALU.add).then_inc(R.sum_ready, 1)
                        R.vector_stats(dve, c, par)
                    for par in range(2):
                        dve.wait_ge(kept, PRIMED + c + par)
                        dve.wait_ge(turned, PRIMED + c * JT)
                        R.vector_norm(dve, c, par)


NH = 16
DH = DM // NH
COMBOS = [(0, 0), (0, 1), (0, 2), (1, 0), (1, 1), (2, 0)]
SR = len(COMBOS) * DH
VW = 32


def qkv(nc, S, D, keep):
    xt, v_all = keep["xt"], keep["v_all"]
    with Mem(nc) as m:
        w_qk = m.sb("s5_w_qk", [P, KD, 2 * DM])
        w_v = m.sb("s5_w_v", [P, KD, DM])
        xs = [m.sb(f"s5_xs{i}", [P, KD, TC]) for i in range(2)]
        parts = [[m.sb(f"s5_parts{i}{t}", [P, 3, TC], BF16) for t in range(4)] for i in range(2)]
        rest = [m.sb(f"s5_rest{t}", [P, TC]) for t in range(4)]
        p_qk = [m.ps(f"s5_p_qk{i}", [P, TC]) for i in range(4)]
        p_v = [m.ps(f"s5_p_v{i}", [P, TC]) for i in range(2)]
        w_loaded, x_taken, v_mm, v_taken = S("w_loaded"), S("x_taken"), S("v_mm"), S("v_taken")
        qk_mm, hi_ready, rest_ready, mid_ready, low_ready = (
            S("qk_mm"), S("hi_ready"), S("rest_ready"), S("mid_ready"), S("low_ready"))
        gate = S("gate")
        qk_out = [[S(f"qk_out{i}{t}") for t in range(4)] for i in range(2)]

        with nc.Block() as block:
            @block.sync
            def _(sp):
                prime(sp, [v_mm, low_ready, *qk_out[0], *qk_out[1]])
                sp.dma_start(w_qk[:], D["w_qk"].rearrange("(k p) n -> p k n", p=P)).then_inc(w_loaded, 16)
                sp.dma_start(w_v[:], D["w_v"].rearrange("(k p) n -> p k n", p=P)).then_inc(w_loaded, 16)
                with sp.Fori(0, NC - 1, 2) as c:
                    for par in range(2):
                        for t in range(4):
                            sp.wait_ge(low_ready, PRIMED + c * 4 + (par * 4 + t + 1))
                            row = (t // 2) * 3 * DM + (t % 2) * P
                            sp.dma_start(D["qk"].rearrange("(a r) n -> r a n", r=DM)[
                                (t % 2) * P:(t % 2 + 1) * P, (t // 2) * 3:(t // 2) * 3 + 3,
                                bass.ds((c + par) * TC, TC)], parts[par][t][:]).then_inc(qk_out[par][t], 16)
                for par in range(2):
                    for t in range(4):
                        sp.wait_ge(qk_out[par][t], PRIMED + 16 * NC // 2)

            @block.gpsimd
            def _(pool):
                with pool.Fori(0, NC - 1, 2) as c:
                    for par in range(2):
                        pool.wait_ge(v_mm, PRIMED + c * JT)
                        pool.tensor_copy(xs[par][:], xt[:, :, bass.ds((c + par) * TC, TC)]).then_inc(x_taken, 1)
                    for par in range(2):
                        for t in range(4):
                            k = par * 4 + t
                            pool.wait_ge(rest_ready, c * 4 + (4 + k + 1))
                            pool.sem_inc(gate, 1)
                            pool.tensor_copy(parts[par][t][:, 1, :], rest[t][:]).then_inc(mid_ready, 1)
                            pool.wait_ge(mid_ready, c * 4 + (k + 1))
                            pool.tensor_tensor(parts[par][t][:, 2, :], rest[t][:], parts[par][t][:, 1, :],
                                               ALU.subtract).then_inc(low_ready, 1)

            @block.tensor
            def _(pe):
                pe.wait_ge(w_loaded, 32)
                with pe.Fori(0, NC - 1, 2) as c:
                    for par in range(2):
                        pe.wait_ge(x_taken, c + (par + 1))
                        for t in range(4):
                            pe.wait_ge(rest_ready, c * 4 + (par * 4 + t + 1))
                            for k in range(KD):
                                mm = nc.tensor.matmul(p_qk[t][:], w_qk[:, k, t * P:(t + 1) * P], xs[par][:, k, :],
                                                      start=k == 0, stop=k == KD - 1)
                            mm.then_inc(qk_mm, 1)
                        for j in range(JT):
                            pe.wait_ge(v_taken, c * JT + (par * JT + j + 1))
                            for k in range(KD):
                                mm = nc.tensor.matmul(p_v[j % 2][:, 0:DM], xs[par][:, k, j * P:(j + 1) * P],
                                                      w_v[:, k, :], start=k == 0, stop=k == KD - 1)
                            mm.then_inc(v_mm, 1)

            @block.scalar
            def _(act):
                act.sem_inc(v_taken, 2)
                with act.Fori(0, NC - 1, 2) as c:
                    for par in range(2):
                        for t in range(4):
                            act.wait_ge(qk_mm, c * 4 + (par * 4 + t + 1))
                            act.wait_ge(qk_out[par][t], PRIMED + c * 8)
                            nc.scalar.copy(parts[par][t][:, 0, :], p_qk[t][:]).then_inc(hi_ready, 1)
                        for j in range(JT):
                            i = par * JT + j
                            act.wait_ge(v_mm, PRIMED + c * JT + (i + 1))
                            nc.scalar.copy(v_all[:, :, c * JT + i, :],
                                           p_v[j % 2][:, 0:DM].rearrange("p (h d) -> p h d", h=NH)).then_inc(v_taken, 1)

            @block.vector
            def _(dve):
                dve.sem_inc(rest_ready, 4)
                with dve.Fori(0, NC - 1, 2) as c:
                    for par in range(2):
                        for t in range(4):
                            k = par * 4 + t
                            dve.wait_ge(hi_ready, c * 4 + (k + 1))
                            dve.wait_ge(low_ready, PRIMED + c * 4 + max(k - 3, 0))
                            nc.vector.tensor_tensor(rest[t][:], p_qk[t][:], parts[par][t][:, 0, :],
                                                    ALU.subtract).then_inc(rest_ready, 1)


def attention(nc, S, D, keep):
    v_all, att = keep["v_all"], keep["att"]
    NB = 3
    R1B, R2B, RPT = 3, 3, 8
    QUADS = [(Q, g) for Q in range(NC) for g in range(Q + 1)]
    LAST = {Q: max(b for b, x in enumerate(QUADS) if x[0] == Q) for Q in range(NC)}
    NQ = len(QUADS)
    TILES1 = [(i, kc) for i in range(TT) for kc in range(i // 4 + 1)]
    N1 = len(TILES1)
    S1 = N1 + 1
    SLOW = 4
    share = [(N1 * (b + 1)) // (NQ - SLOW) - (N1 * b) // (NQ - SLOW) for b in range(NQ - SLOW)] + [0] * SLOW
    TURN_AT = NQ - SLOW + 1
    MISC = NC + 1
    NEG = -3.0e38
    MAX_IN = 16 * 3
    STACK_IN = 16 * 2 * len(COMBOS)

    def count(h, per, more=0):
        return h[0] * per + (h[1] * per + more)

    def turns(h, per):
        return h[0] * (per // NB) + (h[1] // NB + 1) * per

    def comb_of(b):
        return next((Q for Q in range(NC - 1) if LAST[Q] + 2 == b), None)

    with Mem(nc) as m:
        qs = [m.sb(f"s6_qs{i}", [P, L], BF16) for i in range(NB)]
        ks = [m.sb(f"s6_ks{i}", [P, L], BF16) for i in range(NB)]
        vh = [m.sb(f"s6_vh{i}", [P, TT, VW]) for i in range(NB)]
        pt = [m.sb(f"s6_pt{i}", [P, TC]) for i in range(RPT)]
        oT = [m.sb(f"s6_oT{i}", [P, TC]) for i in range(2)]
        rec = [m.sb(f"s6_rec{i}", [P, JT]) for i in range(2)]
        mx = m.sb("s6_mx", [P, TT, NC])
        negm = m.sb("s6_negm", [P, TT])
        m_rest = m.sb("s6_m_rest", [TT, P])
        m_parts = m.sb("s6_m_parts", [TT, 3, P], BF16)
        identb = m.sb("s6_identb", [P, P], BF16)
        ident = m.sb("s6_ident", [P, P])
        comb = m.sb("s6_comb", [P, VW])
        mask1 = m.sb("s6_mask1", [P, P], BF16)
        mask2 = m.sb("s6_mask2", [P, TC], BF16)
        p_1 = [m.ps(f"s6_p_1{i}", [P, TC]) for i in range(R1B)]
        p_2 = [m.ps(f"s6_p_2{i}", [P, TC]) for i in range(R2B)]
        p_oT = m.ps("s6_p_oT", [P, TC])
        p_misc = m.ps("s6_p_misc", [P, TC])
        p_c = p_misc[:, 0:JT * VW].rearrange("p (j d) -> p j d", j=JT)
        p_mT = p_misc[0:TT, JT * VW:JT * VW + P]

        const_step, consts, buf_set = S("const_step"), S("consts"), S("buf_set")
        stack_in = [S(f"stack_in{i}") for i in range(NB)]
        m_in = [S(f"m_in{i}") for i in range(NB)]
        v_ready, s1_mm, s1_taken = S("v_ready"), S("s1_mm"), S("s1_taken")
        misc_mm, misc_taken, mstep, mp_ready = S("misc_mm"), S("misc_taken"), S("mstep"), S("mp_ready")
        s2_mm, exp_ready, pv_done, oT_taken, rec_ready = (
            S("s2_mm"), S("exp_ready"), S("pv_done"), S("oT_taken"), S("rec_ready"))

        with nc.Block() as block:
            @block.sync
            def _(sp):
                prime(sp, [pv_done, misc_mm])
                def send_maxima(h, buf):
                    sp.wait_ge(mp_ready, count(h, 1, 1))
                    for part in range(3):
                        sp.dma_start(qs[buf][SR + part:SR + part + 1, :].rearrange("o (i p) -> o i p", p=P),
                                     m_parts[:, part, :]).then_inc(m_in[buf], 16)

                send_maxima((0, 0), 0)
                with sp.Fori(0, NH - NB, NB) as r:
                    for i in range(1, NB + 1):
                        send_maxima((r, i), i % NB)

            @block.gpsimd
            def _(pool):
                def load(n, buf, behind):
                    if behind:
                        pool.wait_ge(pv_done, PRIMED + (n - (NB - 1)) * NQ)
                    pool.wait_ge(buf_set, 1)
                    for x, (qp, kp) in enumerate(COMBOS):
                        pool.dma_start(qs[buf][x * DH:(x + 1) * DH, :],
                                       D["qk"][bass.ds(n * DH + qp * DM, DH), :]).then_inc(stack_in[buf], 16)
                        pool.dma_start(ks[buf][x * DH:(x + 1) * DH, :],
                                       D["qk"][bass.ds(n * DH + (3 + kp) * DM, DH), :]).then_inc(stack_in[buf], 16)
                    pool.tensor_copy(vh[buf][:, :, 0:DH], v_all[:, n, :, :]).then_inc(v_ready, 1)

                set_identity(pool, ident, const_step, const_step)
                pool.memset(identb[:], 0.0).then_inc(const_step, 1)
                pool.wait_ge(const_step, 3)
                pool.affine_select(out=identb[:], in_=identb[:], compare_op=ALU.not_equal, fill=1.0, base=0,
                                   pattern=[[-1, P]], channel_multiplier=1).then_inc(const_step, 1)
                pool.memset(mask1[:], 0.0).then_inc(const_step, 1)
                pool.memset(mask2[:], NEG).then_inc(const_step, 1)
                pool.memset(comb[:], 0.0).then_inc(const_step, 1)
                pool.wait_ge(const_step, 7)
                pool.affine_select(out=mask1[:], in_=mask1[:], compare_op=ALU.is_ge, fill=NEG, base=0,
                                   pattern=[[-1, P]], channel_multiplier=1).then_inc(const_step, 1)
                pool.affine_select(out=mask2[:, TC - P:], in_=mask2[:, TC - P:], compare_op=ALU.is_gt, fill=0.0,
                                   base=0, pattern=[[-1, P]], channel_multiplier=1).then_inc(const_step, 1)
                for j in range(P // VW):
                    pool.wait_ge(const_step, 9 + j)
                    pool.affine_select(out=comb[:], in_=comb[:], compare_op=ALU.not_equal, fill=1.0, base=-VW * j,
                                       pattern=[[-1, VW]], channel_multiplier=1).then_inc(const_step, 1)
                for n in range(NB):
                    load(n, n, False)
                with pool.Fori(NB, NH - NB, NB) as n:
                    for i in range(NB):
                        load(n + i, i, True)
                load(NH - 1, (NH - 1) % NB, True)

            @block.tensor
            def _(pe):
                def first_pass(h, buf, x):
                    i, kc = TILES1[x]
                    last = kc == i // 4
                    w = (i % 4 + 1) * P if last else TC
                    pe.wait_ge(s1_taken, count(h, S1, x + 1))
                    mm = nc.tensor.matmul(p_1[x % R1B][:, 0:w], qs[buf][0:SR, i * P:(i + 1) * P],
                                          ks[buf][0:SR, kc * TC:kc * TC + w], start=True, stop=not last)
                    if last:
                        mm = nc.tensor.matmul(p_1[x % R1B][:, w - P:w], identb[:], mask1[:], start=False, stop=True)
                    mm.then_inc(s1_mm, 1)

                def second_pass(h, buf, b, x):
                    Q, g = QUADS[b]
                    t, k = 4 * g + x, 4 * b + x
                    over = (t - 4 * Q) * P if t > 4 * Q else 0
                    off = over if Q else 0
                    pe.wait_ge(exp_ready, count(h, 4 * NQ, k + 1))
                    p = p_2[k % R2B]
                    mm = nc.tensor.matmul(p[:, off:TC], ks[buf][0:SR + 3, t * P:(t + 1) * P],
                                          qs[buf][0:SR + 3, Q * TC + off:(Q + 1) * TC], start=True, stop=t < 4 * Q)
                    if t >= 4 * Q:
                        lead = 0 if Q else over
                        mm = nc.tensor.matmul(p[:, off:off + lead + P], identb[:], mask2[:, TC - P - lead:TC],
                                              start=False, stop=True)
                    mm.then_inc(s2_mm, 1)

                def values(h, buf, b):
                    Q, g = QUADS[b]
                    if g == 0:
                        pe.wait_ge(oT_taken, count(h, NC, Q + 1))
                    for x in range(4):
                        t, k = 4 * g + x, 4 * b + x
                        off = (t - 4 * Q) * P if Q and t > 4 * Q else 0
                        pe.wait_ge(exp_ready, count(h, 4 * NQ, R2B + k + 1))
                        mm = nc.tensor.matmul(p_oT[x * VW:(x + 1) * VW, off:TC], vh[buf][:, t, :],
                                              pt[k % RPT][:, off:TC], start=g == 0, stop=g == Q)
                    mm.then_inc(pv_done, 1)

                def combine(h, Q, use):
                    pe.wait_ge(oT_taken, count(h, NC, Q + 2))
                    pe.wait_ge(misc_taken, count(h, MISC, use))
                    for j in range(JT):
                        mm = nc.tensor.matmul(p_c[:, j, 0:DH + 1], oT[Q % 2][:, j * P:(j + 1) * P],
                                              comb[:, 0:DH + 1], start=True, stop=True)
                    mm.then_inc(misc_mm, 1)

                def turn_maxima(h, use):
                    pe.wait_ge(s1_taken, count(h, S1, R1B + S1))
                    pe.wait_ge(misc_taken, use)
                    nc.tensor.transpose(p_mT, negm[:], ident[:]).then_inc(misc_mm, 1)

                def head(h, ahead):
                    after, buf, nxt = (h[0], h[1] + 1), h[1], (h[1] + 1) % NB
                    pe.wait_ge(m_in[buf], turns(h, MAX_IN))
                    pe.wait_ge(v_ready, count(h, 1, 1))
                    if ahead:
                        pe.wait_ge(stack_in[nxt], turns(after, STACK_IN))
                    x1, use = 0, 1
                    for b in range(NQ):
                        n1 = share[b] if ahead else 0
                        for x in range(4):
                            if x == 3 and b:
                                values(h, buf, b - 1)
                            for _ in range(n1 // 4 + (x < n1 % 4)):
                                first_pass(after, nxt, x1)
                                x1 += 1
                            second_pass(h, buf, b, x)
                        if comb_of(b) is not None:
                            combine(h, comb_of(b), use)
                            use += 1
                        if b == TURN_AT and ahead:
                            turn_maxima(after, count(h, MISC, use))
                            use += 1
                    values(h, buf, NQ - 1)
                    combine(h, NC - 1, use)

                pe.wait_ge(buf_set, 1)
                pe.wait_ge(const_step, 9 + P // VW)
                pe.wait_ge(stack_in[0], STACK_IN)
                for x in range(N1):
                    first_pass((0, 0), 0, x)
                turn_maxima((0, 0), 0)
                with pe.Fori(0, NH - NB, NB) as r:
                    for i in range(NB):
                        head((r, i), True)
                head((NH - 1, 0), False)

            @block.scalar
            def _(act):
                def head(h):
                    for b, (Q, g) in enumerate(QUADS):
                        for x in range(4):
                            k = 4 * b + x
                            off = (4 * g + x - 4 * Q) * P if Q and g == Q else 0
                            act.wait_ge(s2_mm, count(h, 4 * NQ, k + 1))
                            if x == 0:
                                act.wait_ge(pv_done, PRIMED + count(h, NQ, max(b - 1, 0)))
                            nc.scalar.activation(pt[k % RPT][:, off:TC], p_2[k % R2B][:, off:TC], ACT.Exp,
                                                 scale=DH ** -0.5).then_inc(exp_ready, 1)
                        done = Q - 1 if g == 0 and Q else (NC - 1 if b == NQ - 1 else None)
                        if done is not None:
                            act.wait_ge(pv_done, PRIMED + count(h, NQ, LAST[done] + 1))
                            act.wait_ge(misc_mm, PRIMED + count(h, MISC, done))
                            nc.scalar.copy(oT[done % 2][:], p_oT[:]).then_inc(oT_taken, 1)

                act.sem_inc(exp_ready, R2B)
                act.sem_inc(oT_taken, 1)
                with act.Fori(0, NH) as r:
                    head((r, 0))

            @block.vector
            def _(dve):
                def row_max(h, x):
                    i, kc = TILES1[x]
                    w = (i % 4 + 1) * P if kc == i // 4 else TC
                    dve.wait_ge(s1_mm, count(h, N1, x + 1))
                    nc.vector.reduce_max(mx[:, i, kc:kc + 1], p_1[x % R1B][:, 0:w], AXX).then_inc(s1_taken, 1)

                def negate(h):
                    dve.wait_ge(s1_taken, count(h, S1, R1B + N1))
                    nc.vector.tensor_reduce(negm[:], mx[:], AXX, ALU.max, negate=True).then_inc(s1_taken, 1)

                def split_maxima(h, use):
                    dve.wait_ge(misc_mm, PRIMED + use + 1)
                    nc.vector.tensor_copy(m_parts[:, 0, :], p_mT).then_inc(mstep, 1)
                    dve.wait_ge(mstep, count(h, 2, 1))
                    nc.vector.tensor_tensor(m_rest[:], p_mT, m_parts[:, 0, :], ALU.subtract).then_inc(misc_taken, 1)
                    dve.wait_ge(misc_taken, use + 1)
                    nc.vector.tensor_copy(m_parts[:, 1, :], m_rest[:]).then_inc(mstep, 1)
                    dve.wait_ge(mstep, count(h, 2, 2))
                    nc.vector.tensor_tensor(m_parts[:, 2, :], m_rest[:], m_parts[:, 1, :],
                                            ALU.subtract).then_inc(mp_ready, 1)

                def divide(h, Q, use):
                    dve.wait_ge(misc_mm, PRIMED + count(h, MISC, use + 1))
                    dve.wait_ge(misc_taken, count(h, MISC, use))
                    nc.vector.reciprocal(rec[Q % 2][:], p_c[:, :, DH]).then_inc(rec_ready, 1)
                    dve.wait_ge(rec_ready, count(h, NC, Q + 1))
                    nc.vector.tensor_tensor(att[:, Q * JT:(Q + 1) * JT, bass.ds(count(h, DH), DH)], p_c[:, :, 0:DH],
                                            rec[Q % 2][:].unsqueeze(2).to_broadcast([P, JT, DH]),
                                            ALU.mult).then_inc(misc_taken, 1)

                def head(h, ahead):
                    after, x1, use = (h[0], h[1] + 1), 0, 1
                    for b in range(NQ):
                        for _ in range(share[b] if ahead else 0):
                            row_max(after, x1)
                            x1 += 1
                        if b == NQ - SLOW - 1 and ahead:
                            negate(after)
                        if comb_of(b) is not None:
                            divide(h, comb_of(b), use)
                            use += 1
                        if b == TURN_AT and ahead:
                            dve.wait_ge(m_in[h[1]], turns(h, MAX_IN))
                            split_maxima(after, count(h, MISC, use))
                            use += 1
                    divide(h, NC - 1, use)

                dve.sem_inc(s1_taken, R1B)
                for i in range(NB):
                    nc.vector.memset(vh[i][:], 0.0).then_inc(consts, 1)
                    nc.vector.memset(ks[i][SR:SR + 3, :], 1.0).then_inc(consts, 1)
                nc.vector.memset(mx[:], NEG).then_inc(consts, 1)
                dve.wait_ge(consts, 2 * NB + 1)
                for i in range(NB):
                    st = nc.vector.memset(vh[i][:, :, DH:DH + 1], 1.0)
                st.then_inc(buf_set, 1)
                for x in range(N1):
                    row_max((0, 0), x)
                negate((0, 0))
                split_maxima((0, 0), 0)
                with dve.Fori(0, NH - NB, NB) as r:
                    for i in range(NB):
                        head((r, i), True)
                head((NH - 1, 0), False)


E1 = 8
DF = 1024
KF = DF // P
BLOCKS = TT + E1 - 1


def attention_out(nc, S, D, keep):
    xn, att, aff = keep["xn"], keep["att"], keep["aff"]
    with Mem(nc) as m:
        w_o = m.sb("s7_w_o", [P, KD, DM])
        cent = m.sb("s7_cent", [P, KD, E1])
        zeros = m.sb("s7_zeros", [P, DM])
        ident = m.sb("s7_ident", [P, P])
        ya = [m.sb(f"s7_ya{i}", [P, JT, DM]) for i in range(2)]
        yT = [m.sb(f"s7_yT{i}", [P, KD, TC]) for i in range(2)]
        p_u = [m.ps(f"s7_p_u{i}", [P, TC]) for i in range(KD)]
        p_t = [m.ps(f"s7_p_t{i}", [P, TC]) for i in range(KD)]
        p_o = [m.ps(f"s7_p_o{i}", [P, 2, DM]) for i in range(JT // 2)]
        p_a = m.ps("s7_p_a", [P, JT, E1])
        R = NormRing(m, S, "s7a")
        R2 = NormRing(m, S, "s7b", of=R)
        x3T = yT
        w_loaded, cleared, ident_ready = S("w_loaded"), S("cleared"), S("ident_ready")
        zeros_ready, zero_out = S("zeros_ready"), S("zero_out")
        gate = S("gate")
        att_taken, att_turned, yT_ready, out_ready = S("att_taken"), S("att_turned"), S("yT_ready"), S("out_ready")
        kept, turned, x3T_ready, aff_mm, aff_taken, kept2 = (
            S("kept"), S("turned"), S("x3T_ready"), S("aff_mm"), S("aff_taken"), S("kept2"))

        with nc.Block() as block:
            @block.sync
            def _(sp):
                prime(sp, [att_turned, yT_ready, x3T_ready, aff_taken, aff_mm, kept, turned, kept2, *R.primed, *R2.primed])
                sp.dma_start(w_o[:], D["w_o"].rearrange("(k p) n -> p k n", p=P)).then_inc(w_loaded, 16)
                sp.dma_start(cent[:], D["cent"].rearrange("(k p) n -> p k n", p=P)).then_inc(w_loaded, 16)
                sp.wait_ge(zeros_ready, 1)
                sp.dma_start(D["sorted_in"].rearrange("(b p) n -> p b n", p=P),
                             zeros[:].unsqueeze(1).to_broadcast([P, BLOCKS, DM])).then_inc(zero_out, 16)
                for e in range(E1):
                    sp.dma_start(keep["w1"][:, e * KD:(e + 1) * KD, :],
                                 D["w1"][e].rearrange("(k p) n -> p k n", p=P)).then_inc(keep["w1_in"], 16)
                sp.wait_ge(zero_out, 16)

            @block.gpsimd
            def _(pool):
                pool.memset(zeros[:], 0.0).then_inc(zeros_ready, 1)
                set_identity(pool, ident, cleared, ident_ready)
                with pool.Fori(0, NC - 1, 2) as c:
                    for par in range(2):
                        pool.wait_ge(att_turned, PRIMED + c)
                        pool.tensor_copy(ya[par][:], att[:, bass.ds((c + par) * JT, JT), :]).then_inc(att_taken, 1)
                    for par in range(2):
                        at = bass.ds((c + par) * JT, JT)
                        pool.wait_ge(R.norm_ready, PRIMED + c * JT + (par + 1) * JT)
                        pool.tensor_tensor(xn[:, at, :], R.y[par][:], R.y[par][:], ALU.add).then_inc(kept, 1)
                    for par in range(2):
                        at = bass.ds((c + par) * JT, JT)
                        pool.wait_ge(R2.norm_ready, PRIMED + c * JT + (par + 1) * JT)
                        pool.wait_ge(att_taken, c + (par + 1))
                        pool.sem_inc(gate, 1)
                        pool.tensor_copy(att[:, at, :], R2.y[par][:]).then_inc(kept2, 1)

            @block.tensor
            def _(pe):
                pe.wait_ge(w_loaded, 32)
                pe.wait_ge(ident_ready, 1)
                with pe.Fori(0, NC - 1, 2) as c:
                    for par in range(2):
                        pe.wait_ge(att_taken, c + (par + 1))
                        pe.wait_ge(yT_ready, PRIMED + c + par)
                        for k in range(KD):
                            for j in range(JT):
                                tr = nc.tensor.transpose(p_u[k][:, j * P:(j + 1) * P],
                                                         ya[par][:, j, k * P:(k + 1) * P], ident[:])
                        tr.then_inc(att_turned, 1)
                    for par in range(2):
                        pe.wait_ge(yT_ready, PRIMED + c + (par + 1))
                        for i in range(JT // 2):
                            pe.wait_ge(R.sum_ready, PRIMED + c * JT + (2 * i + 2 if par else 0))
                            for j in range(2):
                                at = (2 * i + j) * P
                                for k in range(KD):
                                    mm = nc.tensor.matmul(p_o[i][:, j, :], yT[par][:, k, at:at + P], w_o[:, k, :],
                                                          start=k == 0, stop=k == KD - 1)
                            mm.then_inc(out_ready, 1)
                    for par in range(2):
                        pe.wait_ge(R.norm_ready, PRIMED + c * JT + (par + 1) * JT)
                        pe.wait_ge(x3T_ready, PRIMED + c + par)
                        for k in range(KD):
                            for j in range(JT):
                                tr = nc.tensor.transpose(p_t[k][:, j * P:(j + 1) * P],
                                                         R.y[par][:, j, k * P:(k + 1) * P], ident[:])
                        tr.then_inc(turned, 1)
                    for par in range(2):
                        pe.wait_ge(x3T_ready, PRIMED + c + (par + 1))
                        pe.wait_ge(aff_taken, PRIMED + c + par)
                        for j in range(JT):
                            for k in range(KD):
                                mm = nc.tensor.matmul(p_a[:, j, :], x3T[par][:, k, j * P:(j + 1) * P],
                                                      cent[:, k, :], start=k == 0, stop=k == KD - 1)
                        mm.then_inc(aff_mm, 1)

            @block.scalar
            def _(act):
                act.wait_ge(R.eps_ready, 1)
                act.wait_ge(R2.eps_ready, 1)
                with act.Fori(0, NC - 1, 2) as c:
                    for par in range(2):
                        act.wait_ge(att_turned, PRIMED + c + (par + 1))
                        act.wait_ge(aff_mm, PRIMED + c)
                        for k in range(KD):
                            cp = nc.scalar.copy(yT[par][:, k, :], p_u[k][:])
                        cp.then_inc(yT_ready, 1)
                    R.scalar_std(act, c, 0)
                    R.scalar_std(act, c, 1)
                    for par in range(2):
                        act.wait_ge(turned, PRIMED + c + (par + 1))
                        for k in range(KD):
                            cp = nc.scalar.copy(x3T[par][:, k, :], p_t[k][:])
                        cp.then_inc(x3T_ready, 1)
                    R2.scalar_std(act, c, 0)
                    R2.scalar_std(act, c, 1)
                    for par in range(2):
                        act.wait_ge(aff_mm, PRIMED + c + (par + 1))
                        nc.scalar.copy(aff[:, bass.ds((c + par) * JT, JT), :], p_a[:]).then_inc(aff_taken, 1)

            @block.vector
            def _(dve):
                R.vector_setup(dve)
                R2.vector_setup(dve)
                with dve.Fori(0, NC - 1, 2) as c:
                    dve.wait_ge(R.norm_ready, PRIMED + c * JT)
                    for par in range(2):
                        for i in range(JT // 2):
                            dve.wait_ge(out_ready, c * 2 + (2 * par + i + 1))
                            nc.vector.tensor_tensor(R.s[par][:, 2 * i:2 * i + 2, :], p_o[i][:],
                                                    xn[:, bass.ds(c * JT + (par * JT + 2 * i), 2), :],
                                                    ALU.add).then_inc(R.sum_ready, 2)
                        R.vector_stats(dve, c, par)
                    dve.wait_ge(R2.norm_ready, PRIMED + c * JT)
                    for par in range(2):
                        dve.wait_ge(kept, PRIMED + c + par)
                        dve.wait_ge(turned, PRIMED + c)
                        R.vector_norm(dve, c, par)
                    for par in range(2):
                        R2.vector_stats(dve, c, par)
                    for par in range(2):
                        dve.wait_ge(kept2, PRIMED + c + par)
                        R2.vector_norm(dve, c, par)


def route(nc, S, D, keep):
    att, aff, alpha, slot, expert_of = (keep[n] for n in ("att", "aff", "alpha", "slot", "expert_of"))
    with Mem(nc) as m:
        top = m.sb("s8_top", [P, TT])
        order = m.sb("s8_order", [P, 1, E1])
        hit = m.sb("s8_hit", [P, TT, E1])
        first = m.sb("s8_first", [P, TT])
        onehot = m.sb("s8_onehot", [P, TT, E1])
        onehot_b = m.sb("s8_onehot_b", [P, TT, E1], BF16)
        triangle = m.sb("s8_triangle", [P, P], BF16)
        ones = m.sb("s8_ones", [P, P], BF16)
        ex = m.sb("s8_ex", [P, TT])
        count = m.sb("s8_count", [P, E1, TT])
        carry = m.sb("s8_carry", [P, E1, TT])
        upto = m.sb("s8_upto", [P, E1, TT])
        before = m.sb("s8_before", [P, E1, TT])
        steps = m.sb("s8_steps", [P, 1, BLOCKS])
        starts = m.sb("s8_starts", [P, 1, TT])
        over = m.sb("s8_over", [P, E1, TT])
        need = m.sb("s8_need", [P, E1])
        ones8 = m.sb("s8_ones8", [P, E1])
        ends = m.sb("s8_ends", [P, E1])
        base = m.sb("s8_base", [P, E1])
        place = m.sb("s8_place", [P, TT, E1])
        slot_f = m.sb("s8_slot_f", [P, TT])
        past = m.sb("s8_past", [1, BLOCKS, E1])
        number = m.sb("s8_number", [1, BLOCKS])
        p_rank = m.ps("s8_p_rank", [P, TT, E1])
        p_count = m.ps("s8_p_count", [P, TT, E1])
        consts, tri_step, onehot_ready, rank_mm = S("consts"), S("tri_step"), S("onehot_ready"), S("rank_mm")
        step, top_ready, exp_ready, slots_ready, scattered = (
            S("step"), S("top_ready"), S("exp_ready"), S("slots_ready"), S("scattered"))
        NCONST = 6 + E1

        with nc.Block() as block:
            @block.sync
            def _(sp):
                for e in range(E1):
                    sp.dma_start(keep["w2"][:, e * KF:(e + 1) * KF, :],
                                 D["w2"][e].rearrange("(k p) n -> p k n", p=P)).then_inc(keep["w2_in"], 16)

            @block.gpsimd
            def _(pool):
                for e in range(E1):
                    pool.memset(order[:, :, e:e + 1], float(E1 - e)).then_inc(consts, 1)
                pool.iota(steps[:, 0, :], pattern=[[1, BLOCKS]], base=0, channel_multiplier=0,
                          allow_small_or_imprecise_dtypes=True).then_inc(consts, 1)
                pool.iota(starts[:, 0, :], pattern=[[P, TT]], base=0, channel_multiplier=0,
                          allow_small_or_imprecise_dtypes=True).then_inc(consts, 1)
                pool.memset(ones[:], 1.0).then_inc(consts, 1)
                pool.memset(ones8[:], 1.0).then_inc(consts, 1)
                pool.memset(carry[:], 1.0).then_inc(tri_step, 1)
                pool.memset(triangle[:], 1.0).then_inc(tri_step, 1)
                pool.wait_ge(tri_step, 2)
                pool.memset(carry[:, :, 0:1], 0.0).then_inc(consts, 1)
                pool.affine_select(out=triangle[:], in_=triangle[:], compare_op=ALU.is_gt, fill=0.0, base=0,
                                   pattern=[[1, P]], channel_multiplier=-1).then_inc(consts, 1)
                pool.wait_ge(slots_ready, 1)
                for t in range(TT):
                    pool.indirect_dma_start(D["sorted_in"][:], bass.IndirectOffsetOnAxis(ap=slot[:, t:t + 1], axis=0),
                                            att[:, t, :], None).then_inc(scattered, 16)
                pool.wait_ge(scattered, 16 * TT)

            @block.tensor
            def _(pe):
                pe.wait_ge(consts, NCONST)
                pe.wait_ge(onehot_ready, 1)
                nc.tensor.matmul(p_rank[:], triangle[:], onehot_b[:], start=True, stop=True)
                nc.tensor.matmul(p_count[:], ones[:], onehot_b[:], start=True, stop=True).then_inc(rank_mm, 1)

            @block.scalar
            def _(act):
                act.wait_ge(top_ready, 1)
                nc.scalar.activation(ex[:], top[:], ACT.Exp, scale=-1.0).then_inc(exp_ready, 1)

            @block.vector
            def _(dve):
                dve.wait_ge(consts, NCONST)
                nc.vector.tensor_reduce(top[:], aff[:], AXX, ALU.max).then_inc(top_ready, 1)
                dve.wait_ge(top_ready, 1)
                nc.vector.tensor_tensor(hit[:], aff[:], top[:].unsqueeze(2).to_broadcast([P, TT, E1]),
                                        ALU.is_equal).then_inc(step, 1)
                dve.wait_ge(step, 1)
                nc.vector.tensor_tensor(hit[:], hit[:], order[:].to_broadcast([P, TT, E1]), ALU.mult).then_inc(step, 1)
                dve.wait_ge(step, 2)
                nc.vector.tensor_reduce(first[:], hit[:], AXX, ALU.max).then_inc(step, 1)
                dve.wait_ge(step, 3)
                nc.vector.tensor_tensor(onehot[:], hit[:], first[:].unsqueeze(2).to_broadcast([P, TT, E1]),
                                        ALU.is_equal).then_inc(step, 1)
                dve.wait_ge(step, 4)
                nc.vector.tensor_copy(onehot_b[:], onehot[:]).then_inc(onehot_ready, 1)
                dve.wait_ge(exp_ready, 1)
                nc.vector.tensor_scalar(ex[:], ex[:], 1.0, None, ALU.add).then_inc(step, 1)
                dve.wait_ge(step, 5)
                nc.vector.reciprocal(alpha[:], ex[:]).then_inc(step, 1)
                dve.wait_ge(step, 6)
                dve.wait_ge(rank_mm, 1)
                nc.vector.tensor_copy(count[:], p_count[:].rearrange("p t e -> p e t")).then_inc(step, 1)
                dve.wait_ge(step, 7)
                nc.vector.tensor_tensor_scan(upto[:].rearrange("p e t -> p (e t)"),
                                             carry[:].rearrange("p e t -> p (e t)"),
                                             count[:].rearrange("p e t -> p (e t)"), 0.0, ALU.mult, ALU.add).then_inc(step, 1)
                dve.wait_ge(step, 8)
                nc.vector.tensor_tensor(before[:], upto[:], count[:], ALU.subtract).then_inc(step, 1)
                dve.wait_ge(step, 9)
                nc.vector.tensor_tensor(over[:], upto[:, :, TT - 1:TT].to_broadcast([P, E1, TT]),
                                        starts[:].to_broadcast([P, E1, TT]), ALU.is_gt).then_inc(step, 1)
                dve.wait_ge(step, 10)
                nc.vector.tensor_reduce(need[:], over[:], AXX, ALU.add).then_inc(step, 1)
                dve.wait_ge(step, 11)
                nc.vector.tensor_tensor_scan(ends[:], ones8[:], need[:], 0.0, ALU.mult, ALU.add).then_inc(step, 1)
                dve.wait_ge(step, 12)
                nc.vector.tensor_tensor(base[:], ends[:], need[:], ALU.subtract).then_inc(step, 1)
                dve.wait_ge(step, 13)
                nc.vector.tensor_scalar(base[:], base[:], float(P), None, ALU.mult).then_inc(step, 1)
                dve.wait_ge(step, 14)
                nc.vector.tensor_tensor(before[:], before[:], base[:].unsqueeze(2).to_broadcast([P, E1, TT]),
                                        ALU.add).then_inc(step, 1)
                dve.wait_ge(step, 15)
                nc.vector.tensor_tensor(place[:], p_rank[:], before[:].rearrange("p e t -> p t e"), ALU.add).then_inc(step, 1)
                dve.wait_ge(step, 16)
                nc.vector.tensor_tensor(place[:], place[:], onehot[:], ALU.mult).then_inc(step, 1)
                dve.wait_ge(step, 17)
                nc.vector.tensor_reduce(slot_f[:], place[:], AXX, ALU.add).then_inc(step, 1)
                dve.wait_ge(step, 18)
                nc.vector.tensor_copy(slot[:], slot_f[:]).then_inc(slots_ready, 1)
                nc.vector.tensor_tensor(past[:], ends[0:1, :].unsqueeze(1).to_broadcast([1, BLOCKS, E1]),
                                        steps[0:1, 0, :].unsqueeze(2).to_broadcast([1, BLOCKS, E1]), ALU.is_le).then_inc(step, 1)
                dve.wait_ge(step, 19)
                nc.vector.tensor_reduce(number[:], past[:], AXX, ALU.add).then_inc(step, 1)
                dve.wait_ge(step, 20)
                nc.vector.tensor_scalar(number[:], number[:], float(E1 - 1), None, ALU.min).then_inc(step, 1)
                dve.wait_ge(step, 21)
                nc.vector.tensor_copy(expert_of[:], number[:]).then_inc(step, 1)
                dve.wait_ge(step, 22)


def experts(nc, S, D, keep):
    w1, w2, expert_of = keep["w1"], keep["w2"], keep["expert_of"]
    N3 = 3
    TURNS = BLOCKS // N3
    with Mem(nc) as m:
        ln = m.sb("s9_ln", [P, E1, KD, 2])
        b1 = m.sb("s9_b1", [P, E1 * KF])
        b2 = m.sb("s9_b2", [P, E1, DM])
        ident = m.sb("s9_ident", [P, P])
        area = keep["att"][:].rearrange("p (n k) d -> p n (k d)", k=KF // KD)
        h = [area[:, i, :] for i in range(N3)]
        hT = [area[:, N3 + i, :].rearrange("p (k t) -> p k t", t=P) for i in range(N3)]
        xb = [area[:, 2 * N3, i * DM:(i + 1) * DM] for i in range(N3)]
        xT = [area[:, 2 * N3 + 1, i * DM:(i + 1) * DM].rearrange("p (k t) -> p k t", t=P) for i in range(N3)]
        y = [m.sb(f"s9_y{i}", [P, DM]) for i in range(N3)]
        p_x = m.ps("s9_p_x", [P, KD, P])
        p_h = [m.ps(f"s9_p_h{i}", [P, TC]) for i in range(2)]
        p_t = [m.ps(f"s9_p_t{i}", [P, KF // 2, P]) for i in range(2)]
        p_y = m.ps("s9_p_y", [P, DM])
        vec_in, cleared, ident_ready = S("vec_in"), S("cleared"), S("ident_ready")
        x_in = [S(f"x_in{i}") for i in range(N3)]
        y_out = [S(f"y_out{i}") for i in range(N3)]
        x_turned, xT_ready, h_mm, h_taken = S("x_turned"), S("xT_ready"), S("h_mm"), [S("h0_taken"), S("h1_taken")]
        h_turned, hT_ready = S("h_turned"), [S("hT0_ready"), S("hT1_ready")]
        y_mm, y_ready = S("y_mm"), S("y_ready")

        def n(q, i, per, more):
            return q * (N3 * per) + (i * per + more)

        def expert(eng, q, i):
            return eng.value_load(expert_of[0:1, bass.ds(q * N3 + i, 1)], min_val=0, max_val=E1 - 1)

        with nc.Block() as block:
            @block.sync
            def _(sp):
                prime(sp, [*hT_ready, y_ready, *y_out])
                def load(q, i):
                    sp.dma_start(xb[i % N3][:], D["sorted_in"][bass.ds(q * (N3 * P) + i * P, P), :]
                                 ).then_inc(x_in[i % N3], 16)

                def store(q, i):
                    sp.wait_ge(y_ready, PRIMED + n(q, i, 1, 1))
                    sp.dma_start(D["sorted_out"][bass.ds(q * (N3 * P) + i * P, P), :], y[i][:]).then_inc(y_out[i], 16)

                for i in range(N3):
                    load(0, i)
                sp.dma_start(ln[:], D["ln"]).then_inc(vec_in, 16)
                sp.dma_start(b1[:], D["b1"]).then_inc(vec_in, 16)
                sp.dma_start(b2[:], D["b2"]).then_inc(vec_in, 16)
                with sp.Fori(0, TURNS - 1) as q:
                    for i in range(N3):
                        sp.wait_ge(x_turned, n(q, i, 1, 1))
                        load(q, i + N3)
                        store(q, i)
                for i in range(N3):
                    store(TURNS - 1, i)
                for i in range(N3):
                    sp.wait_ge(y_out[i], PRIMED + 16 * TURNS)

            @block.gpsimd
            def _(pool):
                set_identity(pool, ident, cleared, ident_ready)

            @block.tensor
            def _(pe):
                def turn_x(q, i):
                    pe.wait_ge(x_in[i % N3], q * 16 + (i // N3 + 1) * 16)
                    pe.wait_ge(xT_ready, n(q, i, 1, 0))
                    for k in range(KD):
                        tr = nc.tensor.transpose(p_x[:, k, :], xb[i % N3][:, k * P:(k + 1) * P], ident[:])
                    tr.then_inc(x_turned, 1)

                def hidden(q, i, e, half):
                    pe.wait_ge(xT_ready, n(q, i, 1, 1))
                    pe.wait_ge(h_taken[half], n(q, i, 1, 0))
                    for k in range(KD):
                        mm = nc.tensor.matmul(p_h[half][:], xT[i % N3][:, k, :],
                                              w1[:, e * KD + k, half * TC:(half + 1) * TC],
                                              start=k == 0, stop=k == KD - 1)
                    mm.then_inc(h_mm, 1)

                def turn_hidden(q, i, half):
                    pe.wait_ge(h_taken[half], n(q, i, 1, 1))
                    pe.wait_ge(hT_ready[half], PRIMED + n(q, i, 1, 0))
                    for k in range(KF // 2):
                        at = (half * (KF // 2) + k) * P
                        tr = nc.tensor.transpose(p_t[half][:, k, :], h[i][:, at:at + P], ident[:])
                    tr.then_inc(h_turned, 1)

                def down(q, i, e):
                    pe.wait_ge(y_ready, PRIMED + n(q, i, 1, 0))
                    for k in range(KF):
                        if k % (KF // 2) == 0:
                            pe.wait_ge(hT_ready[k // (KF // 2)], PRIMED + n(q, i, 1, 1))
                        mm = nc.tensor.matmul(p_y[:], hT[i][:, k, :], w2[:, e * KF + k, :],
                                              start=k == 0, stop=k == KF - 1)
                    mm.then_inc(y_mm, 1)

                def block_step(q, i, last):
                    ahead = not last or i + 1 < N3
                    if ahead:
                        e_next = expert(pe, q, i + 1)
                    for half in range(2):
                        if ahead:
                            hidden(q, i + 1, e_next, half)
                        turn_hidden(q, i, half)
                    if not last or i + 2 < N3:
                        turn_x(q, i + 2)
                    down(q, i, expert(pe, q, i))

                pe.wait_ge(ident_ready, 1)
                pe.wait_ge(keep["w1_in"], 16 * E1)
                turn_x(0, 0)
                turn_x(0, 1)
                e = expert(pe, 0, 0)
                hidden(0, 0, e, 0)
                hidden(0, 0, e, 1)
                pe.wait_ge(keep["w2_in"], 16 * E1)
                with pe.Fori(0, TURNS - 1) as q:
                    for i in range(N3):
                        block_step(q, i, False)
                for i in range(N3):
                    block_step(TURNS - 1, i, True)

            @block.scalar
            def _(act):
                def take_hidden(q, i):
                    act.wait_ge(h_mm, n(q, i, 2, 1))
                    nc.scalar.copy(h[i % N3][:, 0:TC], p_h[0][:]).then_inc(h_taken[0], 1)

                def block_step(q, i, last):
                    if not last or i + 1 < N3:
                        take_hidden(q, i + 1)
                    e = expert(act, q, i)
                    act.wait_ge(h_turned, n(q, i, 2, 1))
                    for k in range(KF // 2):
                        rl = nc.scalar.activation(hT[i][:, k, :], p_t[0][:, k, :], ACT.Relu,
                                                  bias=b1[:, bass.ds(e * KF + k, 1)])
                    rl.then_inc(hT_ready[0], 1)

                act.wait_ge(vec_in, 48)
                take_hidden(0, 0)
                with act.Fori(0, TURNS - 1) as q:
                    for i in range(N3):
                        block_step(q, i, False)
                for i in range(N3):
                    block_step(TURNS - 1, i, True)

            @block.vector
            def _(dve):
                def take_x(q, i):
                    e = expert(dve, q, i)
                    dve.wait_ge(x_turned, n(q, i, 1, 1))
                    for k in range(KD):
                        ts = nc.vector.tensor_scalar(xT[i % N3][:, k, :], p_x[:, k, :], ln[:, e, k, 0:1],
                                                     ln[:, e, k, 1:2], ALU.mult, ALU.add)
                    ts.then_inc(xT_ready, 1)

                def take_hidden(q, i):
                    dve.wait_ge(h_mm, n(q, i, 2, 2))
                    nc.vector.tensor_copy(h[i % N3][:, TC:2 * TC], p_h[1][:]).then_inc(h_taken[1], 1)

                def block_step(q, i, last):
                    if not last or i + 1 < N3:
                        take_hidden(q, i + 1)
                    e = expert(dve, q, i)
                    dve.wait_ge(h_turned, n(q, i, 2, 2))
                    for k in range(KF // 2):
                        rl = nc.vector.tensor_scalar(hT[i][:, KF // 2 + k, :], p_t[1][:, k, :],
                                                     b1[:, bass.ds(e * KF + KF // 2 + k, 1)], 0.0, ALU.add, ALU.max)
                    rl.then_inc(hT_ready[1], 1)
                    if not last or i + 2 < N3:
                        take_x(q, i + 2)
                    dve.wait_ge(y_mm, n(q, i, 1, 1))
                    dve.wait_ge(y_out[i], PRIMED + q * 16)
                    nc.vector.tensor_tensor(y[i][:], p_y[:], b2[:, e, :], ALU.add).then_inc(y_ready, 1)

                dve.wait_ge(vec_in, 48)
                take_x(0, 0)
                take_x(0, 1)
                take_hidden(0, 0)
                with dve.Fori(0, TURNS - 1) as q:
                    for i in range(N3):
                        block_step(q, i, False)
                for i in range(N3):
                    block_step(TURNS - 1, i, True)


def finish(nc, S, D, keep):
    xn, alpha, slot = keep["xn"], keep["alpha"], keep["slot"]
    with Mem(nc) as m:
        f = [m.sb(f"s10_f{i}", [P, JT, DM]) for i in range(2)]
        R = NormRing(m, S, "s10")
        gathered = [S(f"gathered{i}") for i in range(2)]
        out_done = [S(f"out_done{i}") for i in range(2)]

        with nc.Block() as block:
            @block.sync
            def _(sp):
                prime(sp, [*out_done, *R.primed])
                with sp.Fori(0, NC - 1, 2) as c:
                    for par in range(2):
                        sp.wait_ge(R.norm_ready, PRIMED + c * JT + (par + 1) * JT)
                        sp.dma_start(D["out"][0, bass.ds((c + par) * TC, TC), :].rearrange("(j p) n -> p j n", p=P),
                                     R.y[par][:]).then_inc(out_done[par], 16)
                for par in range(2):
                    sp.wait_ge(out_done[par], PRIMED + 16 * NC // 2)

            @block.gpsimd
            def _(pool):
                for t in range(TT):
                    par = t // JT % 2
                    if t >= 2 * JT:
                        pool.wait_ge(R.sum_ready, PRIMED + t - 2 * JT + 1)
                    pool.indirect_dma_start(f[par][:, t % JT, :], None, D["sorted_out"][:],
                                            bass.IndirectOffsetOnAxis(ap=slot[:, t:t + 1], axis=0)
                                            ).then_inc(gathered[par], 16)

            @block.scalar
            def _(act):
                act.wait_ge(R.eps_ready, 1)
                with act.Fori(0, NC - 1, 2) as c:
                    R.scalar_std(act, c, 0)
                    R.scalar_std(act, c, 1)

            @block.vector
            def _(dve):
                R.vector_setup(dve)
                with dve.Fori(0, NC - 1, 2) as c:
                    dve.wait_ge(R.norm_ready, PRIMED + c * JT)
                    for par in range(2):
                        dve.wait_ge(gathered[par], c * (8 * JT) + 16 * JT)
                        for j in range(JT):
                            t = c * JT + (par * JT + j)
                            nc.vector.scalar_tensor_tensor(
                                out=R.s[par][:, j, :], in0=f[par][:, j, :], scalar=alpha[:, bass.ds(t, 1)],
                                in1=xn[:, t, :], op0=ALU.mult, op1=ALU.add).then_inc(R.sum_ready, 1)
                        R.vector_stats(dve, c, par)
                    for par in range(2):
                        dve.wait_ge(out_done[par], PRIMED + c * 8)
                        R.vector_norm(dve, c, par)


SCRATCH = {
    "sz": ((DI, L), F32), "u": ((DI, L), F32), "delta": ((DI, L), F32), "yz": ((DI, L), F32),
    "qk": ((2 * 3 * DM, L), BF16),
    "sorted_in": ((BLOCKS * P, DM), F32), "sorted_out": ((BLOCKS * P, DM), F32),
}


def build(nc, D, out):
    D = dict(D)
    D["out"] = out
    for name, (shape, dt) in SCRATCH.items():
        D[name] = nc.dram_tensor(name, shape, dt, kind="Internal").ap()
    with Mem(nc) as top:
        keep = {}
        with Mem(nc) as m:
            keep["bc_parts"] = m.sb("bc_parts", [3 * 2 * NS, L], BF16)
            with Mem(nc) as st:
                mixer_front(nc, st.sem, D, keep)
                st.clear_sems()
            with Mem(nc) as st:
                mixer_scan(nc, st.sem, D, keep)
                st.clear_sems()
        keep["xn"] = top.sb("xn", [P, TT, DM])
        keep["aff"] = top.sb("aff", [P, TT, E1])
        keep["alpha"] = top.sb("alpha", [P, TT])
        keep["slot"] = top.sb("slot", [P, TT], U32)
        keep["expert_of"] = top.sb("expert_of", [1, BLOCKS], I32)
        keep["w1_in"], keep["w2_in"] = top.sem("w1_in"), top.sem("w2_in")
        with Mem(nc) as ex:
            keep["att"] = ex.sb("att", [P, TT, DM])
            with Mem(nc) as v:
                keep["v_all"] = v.sb("v_all", [P, NH, TT, DH])
                with Mem(nc) as m:
                    keep["xt"] = m.sb("xt", [P, KD, L])
                    for n, stage in ((3, mixer_out), (4, adapter), (5, qkv)):
                        with Mem(nc) as st:
                            stage(nc, st.sem, D, keep)
                with Mem(nc) as st:
                    attention(nc, st.sem, D, keep)
            keep["w1"] = ex.sb("w1", [P, E1 * KD, DF])
            with Mem(nc) as st:
                attention_out(nc, st.sem, D, keep)
            keep["w2"] = ex.sb("w2", [P, E1 * KF, DM])
            with Mem(nc) as st:
                route(nc, st.sem, D, keep)
            with Mem(nc) as st:
                experts(nc, st.sem, D, keep)
        with Mem(nc) as st:
            finish(nc, st.sem, D, keep)


def lay_out(x):
    import numpy as np

    def T(a):
        return np.ascontiguousarray(a.T)
    X = x["L0_attn_x"][0]
    w_x = x["L0_attn_W_x"]
    a = {
        "xT": T(X), "x": np.ascontiguousarray(X),
        "w_in": T(x["L0_attn_W_in"]),
        "w_x": T(np.concatenate([w_x[RK:], w_x[:RK]])),
        "w_dt": T(x["L0_attn_W_dt"]),
        "mixer_vecs": np.concatenate([x["L0_attn_conv_w"][:, 0, :], x["L0_attn_conv_b"][:, None],
                                      x["L0_attn_b_dt"][:, None]], 1),
        "scan_vecs": np.concatenate([x["L0_attn_A_log"], x["L0_attn_D_param"][:, None]], 1),
        "w_out": T(x["L0_attn_W_out"]),
        "disc": np.concatenate([T(x["L0_ffn_disc_mu"]), T(x["L0_ffn_disc_sigma"])], 1),
        "base": T(x["L0_ffn_base_W"]), "base_b": x["L0_ffn_base_b"][None],
        "down": x["L0_ffn_down_W"], "down_b": x["L0_ffn_down_b"].reshape(-1, 1),
        "up": np.concatenate([x["L0_ffn_up_W"].transpose(0, 2, 1), x["L0_ffn_up_b"][:, :, None]], 2),
        "w_qk": np.concatenate([T(x["L1_attn_W_Q"]), T(x["L1_attn_W_K"])], 1), "w_v": T(x["L1_attn_W_V"]),
        "outm": x["L0_ffn_conv_W"].transpose(0, 2, 1), "outm_b": x["L0_ffn_conv_b"],
        "w_o": T(x["L1_attn_W_O"]), "cent": T(x["L1_ffn_centroids"]),
        "ln": np.stack([x["L1_ffn_ln_g"], x["L1_ffn_ln_b"]], -1).reshape(E1, KD, P, 2).transpose(2, 0, 1, 3),
        "w1": x["L1_ffn_w1"].transpose(0, 2, 1), "w2": x["L1_ffn_w2"].transpose(0, 2, 1),
        "b1": T(x["L1_ffn_b1"].reshape(E1 * KF, P)),
        "b2": np.broadcast_to(x["L1_ffn_b2"][None], (P, E1, DM)),
    }
    return {k: np.ascontiguousarray(v) for k, v in a.items()}


def kernel(**inputs):
    import numpy as np
    import concourse.bacc as _bacc
    from concourse.bass_utils import run_bass_kernel_spmd as _run

    arrays = lay_out({name: np.asarray(a) for name, a in inputs.items()})
    nc = _bacc.Bacc("TRN2", target_bir_lowering=False, num_devices=1)
    D = {n: nc.dram_tensor(f"in_{n}", a.shape, mybir.dt.from_np(a.dtype), kind="ExternalInput").ap()
         for n, a in arrays.items()}
    out = nc.dram_tensor("out", (1, L, DM), F32, kind="ExternalOutput").ap()
    build(nc, D, out)
    r = _run(nc, [{f"in_{n}": a for n, a in arrays.items()}], core_ids=[0])
    return r.results[0]["out"]
```

```python
from contextlib import ExitStack

import concourse.bass as bass
from concourse import mybir

F32 = mybir.dt.float32
BF16 = mybir.dt.bfloat16
I32 = mybir.dt.int32
U32 = mybir.dt.uint32
ALU = mybir.AluOpType
ACT = mybir.ActivationFunctionType
AXX = mybir.AxisListType.X

P = 128
L = 4096
DM = 256
KD = DM // P
DI = 512
ND = DI // P
NS = 16
RK = 16
KC = 4
TC = 512
NC = L // TC
TT = L // P
JT = TC // P
EPS = 1e-5


PRIMED = 1


def prime(sp, sems):
    for sem in sems:
        sp.sem_inc(sem, PRIMED)


class Mem:

    def __init__(self, nc):
        self.nc, self.stack, self.sems = nc, ExitStack(), []

    def __enter__(self):
        self.stack.__enter__()
        return self

    def __exit__(self, *a):
        return self.stack.__exit__(*a)

    def sb(self, name, shape, dt=F32):
        return self.stack.enter_context(self.nc.sbuf_tensor(name, shape, dt))

    def ps(self, name, shape, dt=F32):
        return self.stack.enter_context(self.nc.psum_tensor(name, shape, dt))

    def sem(self, name):
        self.sems.append(self.stack.enter_context(self.nc.semaphore(name)))
        return self.sems[-1]

    def clear_sems(self):
        with self.nc.Block() as block:
            @block.gpsimd
            def _(pool):
                pool.sem_clear(range(self.sems[0].num, self.sems[-1].num + 1))


def mixer_front(nc, S, D, keep):
    bc_parts = keep["bc_parts"]
    with Mem(nc) as m:
        xT = m.sb("s1_xT", [P, KD, L])
        w_in = m.sb("s1_w_in", [P, KD, 2 * DI])
        w_x = m.sb("s1_w_x", [P, ND, RK + 2 * NS])
        w_dt = m.sb("s1_w_dt", [RK, DI])
        vecs = m.sb("s1_vecs", [P, ND, KC + 2])
        xp = m.sb("s1_xp", [P, ND, KC - 1 + TC])
        conv = m.sb("s1_conv", [P, ND, TC])
        u = m.sb("s1_u", [P, ND, TC])
        sz = m.sb("s1_sz", [P, ND, TC])
        dlt = m.sb("s1_dlt", [RK, TC])
        bc_rest = m.sb("s1_bc_rest", [2 * NS, TC])
        bc_mid = m.sb("s1_bc_mid", [2 * NS, TC], BF16)
        absv = m.sb("s1_absv", [P, ND, TC])
        ex = m.sb("s1_ex", [P, ND, TC])
        ex1 = m.sb("s1_ex1", [P, ND, TC])
        lost = m.sb("s1_lost", [P, ND, TC])
        lnv = m.sb("s1_lnv", [P, ND, TC])
        relu = m.sb("s1_relu", [P, ND, TC])
        delta = m.sb("s1_delta", [P, ND, TC])
        p_proj = [m.ps(f"s1_p_proj{i}", [P, TC]) for i in range(4)]
        p_x = m.ps("s1_p_x", [P, TC])
        p_dt = [m.ps(f"s1_p_dt{i}", [P, TC]) for i in range(2)]

        loaded, rest_loaded, zeroed = S("loaded"), S("rest_loaded"), S("history_zeroed")
        xp_shifted = S("xp_shifted")
        proj_ready, xp_ready, conv_step, conv_ready = S("proj_ready"), S("xp_ready"), S("conv_step"), S("conv_ready")
        z_ready, u_ready, xdbl_ready = S("z_ready"), S("u_ready"), S("xdbl_ready")
        hi_ready, rest_ready, mid_ready, low_ready = S("hi_ready"), S("rest_ready"), S("mid_ready"), S("low_ready")
        dlt_ready, dt_ready, abs_ready, relu_ready = S("dlt_ready"), S("dt_ready"), S("abs_ready"), S("relu_ready")
        ex_ready, ex1_ready, lost_ready, ln_ready = S("ex_ready"), S("ex1_ready"), S("lost_ready"), S("ln_ready")
        log1p_ready, delta_ready = S("log1p_ready"), S("delta_ready")
        z_out = [S(f"z_out{d}") for d in range(ND)]
        u_out = [S(f"u_out{d}") for d in range(ND)]
        delta_out = [S(f"delta_out{d}") for d in range(ND)]
        LOADS = 5
        Z0, U0, CONV0, RELU0 = ND, ND, ND, 2

        with nc.Block() as block:
            @block.sync
            def _(sp):
                prime(sp, [dlt_ready, rest_ready, xdbl_ready, dt_ready, low_ready, delta_ready, *z_out, *u_out, *delta_out])
                x_from = D["xT"].rearrange("(k p) n -> p k n", p=P)
                sp.dma_start(w_in[:], D["w_in"].rearrange("(k p) n -> p k n", p=P)).then_inc(loaded, 16)
                sp.dma_start(xT[:, :, 0:TC], x_from[:, :, 0:TC]).then_inc(loaded, 16)
                sp.dma_start(vecs[:], D["mixer_vecs"].rearrange("(k p) n -> p k n", p=P)).then_inc(loaded, 16)
                sp.dma_start(w_x[:], D["w_x"].rearrange("(k p) n -> p k n", p=P)).then_inc(loaded, 16)
                sp.dma_start(w_dt[:], D["w_dt"]).then_inc(loaded, 16)
                sp.dma_start(xT[:, :, TC:L], x_from[:, :, TC:L]).then_inc(rest_loaded, 16)
                with sp.Fori(0, NC) as c:
                    for d in range(ND):
                        sp.wait_ge(z_ready, c * ND + (Z0 + d + 1))
                        sp.dma_start(D["sz"][d * P:(d + 1) * P, bass.ds(c * TC, TC)], sz[:, d, :]).then_inc(z_out[d], 16)
                        sp.wait_ge(u_ready, c * ND + (U0 + d + 1))
                        sp.dma_start(D["u"][d * P:(d + 1) * P, bass.ds(c * TC, TC)], u[:, d, :]).then_inc(u_out[d], 16)
                    for d in range(ND):
                        sp.wait_ge(delta_ready, PRIMED + c * ND + (d + 1))
                        sp.dma_start(D["delta"][d * P:(d + 1) * P, bass.ds(c * TC, TC)],
                                     delta[:, d, :]).then_inc(delta_out[d], 16)
                for d in range(ND):
                    sp.wait_ge(z_out[d], PRIMED + 16 * NC)
                    sp.wait_ge(u_out[d], PRIMED + 16 * NC)
                    sp.wait_ge(delta_out[d], PRIMED + 16 * NC)

            @block.tensor
            def _(pe):
                pe.wait_ge(loaded, 16 * LOADS)
                with pe.Fori(0, NC) as c:
                    for n in range(2 * ND):
                        if n < ND:
                            pe.wait_ge(z_ready, c * ND + (n + 1))
                        else:
                            pe.wait_ge(xp_ready, c * ND + (n - ND + 1))
                        for k in range(KD):
                            mm = nc.tensor.matmul(p_proj[n % ND][:], w_in[:, k, n * P:(n + 1) * P],
                                                  xT[:, k, bass.ds(c * TC, TC)], start=k == 0, stop=k == KD - 1)
                        mm.then_inc(proj_ready, 1)
                    pe.wait_ge(rest_loaded, 16)
                    pe.wait_ge(dlt_ready, PRIMED + c)
                    pe.wait_ge(rest_ready, PRIMED + c)
                    for k in range(ND):
                        pe.wait_ge(u_ready, c * ND + (U0 + k + 1))
                        mm = nc.tensor.matmul(p_x[0:RK + 2 * NS, :], w_x[:, k, :], u[:, k, :],
                                              start=k == 0, stop=k == ND - 1)
                    mm.then_inc(xdbl_ready, 1)
                    pe.wait_ge(dlt_ready, PRIMED + c + 1)
                    for d in range(ND):
                        pe.wait_ge(relu_ready, c * ND + (d + 1))
                        nc.tensor.matmul(p_dt[d % 2][:], w_dt[:, d * P:(d + 1) * P], dlt[:],
                                         start=True, stop=True).then_inc(dt_ready, 1)

            @block.scalar
            def _(act):
                act.sem_inc(z_ready, Z0)
                act.sem_inc(u_ready, U0)
                act.sem_inc(relu_ready, RELU0)
                act.wait_ge(loaded, 16 * LOADS)
                act.wait_ge(zeroed, 1)
                with act.Fori(0, NC) as c:
                    for d in range(ND):
                        act.wait_ge(conv_ready, c * ND + (d + 1))
                        nc.scalar.copy(xp[:, d, 0:KC - 1], xp[:, d, TC:TC + KC - 1]).then_inc(xp_shifted, 1)
                        act.wait_ge(proj_ready, c * (2 * ND) + (d + 1))
                        act.wait_ge(xp_shifted, c * ND + (d + 1))
                        nc.scalar.copy(xp[:, d, KC - 1:], p_proj[d][:]).then_inc(xp_ready, 1)
                    act.wait_ge(xdbl_ready, PRIMED + c)
                    for d in range(ND):
                        act.wait_ge(proj_ready, c * (2 * ND) + (ND + d + 1))
                        act.wait_ge(z_out[d], PRIMED + c * 16)
                        nc.scalar.activation(sz[:, d, :], p_proj[d][:], ACT.Silu).then_inc(z_ready, 1)
                        act.wait_ge(conv_ready, c * ND + (CONV0 + d + 1))
                        act.wait_ge(u_out[d], PRIMED + c * 16)
                        nc.scalar.activation(u[:, d, :], conv[:, d, :], ACT.Silu,
                                             bias=vecs[:, d, KC:KC + 1]).then_inc(u_ready, 1)
                    act.wait_ge(xdbl_ready, PRIMED + c + 1)
                    act.wait_ge(dt_ready, PRIMED + c * ND)
                    nc.scalar.copy(bc_parts[0:2 * NS, bass.ds(c * TC, TC)], p_x[0:2 * NS, :]).then_inc(hi_ready, 1)
                    nc.scalar.copy(dlt[:], p_x[2 * NS:2 * NS + RK, :]).then_inc(dlt_ready, 1)
                    act.wait_ge(rest_ready, PRIMED + c + 1)
                    act.wait_ge(low_ready, PRIMED + c)
                    nc.scalar.copy(bc_mid[:], bc_rest[:]).then_inc(mid_ready, 1)
                    act.wait_ge(mid_ready, c + 1)
                    nc.scalar.copy(bc_parts[2 * NS:4 * NS, bass.ds(c * TC, TC)], bc_mid[:])
                    act.wait_ge(delta_ready, PRIMED + c * ND)
                    for d in range(ND):
                        act.wait_ge(dt_ready, PRIMED + c * ND + (d + 1))
                        nc.scalar.activation(absv[:, d, :], p_dt[d % 2][:], ACT.Abs,
                                             bias=vecs[:, d, KC + 1:KC + 2]).then_inc(abs_ready, 1)
                        nc.scalar.activation(relu[:, d, :], p_dt[d % 2][:], ACT.Relu,
                                             bias=vecs[:, d, KC + 1:KC + 2]).then_inc(relu_ready, 1)
                        act.wait_ge(abs_ready, c * ND + (d + 1))
                        nc.scalar.activation(ex[:, d, :], absv[:, d, :], ACT.Exp, scale=-1.0).then_inc(ex_ready, 1)
                    for d in range(ND):
                        act.wait_ge(ex1_ready, c * ND + (d + 1))
                        nc.scalar.activation(lnv[:, d, :], ex1[:, d, :], ACT.Ln).then_inc(ln_ready, 1)

            @block.vector
            def _(dve):
                dve.sem_inc(conv_ready, CONV0)
                nc.vector.memset(xp[:], 0.0).then_inc(zeroed, 1)
                dve.wait_ge(loaded, 16 * LOADS)
                with dve.Fori(0, NC) as c:
                    for d in range(ND):
                        dve.wait_ge(xp_ready, c * ND + (d + 1))
                        dve.wait_ge(u_ready, c * ND + (d + 1))
                        nc.vector.tensor_scalar(conv[:, d, :], xp[:, d, 0:TC], vecs[:, d, 0:1], None,
                                                ALU.mult).then_inc(conv_step, 1)
                        for k in range(1, KC):
                            dve.wait_ge(conv_step, (c * ND + d) * (KC - 1) + k)
                            nc.vector.scalar_tensor_tensor(
                                out=conv[:, d, :], in0=xp[:, d, k:k + TC], scalar=vecs[:, d, k:k + 1],
                                in1=conv[:, d, :], op0=ALU.mult, op1=ALU.add,
                            ).then_inc(conv_step if k < KC - 1 else conv_ready, 1)
                    dve.wait_ge(hi_ready, c + 1)
                    nc.vector.tensor_tensor(bc_rest[:], p_x[0:2 * NS, :], bc_parts[0:2 * NS, bass.ds(c * TC, TC)],
                                            ALU.subtract).then_inc(rest_ready, 1)
                    dve.wait_ge(mid_ready, c + 1)
                    nc.vector.tensor_tensor(bc_parts[4 * NS:6 * NS, bass.ds(c * TC, TC)], bc_rest[:], bc_mid[:],
                                            ALU.subtract).then_inc(low_ready, 1)
                    for d in range(ND):
                        dve.wait_ge(ex_ready, c * ND + (d + 1))
                        nc.vector.tensor_scalar(ex1[:, d, :], ex[:, d, :], 1.0, None, ALU.add).then_inc(ex1_ready, 1)
                        dve.wait_ge(ex1_ready, c * ND + (d + 1))
                        nc.vector.scalar_tensor_tensor(out=lost[:, d, :], in0=ex1[:, d, :], scalar=-1.0,
                                                       in1=ex[:, d, :], op0=ALU.add,
                                                       op1=ALU.subtract).then_inc(lost_ready, 1)
                    for d in range(ND):
                        dve.wait_ge(ln_ready, c * ND + (d + 1))
                        dve.wait_ge(lost_ready, c * ND + (d + 1))
                        nc.vector.tensor_tensor(lost[:, d, :], lnv[:, d, :], lost[:, d, :],
                                                ALU.subtract).then_inc(log1p_ready, 1)
                        dve.wait_ge(log1p_ready, c * ND + (d + 1))
                        dve.wait_ge(delta_out[d], PRIMED + c * 16)
                        nc.vector.tensor_tensor(delta[:, d, :], lost[:, d, :], relu[:, d, :],
                                                ALU.add).then_inc(delta_ready, 1)


def set_identity(pool, tile, cleared, done):
    n = tile.shape[0]
    nc_pool = pool
    nc_pool.memset(tile[:], 0.0).then_inc(cleared, 1)
    pool.wait_ge(cleared, 1)
    nc_pool.affine_select(out=tile[:], in_=tile[:], compare_op=ALU.not_equal, fill=1.0, base=0,
                          pattern=[[-1, n]], channel_multiplier=1).then_inc(done, 1)


def mixer_scan(nc, S, D, keep):
    bc_parts = keep["bc_parts"]
    GN = 4
    NG = NS // GN
    Q = ND * NG
    RH, RA, RP = 4, 2, 4
    with Mem(nc) as m:
        rep = m.sb("s2_rep", [P, 2, NS, TC])
        dA = [m.sb(f"s2_dA{i}", [P, GN, TC]) for i in range(RA)]
        h = [m.sb(f"s2_h{i}", [P, GN, TC]) for i in range(RH)]
        hC = [m.sb(f"s2_hC{i}", [P, GN, TC]) for i in range(RA)]
        delta = m.sb("s2_delta", [P, ND, TC])
        u = m.sb("s2_u", [P, ND, TC])
        sz = m.sb("s2_sz", [P, ND, TC])
        du = m.sb("s2_du", [P, ND, TC])
        yz = m.sb("s2_yz", [P, ND, TC])
        state = m.sb("s2_state", [P, ND, NS])
        scanv = m.sb("s2_scanv", [P, ND, NS + 1])
        A = m.sb("s2_A", [P, ND, NS])
        sel = m.sb("s2_sel", [3 * 2 * NS, 2 * NS, P], BF16)
        ident = m.sb("s2_ident", [P, P])
        diag = m.sb("s2_diag", [P, ND, P])
        p_rep = [m.ps(f"s2_p_rep{i}", [P, TC]) for i in range(RP)]
        p_y = [m.ps(f"s2_p_y{i}", [P, TC]) for i in range(2)]

        cleared, ident_ready, sel_cleared, sel_step = S("cleared"), S("ident_ready"), S("sel_cleared"), S("sel_step")
        vec_in, exp_a, a_ready, state_ready = S("vec_in"), S("exp_a"), S("a_ready"), S("state_ready")
        chunk_in = [S(f"chunk_in{d}") for d in range(ND)]
        rep_mm, rep_ready = S("rep_mm"), S("rep_ready")
        da_ready, du_ready, dbu_ready, scan_ready = S("da_ready"), S("du_ready"), S("dbu_ready"), S("scan_ready")
        hc_ready, sum_done, diag_ready, yz_ready = S("hc_ready"), S("sum_done"), S("diag_ready"), S("yz_ready")
        yz_out = [S(f"yz_out{d}") for d in range(ND)]
        STATE0, SCAN0, REP0, SUM0, YZ0 = Q, RA, RP, RA, 2

        with nc.Block() as block:
            @block.sync
            def _(sp):
                prime(sp, yz_out)
                def load(c, d):
                    at = (slice(d * P, (d + 1) * P), bass.ds(c * TC, TC))
                    sp.dma_start(delta[:, d, :], D["delta"][at]).then_inc(chunk_in[d], 16)
                    sp.dma_start(u[:, d, :], D["u"][at]).then_inc(chunk_in[d], 16)
                    sp.dma_start(sz[:, d, :], D["sz"][at]).then_inc(chunk_in[d], 16)

                def store(c, d):
                    sp.dma_start(D["yz"][d * P:(d + 1) * P, bass.ds(c * TC, TC)], yz[:, d, :]).then_inc(yz_out[d], 16)

                sp.dma_start(scanv[:], D["scan_vecs"].rearrange("(k p) n -> p k n", p=P)).then_inc(vec_in, 16)
                for d in range(ND):
                    load(0, d)
                with sp.Fori(1, NC) as c:
                    for d in range(ND):
                        sp.wait_ge(yz_ready, c * ND + (YZ0 - ND + d + 1))
                        store(c - 1, d)
                        load(c, d)
                for d in range(ND):
                    sp.wait_ge(yz_ready, (NC - 1) * ND + YZ0 + d + 1)
                    store(NC - 1, d)
                for d in range(ND):
                    sp.wait_ge(yz_out[d], PRIMED + 16 * NC)

            @block.gpsimd
            def _(pool):
                set_identity(pool, ident, cleared, ident_ready)
                pool.memset(sel[:], 0.0).then_inc(sel_cleared, 1)
                pool.wait_ge(sel_cleared, 1)
                for part in range(3):
                    pool.wait_ge(sel_step, part)
                    pool.affine_select(out=sel[:], in_=sel[:], compare_op=ALU.not_equal, fill=1.0,
                                       base=-2 * NS * part, pattern=[[-1, 2 * NS], [0, P]],
                                       channel_multiplier=1).then_inc(sel_step, 1)
                def delta_u(c, d):
                    pool.wait_ge(chunk_in[d], c * 48 + 48)
                    pool.tensor_tensor(du[:, d, :], delta[:, d, :], u[:, d, :], ALU.mult).then_inc(du_ready, 1)

                def chunk(c, last):
                    for q in range(Q):
                        d, g = divmod(q, NG)
                        pool.wait_ge(scan_ready, c * Q + (SCAN0 + q + 1))
                        pool.wait_ge(sum_done, c * Q + (q + 1))
                        pool.tensor_tensor(hC[q % RA][:], h[q % RH][:], rep[:, 1, g * GN:(g + 1) * GN, :],
                                           ALU.mult).then_inc(hc_ready, 1)
                        pool.tensor_copy(state[:, d, g * GN:(g + 1) * GN],
                                         h[q % RH][:, :, TC - 1]).then_inc(state_ready, 1)
                        if g == 1 and d < ND - 1:
                            delta_u(c, d + 1)
                        elif g == 1 and not last:
                            delta_u(c + 1, 0)

                delta_u(0, 0)
                with pool.Fori(0, NC - 1) as c:
                    chunk(c, False)
                chunk(NC - 1, True)

            @block.scalar
            def _(act):
                act.sem_inc(rep_ready, REP0)
                act.wait_ge(vec_in, 16)
                nc.scalar.activation(A[:], scanv[:, :, 0:NS], ACT.Exp).then_inc(exp_a, 1)
                act.wait_ge(exp_a, 1)
                nc.scalar.mul(A[:], A[:], -1.0).then_inc(a_ready, 1)
                act.wait_ge(a_ready, 1)
                with act.Fori(0, NC) as c:
                    for q in range(Q):
                        d, g = divmod(q, NG)
                        if q < NG:
                            act.wait_ge(state_ready, c * Q + (STATE0 - NG + q + 1))
                            for j in range(2 * GN):
                                k = q * 2 * GN + j
                                act.wait_ge(rep_mm, c * (2 * NS) + (k + 1))
                                nc.scalar.copy(rep[:, j // GN, g * GN + j % GN, :], p_rep[k % RP][:]).then_inc(rep_ready, 1)
                        if g == 0:
                            act.wait_ge(chunk_in[d], c * 48 + 48)
                        act.wait_ge(scan_ready, c * Q + (q + 1))
                        for n in range(GN):
                            ex = nc.scalar.activation(dA[q % RA][:, n, :], delta[:, d, :], ACT.Exp,
                                                      scale=A[:, d, g * GN + n:g * GN + n + 1])
                        ex.then_inc(da_ready, 1)

            @block.vector
            def _(dve):
                def chunk(c, first):
                    for q in range(Q):
                        d, g = divmod(q, NG)
                        hb = h[q % RH]
                        if g == 0:
                            dve.wait_ge(du_ready, c * ND + (d + 1))
                        if d == 0:
                            dve.wait_ge(rep_ready, c * (2 * NS) + (REP0 + (g + 1) * 2 * GN))
                        dve.wait_ge(state_ready, c * Q + (STATE0 - RH + q + 1))
                        nc.vector.tensor_tensor(hb[:], du[:, d:d + 1, :].to_broadcast([P, GN, TC]),
                                                rep[:, 0, g * GN:(g + 1) * GN, :], ALU.mult).then_inc(dbu_ready, 1)
                        dve.wait_ge(dbu_ready, c * Q + (q + 1))
                        dve.wait_ge(da_ready, c * Q + (q + 1))
                        for n in range(GN):
                            at = g * GN + n
                            sc = nc.vector.tensor_tensor_scan(hb[:, n, :], dA[q % RA][:, n, :], hb[:, n, :],
                                                              state[:, d, at:at + 1], ALU.mult, ALU.add)
                        sc.then_inc(scan_ready, 1)
                        if q % NG == 2 and not (first and d == 0):
                            epilogue(c, d - 1) if d else epilogue(c - 1, ND - 1)

                def epilogue(c, d):
                    dve.wait_ge(sum_done, c * Q + (SUM0 + (d + 1) * NG))
                    dve.wait_ge(chunk_in[d], c * 48 + 48)
                    dve.wait_ge(yz_out[d], PRIMED + c * 16)
                    nc.vector.tensor_tensor(yz[:, d, :], p_y[d % 2][:], sz[:, d, :], ALU.mult).then_inc(yz_ready, 1)

                dve.sem_inc(scan_ready, SCAN0)
                dve.sem_inc(yz_ready, YZ0)
                nc.vector.memset(state[:], 0.0).then_inc(state_ready, STATE0)
                dve.wait_ge(vec_in, 16)
                dve.wait_ge(ident_ready, 1)
                for d in range(ND):
                    nc.vector.tensor_scalar(diag[:, d, :], ident[:], scanv[:, d, NS:NS + 1], None,
                                            ALU.mult).then_inc(diag_ready, 1)
                chunk(0, True)
                with dve.Fori(1, NC) as c:
                    chunk(c, False)
                epilogue(NC - 1, ND - 1)

            @block.tensor
            def _(pe):
                def spread(c, g):
                    for j in range(2 * GN):
                        k = g * 2 * GN + j
                        row = (j // GN) * NS + g * GN + j % GN
                        pe.wait_ge(rep_ready, c * (2 * NS) + (k + 1))
                        nc.tensor.matmul(p_rep[k % RP][:], sel[:, row, :], bc_parts[:, bass.ds(c * TC, TC)],
                                         start=True, stop=True).then_inc(rep_mm, 1)

                def add_states(c, q):
                    d, g = divmod(q, NG)
                    if g == 0:
                        pe.wait_ge(yz_ready, c * ND + (d + 1))
                        pe.wait_ge(chunk_in[d], c * 48 + 48)
                        nc.tensor.matmul(p_y[d % 2][:], diag[:, d, :], u[:, d, :], start=True, stop=False)
                    pe.wait_ge(hc_ready, c * Q + (q + 1))
                    for n in range(GN):
                        mm = nc.tensor.matmul(p_y[d % 2][:], ident[:], hC[q % RA][:, n, :],
                                              start=False, stop=g == NG - 1 and n == GN - 1)
                    mm.then_inc(sum_done, 1)

                def chunk(c, first):
                    for g in range(NG):
                        spread(c, g)
                        if not first:
                            add_states(c - 1, Q - NG + g)
                    for q in range(Q - NG):
                        add_states(c, q)

                pe.sem_inc(sum_done, SUM0)
                pe.wait_ge(ident_ready, 1)
                pe.wait_ge(sel_step, 3)
                pe.wait_ge(diag_ready, ND)
                chunk(0, True)
                with pe.Fori(1, NC) as c:
                    chunk(c, False)
                for q in range(Q - NG, Q):
                    add_states(NC - 1, q)


FREE = 2


class NormRing:

    N0 = FREE * JT

    def __init__(self, m, S, tag, of=None):
        self.s = of.y if of else [m.sb(f"{tag}_sum{i}", [P, JT, DM]) for i in range(2)]
        self.y = [m.sb(f"{tag}_norm{i}", [P, JT, DM]) for i in range(2)]
        self.bst = m.sb(f"{tag}_bst", [P, 2, JT, 6])
        self.mv = m.sb(f"{tag}_mv", [P, 2, JT, 2])
        self.std = m.sb(f"{tag}_std", [P, 2, JT])
        self.rs = m.sb(f"{tag}_rs", [P, 2, JT])
        self.eps = m.sb(f"{tag}_eps", [P, 1])
        self.gate = S(f"{tag}_gate")
        self.sum_ready = of.norm_ready if of else S(f"{tag}_sum_ready")
        self.sum0 = self.N0 if of else PRIMED
        self.eps_ready, self.stat_ready, self.mv_ready = (
            S(f"{tag}_eps_ready"), S(f"{tag}_stat_ready"), S(f"{tag}_mv_ready"))
        self.std_ready, self.rs_ready, self.norm_ready = (
            S(f"{tag}_std_ready"), S(f"{tag}_rs_ready"), S(f"{tag}_norm_ready"))

    def vector_setup(self, dve):
        dve.memset(self.eps[:], EPS).then_inc(self.eps_ready, 1)
        dve.sem_inc(self.norm_ready, self.N0)
        if self.sum0 == PRIMED:
            dve.sem_inc(self.sum_ready, PRIMED)

    def wait_free(self, eng, c, n):
        eng.wait_ge(self.norm_ready, c * JT + (n + 1) * JT)

    def wait_normed(self, eng, c, n):
        eng.wait_ge(self.norm_ready, c * JT + (self.N0 + (n + 1) * JT))

    def vector_stats(self, dve, c, n):
        for j in range(JT):
            dve.wait_ge(self.sum_ready, c * JT + (self.sum0 + n * JT + j + 1))
            dve.bn_stats(self.bst[:, n % 2, j, :], self.s[n % 2][:, j, :]).then_inc(self.stat_ready, 1)
        for j in range(JT):
            dve.wait_ge(self.stat_ready, c * JT + (n * JT + j + 1))
            dve.sem_inc(self.gate, 1)
            dve.bn_aggr(self.mv[:, n % 2, j, :], self.bst[:, n % 2, j, :]).then_inc(self.mv_ready, 1)

    def scalar_std(self, act, c, n):
        act.wait_ge(self.mv_ready, c * JT + (n + 1) * JT)
        act.activation(self.std[:, n % 2, :], self.mv[:, n % 2, :, 1], ACT.Sqrt,
                       bias=self.eps[:, 0:1]).then_inc(self.std_ready, 1)

    def vector_norm(self, dve, c, n):
        dve.wait_ge(self.std_ready, c + (n + 1))
        dve.reciprocal(self.rs[:, n % 2, :], self.std[:, n % 2, :]).then_inc(self.rs_ready, 1)
        dve.wait_ge(self.rs_ready, c + (n + 1))
        for j in range(JT):
            dve.tensor_scalar(self.y[n % 2][:, j, :], self.s[n % 2][:, j, :], self.mv[:, n % 2, j, 0:1],
                              self.rs[:, n % 2, j:j + 1], ALU.subtract, ALU.mult).then_inc(self.norm_ready, 1)


def mixer_out(nc, S, D, keep):
    xn, xt = keep["xn"], keep["xt"]
    with Mem(nc) as m:
        w_out = m.sb("s3_w_out", [P, ND, DM])
        yz = [m.sb(f"s3_yz{i}", [P, ND, TC]) for i in range(2)]
        xin = [m.sb(f"s3_xin{i}", [P, JT, DM]) for i in range(2)]
        ident = m.sb("s3_ident", [P, P])
        p_o = [m.ps(f"s3_p_o{i}", [P, TC]) for i in range(4)]
        p_t = [m.ps(f"s3_p_t{i}", [P, TC]) for i in range(2)]
        R = NormRing(m, S, "s3")
        cleared, ident_ready, w_loaded = S("cleared"), S("ident_ready"), S("w_loaded")
        chunk_in = [S(f"chunk_in{i}") for i in range(2)]
        out_ready, turned, turn_taken, kept = S("out_ready"), S("turned"), S("turn_taken"), S("kept")

        with nc.Block() as block:
            @block.sync
            def _(sp):
                def load(c, n):
                    sp.dma_start(yz[n % 2][:], D["yz"].rearrange("(k p) n -> p k n", p=P)[
                        :, :, bass.ds((c + n) * TC, TC)]).then_inc(chunk_in[n % 2], 16)
                    sp.dma_start(xin[n % 2][:], D["x"][bass.ds((c + n) * TC, TC), :].rearrange(
                        "(j p) n -> p j n", p=P)).then_inc(chunk_in[n % 2], 16)

                sp.dma_start(w_out[:], D["w_out"].rearrange("(k p) n -> p k n", p=P)).then_inc(w_loaded, 16)
                load(0, 0)
                load(0, 1)
                with sp.Fori(0, NC - 3, 2) as c:
                    for n in (2, 3):
                        sp.wait_ge(R.sum_ready, c * JT + (PRIMED + (n - 1) * JT))
                        load(c, n)

            @block.gpsimd
            def _(pool):
                set_identity(pool, ident, cleared, ident_ready)
                pool.sem_inc(kept, FREE)
                with pool.Fori(0, NC - 1, 2) as c:
                    for n in range(2):
                        R.wait_normed(pool, c, n)
                        pool.tensor_copy(xn[:, bass.ds((c + n) * JT, JT), :], R.y[n][:]).then_inc(kept, 1)

            @block.tensor
            def _(pe):
                def project(c, n):
                    pe.wait_ge(chunk_in[n % 2], c * 16 + (n // 2 + 1) * 32)
                    for j in range(JT):
                        if n:
                            pe.wait_ge(R.sum_ready, c * JT + (PRIMED + (n - 1) * JT + j + 1))
                        for d in range(ND):
                            mm = nc.tensor.matmul(p_o[j][:, 0:DM], yz[n % 2][:, d, j * P:(j + 1) * P],
                                                  w_out[:, d, :], start=d == 0, stop=d == ND - 1)
                        mm.then_inc(out_ready, 1)

                def turn(c, n):
                    turn_tiles(pe, c, n, R, p_t, ident, turned, turn_taken)

                pe.wait_ge(w_loaded, 16)
                pe.wait_ge(ident_ready, 1)
                project(0, 0)
                project(0, 1)
                with pe.Fori(0, NC - 3, 2) as c:
                    for n in range(2):
                        project(c, n + 2)
                        turn(c, n)
                turn(NC - 2, 0)
                turn(NC - 2, 1)

            @block.scalar
            def _(act):
                def take(c, n):
                    take_turned(act, c, n, xt, p_t, turned, turn_taken)

                act.sem_inc(turn_taken, 2)
                act.wait_ge(R.eps_ready, 1)
                R.scalar_std(act, 0, 0)
                with act.Fori(0, NC - 3, 2) as c:
                    R.scalar_std(act, c, 1)
                    take(c, 0)
                    R.scalar_std(act, c, 2)
                    take(c, 1)
                R.scalar_std(act, NC - 2, 1)
                take(NC - 2, 0)
                take(NC - 2, 1)

            @block.vector
            def _(dve):
                def add(c, n):
                    if n:
                        R.wait_free(dve, c, n)
                    dve.wait_ge(chunk_in[n % 2], c * 16 + (n // 2 + 1) * 32)
                    for j in range(JT):
                        dve.wait_ge(out_ready, c * JT + (n * JT + j + 1))
                        nc.vector.tensor_tensor(R.s[n % 2][:, j, :], p_o[j][:, 0:DM], xin[n % 2][:, j, :],
                                                ALU.add).then_inc(R.sum_ready, 1)
                    R.vector_stats(dve, c, n)

                def norm(c, n):
                    dve.wait_ge(kept, c + (n + 1))
                    R.vector_norm(dve, c, n)

                R.vector_setup(dve)
                add(0, 0)
                with dve.Fori(0, NC - 3, 2) as c:
                    add(c, 1)
                    norm(c, 0)
                    add(c, 2)
                    norm(c, 1)
                add(NC - 2, 1)
                norm(NC - 2, 0)
                dve.wait_ge(turned, (NC - 2) * JT)
                norm(NC - 2, 1)


def turn_tiles(pe, c, n, R, p_t, ident, turned, turn_taken):
    for j in range(JT):
        pe.wait_ge(R.norm_ready, c * JT + (R.N0 + n * JT + j + 1))
        pe.wait_ge(turn_taken, c * JT + (n * JT + j + 1))
        for half in range(KD):
            tr = pe.transpose(p_t[j % 2][:, half * P:(half + 1) * P], R.y[n % 2][:, j, half * P:(half + 1) * P],
                              ident[:])
        tr.then_inc(turned, 1)


def take_turned(act, c, n, xt, p_t, turned, turn_taken):
    for j in range(JT):
        act.wait_ge(turned, c * JT + (n * JT + j + 1))
        act.copy(xt[:, :, bass.ds((c * JT + (n * JT + j)) * P, P)],
                 p_t[j % 2][:, 0:DM].rearrange("p (h t) -> p h t", h=KD)).then_inc(turn_taken, 1)


R1 = 64
E0 = 8


def adapter(nc, S, D, keep):
    xn, xt = keep["xn"], keep["xt"]
    with Mem(nc) as m:
        base = m.sb("s4_base", [P, KD, DM])
        disc = m.sb("s4_disc", [P, KD, 2 * E0])
        bias = m.sb("s4_bias", [R1 + 1, 2, DM])
        down = m.sb("s4_down", [P, KD, R1])
        down_b = m.sb("s4_down_b", [R1, 1])
        up = m.sb("s4_up", [P, KD, R1 + 1])
        outm = m.sb("s4_outm", [P, KD, DM])
        fused = m.sb("s4_fused", [R1 + 1, DM])
        bst = m.sb("s4_bstT", [P, KD, NC, 6])
        mv = m.sb("s4_mvT", [P, KD, 2])
        vec = m.sb("s4_vec", [P, KD, 4])
        iv = m.sb("s4_iv", [P, KD, E0])
        t = m.sb("s4_t", [P, KD, E0])
        ones = m.sb("s4_ones", [P, 1])
        loss = m.sb("s4_loss", [1, 3, E0])
        choice = m.sb("s4_choice", [1, E0], U32)
        xs = [m.sb(f"s4_xs{i}", [P, KD, TC]) for i in range(2)]
        hid = [m.sb(f"s4_hid{i}", [R1 + 1, TC]) for i in range(2)]
        ident = m.sb("s4_ident", [P, P])
        p_m = m.ps("s4_p_m", [P, TC])
        p_h = m.ps("s4_p_h", [P, TC])
        p_o = [m.ps(f"s4_p_o{i}", [P, TC]) for i in range(4)]
        p_t = [m.ps(f"s4_p_t{i}", [P, TC]) for i in range(2)]
        R = NormRing(m, S, "s4")
        cleared, ident_ready, w_loaded, e_loaded = S("cleared"), S("ident_ready"), S("w_loaded"), S("e_loaded")
        ones_ready, step, loss_mm, chosen = S("ones_ready"), S("step"), S("loss_mm"), S("chosen")
        fuse_mm, fused_ready, x_taken, hid_mm, hid_ready = (
            S("fuse_mm"), S("fused_ready"), S("x_taken"), S("hid_mm"), S("hid_ready"))
        out_ready, turned, turn_taken, kept = S("out_ready"), S("turned"), S("turn_taken"), S("kept")

        with nc.Block() as block:
            @block.sync
            def _(sp):
                sp.dma_start(disc[:], D["disc"].rearrange("(k p) n -> p k n", p=P)).then_inc(w_loaded, 16)
                sp.dma_start(base[:], D["base"].rearrange("(k p) n -> p k n", p=P)).then_inc(w_loaded, 16)
                sp.dma_start(bias[R1:R1 + 1, 0, :], D["base_b"]).then_inc(w_loaded, 16)
                sp.wait_ge(chosen, 1)
                e = sp.value_load(choice[0:1, 0:1], min_val=0, max_val=E0 - 1)
                sp.dma_start(down[:], D["down"].rearrange("e (k p) n -> p (e k) n", p=P)[
                    :, bass.ds(e * KD, KD), :]).then_inc(e_loaded, 16)
                sp.dma_start(up[:], D["up"].rearrange("e (k p) n -> p (e k) n", p=P)[
                    :, bass.ds(e * KD, KD), :]).then_inc(e_loaded, 16)
                sp.dma_start(outm[:], D["outm"].rearrange("e (k p) n -> p (e k) n", p=P)[
                    :, bass.ds(e * KD, KD), :]).then_inc(e_loaded, 16)
                sp.dma_start(down_b[:], D["down_b"][bass.ds(e * R1, R1), :]).then_inc(e_loaded, 16)
                sp.dma_start(bias[R1:R1 + 1, 1, :], D["outm_b"][bass.ds(e, 1), :]).then_inc(e_loaded, 16)

            @block.gpsimd
            def _(pool):
                set_identity(pool, ident, cleared, ident_ready)
                pool.sem_inc(kept, FREE)

                def take_x(c, n):
                    pool.tensor_copy(xs[n % 2][:], xt[:, :, bass.ds((c + n) * TC, TC)]).then_inc(x_taken, 1)

                def keep_norm(c, n):
                    R.wait_normed(pool, c, n)
                    pool.tensor_copy(xn[:, bass.ds((c + n) * JT, JT), :], R.y[n][:]).then_inc(kept, 1)

                take_x(0, 0)
                take_x(0, 1)
                with pool.Fori(0, NC - 3, 2) as c:
                    for n in range(2):
                        pool.wait_ge(out_ready, c * JT + (n + 1) * JT)
                        take_x(c, n + 2)
                        keep_norm(c, n)
                keep_norm(NC - 2, 0)
                keep_norm(NC - 2, 1)

            @block.tensor
            def _(pe):
                pe.wait_ge(ones_ready, 1)
                pe.wait_ge(step, 7)
                for k in range(KD):
                    mm = nc.tensor.matmul(p_m[0:1, 0:E0], ones[:], t[:, k, :], start=k == 0, stop=k == KD - 1)
                mm.then_inc(loss_mm, 1)
                pe.wait_ge(e_loaded, 16 * 5)
                pe.wait_ge(step, 8)
                for k in range(KD):
                    mm = nc.tensor.matmul(p_m[0:R1 + 1, 0:DM], up[:, k, :], outm[:, k, :],
                                          start=k == 0, stop=k == KD - 1)
                mm.then_inc(fuse_mm, 1)
                pe.wait_ge(w_loaded, 48)
                pe.wait_ge(ident_ready, 1)
                pe.wait_ge(fused_ready, 2)

                def hidden(c, n):
                    pe.wait_ge(x_taken, c + (n + 1))
                    pe.wait_ge(hid_ready, c + (n + 1))
                    for k in range(KD):
                        mm = nc.tensor.matmul(p_h[0:R1, :], down[:, k, :], xs[n % 2][:, k, :],
                                              start=k == 0, stop=k == KD - 1)
                    mm.then_inc(hid_mm, 1)

                def project(c, n):
                    pe.wait_ge(hid_ready, c + (n + 2))
                    for j in range(JT):
                        if n:
                            pe.wait_ge(R.sum_ready, c * JT + (PRIMED + (n - 1) * JT + j + 1))
                        for k in range(KD):
                            nc.tensor.matmul(p_o[j][:, 0:DM], xs[n % 2][:, k, j * P:(j + 1) * P], base[:, k, :],
                                             start=k == 0, stop=False)
                        nc.tensor.matmul(p_o[j][:, 0:DM], hid[n % 2][:, j * P:(j + 1) * P], fused[:],
                                         start=False, stop=True).then_inc(out_ready, 1)

                def turn(c, n):
                    turn_tiles(pe, c, n, R, p_t, ident, turned, turn_taken)

                hidden(0, 0)
                hidden(0, 1)
                project(0, 0)
                project(0, 1)
                with pe.Fori(0, NC - 3, 2) as c:
                    for n in range(2):
                        hidden(c, n + 2)
                        turn(c, n)
                        project(c, n + 2)
                turn(NC - 2, 0)
                turn(NC - 2, 1)

            @block.scalar
            def _(act):
                def hide(c, n):
                    act.wait_ge(hid_mm, c + (n + 1))
                    if n > 1:
                        act.wait_ge(out_ready, c * JT + (n - 1) * JT)
                    nc.scalar.activation(hid[n % 2][0:R1, :], p_h[0:R1, :], ACT.Relu,
                                         bias=down_b[:, 0:1]).then_inc(hid_ready, 1)

                def take(c, n):
                    act.wait_ge(x_taken, c + (n + 1))
                    take_turned(act, c, n, xt, p_t, turned, turn_taken)

                act.sem_inc(turn_taken, 2)
                act.wait_ge(R.eps_ready, 1)
                act.wait_ge(e_loaded, 16 * 5)
                act.wait_ge(ones_ready, 3)
                act.sem_inc(hid_ready, 1)
                hide(0, 0)
                hide(0, 1)
                R.scalar_std(act, 0, 0)
                with act.Fori(0, NC - 3, 2) as c:
                    for n in range(2):
                        hide(c, n + 2)
                        R.scalar_std(act, c, n + 1)
                        take(c, n)
                R.scalar_std(act, NC - 2, 1)
                take(NC - 2, 0)
                take(NC - 2, 1)

            @block.vector
            def _(dve):
                R.vector_setup(dve)
                nc.vector.memset(ones[:], 1.0).then_inc(ones_ready, 1)
                for i in range(2):
                    nc.vector.memset(hid[i][:], 1.0).then_inc(ones_ready, 1)
                for k in range(KD):
                    for c in range(NC):
                        st = nc.vector.bn_stats(bst[:, k, c, :], xt[:, k, c * TC:(c + 1) * TC])
                st.then_inc(step, 1)
                dve.wait_ge(step, 1)
                for k in range(KD):
                    st = nc.vector.bn_aggr(mv[:, k, :], bst[:, k, :, :].rearrange("p c s -> p (c s)"))
                st.then_inc(step, 1)
                dve.wait_ge(step, 2)
                dve.wait_ge(w_loaded, 48)
                for k in range(KD):
                    nc.vector.tensor_scalar(vec[:, k, 0:1], mv[:, k, 0:1], -2.0, None, ALU.mult)
                    nc.vector.scalar_tensor_tensor(out=vec[:, k, 1:2], in0=mv[:, k, 0:1], scalar=mv[:, k, 0:1],
                                                   in1=mv[:, k, 1:2], op0=ALU.mult, op1=ALU.add)
                    st = nc.vector.tensor_tensor(iv[:, k, :], disc[:, k, E0:2 * E0], disc[:, k, E0:2 * E0], ALU.mult)
                st.then_inc(step, 1)
                dve.wait_ge(step, 3)
                nc.vector.reciprocal(iv[:], iv[:]).then_inc(step, 1)
                for k in range(KD):
                    st = nc.vector.scalar_tensor_tensor(out=t[:, k, :], in0=disc[:, k, 0:E0], scalar=vec[:, k, 0:1],
                                                        in1=disc[:, k, 0:E0], op0=ALU.add, op1=ALU.mult)
                st.then_inc(step, 1)
                dve.wait_ge(step, 5)
                for k in range(KD):
                    st = nc.vector.tensor_scalar(t[:, k, :], t[:, k, :], vec[:, k, 1:2], None, ALU.add)
                st.then_inc(step, 1)
                dve.wait_ge(step, 6)
                nc.vector.tensor_tensor(t[:], t[:], iv[:], ALU.mult).then_inc(step, 1)
                dve.wait_ge(loss_mm, 1)
                nc.vector.tensor_scalar(loss[:, 0, :], p_m[0:1, 0:E0], -1.0 / DM, None, ALU.mult).then_inc(step, 1)
                dve.wait_ge(step, 8)
                nc.vector.max(loss[:, 1, :], loss[:, 0, :]).then_inc(step, 1)
                dve.wait_ge(step, 9)
                nc.vector.max_index(choice[:], loss[:, 1, :], loss[:, 0, :]).then_inc(chosen, 1)
                dve.wait_ge(fuse_mm, 1)
                dve.wait_ge(e_loaded, 16 * 5)
                nc.vector.tensor_copy(fused[0:R1, :], p_m[0:R1, 0:DM]).then_inc(fused_ready, 1)
                nc.vector.tensor_tensor(bias[R1:R1 + 1, 0, :], bias[R1:R1 + 1, 0, :], bias[R1:R1 + 1, 1, :],
                                        ALU.add).then_inc(step, 1)
                dve.wait_ge(step, 10)
                nc.vector.tensor_tensor(fused[R1:R1 + 1, :], p_m[R1:R1 + 1, 0:DM], bias[R1:R1 + 1, 0, :],
                                        ALU.add).then_inc(fused_ready, 1)

                def add(c, n):
                    if n:
                        R.wait_free(dve, c, n)
                    for j in range(JT):
                        dve.wait_ge(out_ready, c * JT + (n * JT + j + 1))
                        nc.vector.tensor_tensor(R.s[n % 2][:, j, :], p_o[j][:, 0:DM], xn[:, c * JT + (n * JT + j), :],
                                                ALU.add).then_inc(R.sum_ready, 1)
                    R.vector_stats(dve, c, n)

                def norm(c, n):
                    dve.wait_ge(kept, c + (n + 1))
                    R.vector_norm(dve, c, n)

                add(0, 0)
                with dve.Fori(0, NC - 3, 2) as c:
                    add(c, 1)
                    norm(c, 0)
                    add(c, 2)
                    norm(c, 1)
                add(NC - 2, 1)
                norm(NC - 2, 0)
                norm(NC - 2, 1)


NH = 16
DH = DM // NH
COMBOS = [(0, 0), (0, 1), (0, 2), (1, 0), (1, 1), (2, 0)]
SR = len(COMBOS) * DH
VW = 32


def qkv(nc, S, D, keep):
    xt, v_all = keep["xt"], keep["v_all"]
    with Mem(nc) as m:
        w_qk = m.sb("s5_w_qk", [P, KD, 2 * DM])
        w_v = m.sb("s5_w_v", [P, KD, DM])
        xs = [m.sb(f"s5_xs{i}", [P, KD, TC]) for i in range(2)]
        parts = [[m.sb(f"s5_parts{i}{t}", [P, 3, TC], BF16) for t in range(4)] for i in range(2)]
        rest = [m.sb(f"s5_rest{t}", [P, TC]) for t in range(4)]
        p_qk = [m.ps(f"s5_p_qk{i}", [P, TC]) for i in range(4)]
        p_v = [m.ps(f"s5_p_v{i}", [P, TC]) for i in range(2)]
        w_loaded, x_taken, v_mm, v_taken = S("w_loaded"), S("x_taken"), S("v_mm"), S("v_taken")
        qk_mm, hi_ready, rest_ready, mid_ready, low_ready = (
            S("qk_mm"), S("hi_ready"), S("rest_ready"), S("mid_ready"), S("low_ready"))
        gate = S("gate")
        qk_out = [[S(f"qk_out{i}{t}") for t in range(4)] for i in range(2)]

        with nc.Block() as block:
            @block.sync
            def _(sp):
                prime(sp, [v_mm, low_ready, *qk_out[0], *qk_out[1]])
                sp.dma_start(w_qk[:], D["w_qk"].rearrange("(k p) n -> p k n", p=P)).then_inc(w_loaded, 16)
                sp.dma_start(w_v[:], D["w_v"].rearrange("(k p) n -> p k n", p=P)).then_inc(w_loaded, 16)
                with sp.Fori(0, NC - 1, 2) as c:
                    for par in range(2):
                        for t in range(4):
                            sp.wait_ge(low_ready, PRIMED + c * 4 + (par * 4 + t + 1))
                            row = (t // 2) * 3 * DM + (t % 2) * P
                            sp.dma_start(D["qk"].rearrange("(a r) n -> r a n", r=DM)[
                                (t % 2) * P:(t % 2 + 1) * P, (t // 2) * 3:(t // 2) * 3 + 3,
                                bass.ds((c + par) * TC, TC)], parts[par][t][:]).then_inc(qk_out[par][t], 16)
                for par in range(2):
                    for t in range(4):
                        sp.wait_ge(qk_out[par][t], PRIMED + 16 * NC // 2)

            @block.gpsimd
            def _(pool):
                def take_x(c, n):
                    pool.tensor_copy(xs[n % 2][:], xt[:, :, bass.ds((c + n) * TC, TC)]).then_inc(x_taken, 1)

                def low_parts(c, n):
                    for t in range(4):
                        pool.wait_ge(mid_ready, c * 4 + (n * 4 + t + 1))
                        pool.tensor_tensor(parts[n][t][:, 2, :], rest[t][:], parts[n][t][:, 1, :],
                                           ALU.subtract).then_inc(low_ready, 1)

                take_x(0, 0)
                take_x(0, 1)
                with pool.Fori(0, NC - 3, 2) as c:
                    for n in range(2):
                        low_parts(c, n)
                        pool.wait_ge(v_mm, c * JT + (PRIMED + (n + 1) * JT))
                        pool.sem_inc(gate, 1)
                        take_x(c, n + 2)
                low_parts(NC - 2, 0)
                low_parts(NC - 2, 1)

            @block.tensor
            def _(pe):
                pe.wait_ge(w_loaded, 32)
                with pe.Fori(0, NC - 1, 2) as c:
                    for par in range(2):
                        pe.wait_ge(x_taken, c + (par + 1))
                        for t in range(4):
                            pe.wait_ge(rest_ready, c * 4 + (par * 4 + t + 1))
                            for k in range(KD):
                                mm = nc.tensor.matmul(p_qk[t][:], w_qk[:, k, t * P:(t + 1) * P], xs[par][:, k, :],
                                                      start=k == 0, stop=k == KD - 1)
                            mm.then_inc(qk_mm, 1)
                        for j in range(JT):
                            pe.wait_ge(v_taken, c * JT + (par * JT + j + 1))
                            for k in range(KD):
                                mm = nc.tensor.matmul(p_v[j % 2][:, 0:DM], xs[par][:, k, j * P:(j + 1) * P],
                                                      w_v[:, k, :], start=k == 0, stop=k == KD - 1)
                            mm.then_inc(v_mm, 1)

            @block.scalar
            def _(act):
                act.sem_inc(v_taken, 2)
                with act.Fori(0, NC - 1, 2) as c:
                    for par in range(2):
                        for t in range(4):
                            act.wait_ge(qk_mm, c * 4 + (par * 4 + t + 1))
                            act.wait_ge(qk_out[par][t], PRIMED + c * 8)
                            nc.scalar.copy(parts[par][t][:, 0, :], p_qk[t][:]).then_inc(hi_ready, 1)
                        for j in range(JT):
                            i = par * JT + j
                            act.wait_ge(rest_ready, c * 4 + (4 + i + 1))
                            nc.scalar.copy(parts[par][j][:, 1, :], rest[j][:]).then_inc(mid_ready, 1)
                            act.wait_ge(v_mm, PRIMED + c * JT + (i + 1))
                            nc.scalar.copy(v_all[:, :, c * JT + i, :],
                                           p_v[j % 2][:, 0:DM].rearrange("p (h d) -> p h d", h=NH)).then_inc(v_taken, 1)

            @block.vector
            def _(dve):
                dve.sem_inc(rest_ready, 4)
                with dve.Fori(0, NC - 1, 2) as c:
                    for par in range(2):
                        for t in range(4):
                            k = par * 4 + t
                            dve.wait_ge(hi_ready, c * 4 + (k + 1))
                            dve.wait_ge(low_ready, PRIMED + c * 4 + max(k - 3, 0))
                            nc.vector.tensor_tensor(rest[t][:], p_qk[t][:], parts[par][t][:, 0, :],
                                                    ALU.subtract).then_inc(rest_ready, 1)


def attention(nc, S, D, keep):
    v_all, att = keep["v_all"], keep["att"]
    NB = 3
    R1B, R2B, RPT = 3, 3, 8
    QUADS = [(Q, g) for Q in range(NC) for g in range(Q + 1)]
    LAST = {Q: max(b for b, x in enumerate(QUADS) if x[0] == Q) for Q in range(NC)}
    NQ = len(QUADS)
    TILES1 = [(i, kc) for i in range(TT) for kc in range(i // 4 + 1)]
    N1 = len(TILES1)
    S1 = N1 + 1
    SLOW = 4
    share = [(N1 * (b + 1)) // (NQ - SLOW) - (N1 * b) // (NQ - SLOW) for b in range(NQ - SLOW)] + [0] * SLOW
    TURN_AT = NQ - SLOW + 1
    MISC = NC + 1
    NEG = -3.0e38
    MAX_IN = 16 * 3
    STACK_IN = 16 * 2 * len(COMBOS)

    def count(h, per, more=0):
        return h[0] * per + (h[1] * per + more)

    def turns(h, per):
        return h[0] * (per // NB) + (h[1] // NB + 1) * per

    def comb_of(b):
        return next((Q for Q in range(NC - 1) if LAST[Q] + 2 == b), None)

    with Mem(nc) as m:
        qs = [m.sb(f"s6_qs{i}", [P, L], BF16) for i in range(NB)]
        ks = [m.sb(f"s6_ks{i}", [P, L], BF16) for i in range(NB)]
        vh = [m.sb(f"s6_vh{i}", [P, TT, VW]) for i in range(NB)]
        pt = [m.sb(f"s6_pt{i}", [P, TC]) for i in range(RPT)]
        oT = [m.sb(f"s6_oT{i}", [P, TC]) for i in range(2)]
        rec = [m.sb(f"s6_rec{i}", [P, JT]) for i in range(2)]
        mx = m.sb("s6_mx", [P, TT, NC])
        negm = m.sb("s6_negm", [P, TT])
        m_rest = m.sb("s6_m_rest", [TT, P])
        m_parts = m.sb("s6_m_parts", [TT, 3, P], BF16)
        identb = m.sb("s6_identb", [P, P], BF16)
        ident = m.sb("s6_ident", [P, P])
        comb = m.sb("s6_comb", [P, VW])
        mask1 = m.sb("s6_mask1", [P, P], BF16)
        mask2 = m.sb("s6_mask2", [P, TC], BF16)
        p_1 = [m.ps(f"s6_p_1{i}", [P, TC]) for i in range(R1B)]
        p_2 = [m.ps(f"s6_p_2{i}", [P, TC]) for i in range(R2B)]
        p_oT = m.ps("s6_p_oT", [P, TC])
        p_misc = m.ps("s6_p_misc", [P, TC])
        p_c = p_misc[:, 0:JT * VW].rearrange("p (j d) -> p j d", j=JT)
        p_mT = p_misc[0:TT, JT * VW:JT * VW + P]

        const_step, consts, buf_set = S("const_step"), S("consts"), S("buf_set")
        stack_in = [S(f"stack_in{i}") for i in range(NB)]
        m_in = [S(f"m_in{i}") for i in range(NB)]
        v_ready, s1_mm, s1_taken = S("v_ready"), S("s1_mm"), S("s1_taken")
        misc_mm, misc_taken, mstep, mp_ready = S("misc_mm"), S("misc_taken"), S("mstep"), S("mp_ready")
        s2_mm, exp_ready, pv_done, oT_taken, rec_ready = (
            S("s2_mm"), S("exp_ready"), S("pv_done"), S("oT_taken"), S("rec_ready"))

        with nc.Block() as block:
            @block.sync
            def _(sp):
                prime(sp, [pv_done, misc_mm])
                def send_maxima(h, buf):
                    sp.wait_ge(mp_ready, count(h, 1, 1))
                    for part in range(3):
                        sp.dma_start(qs[buf][SR + part:SR + part + 1, :].rearrange("o (i p) -> o i p", p=P),
                                     m_parts[:, part, :]).then_inc(m_in[buf], 16)

                send_maxima((0, 0), 0)
                with sp.Fori(0, NH - NB, NB) as r:
                    for i in range(1, NB + 1):
                        send_maxima((r, i), i % NB)

            @block.gpsimd
            def _(pool):
                def load(n, buf, behind):
                    if behind:
                        pool.wait_ge(pv_done, PRIMED + (n - (NB - 1)) * NQ)
                    pool.wait_ge(buf_set, 1)
                    for x, (qp, kp) in enumerate(COMBOS):
                        pool.dma_start(qs[buf][x * DH:(x + 1) * DH, :],
                                       D["qk"][bass.ds(n * DH + qp * DM, DH), :]).then_inc(stack_in[buf], 16)
                        pool.dma_start(ks[buf][x * DH:(x + 1) * DH, :],
                                       D["qk"][bass.ds(n * DH + (3 + kp) * DM, DH), :]).then_inc(stack_in[buf], 16)
                    pool.tensor_copy(vh[buf][:, :, 0:DH], v_all[:, n, :, :]).then_inc(v_ready, 1)

                set_identity(pool, ident, const_step, const_step)
                pool.memset(identb[:], 0.0).then_inc(const_step, 1)
                pool.wait_ge(const_step, 3)
                pool.affine_select(out=identb[:], in_=identb[:], compare_op=ALU.not_equal, fill=1.0, base=0,
                                   pattern=[[-1, P]], channel_multiplier=1).then_inc(const_step, 1)
                pool.memset(mask1[:], 0.0).then_inc(const_step, 1)
                pool.memset(mask2[:], NEG).then_inc(const_step, 1)
                pool.memset(comb[:], 0.0).then_inc(const_step, 1)
                pool.wait_ge(const_step, 7)
                pool.affine_select(out=mask1[:], in_=mask1[:], compare_op=ALU.is_ge, fill=NEG, base=0,
                                   pattern=[[-1, P]], channel_multiplier=1).then_inc(const_step, 1)
                pool.affine_select(out=mask2[:, TC - P:], in_=mask2[:, TC - P:], compare_op=ALU.is_gt, fill=0.0,
                                   base=0, pattern=[[-1, P]], channel_multiplier=1).then_inc(const_step, 1)
                for j in range(P // VW):
                    pool.wait_ge(const_step, 9 + j)
                    pool.affine_select(out=comb[:], in_=comb[:], compare_op=ALU.not_equal, fill=1.0, base=-VW * j,
                                       pattern=[[-1, VW]], channel_multiplier=1).then_inc(const_step, 1)
                for n in range(NB):
                    load(n, n, False)
                with pool.Fori(NB, NH - NB, NB) as n:
                    for i in range(NB):
                        load(n + i, i, True)
                load(NH - 1, (NH - 1) % NB, True)

            @block.tensor
            def _(pe):
                def first_pass(h, buf, x):
                    i, kc = TILES1[x]
                    last = kc == i // 4
                    w = (i % 4 + 1) * P if last else TC
                    pe.wait_ge(s1_taken, count(h, S1, x + 1))
                    mm = nc.tensor.matmul(p_1[x % R1B][:, 0:w], qs[buf][0:SR, i * P:(i + 1) * P],
                                          ks[buf][0:SR, kc * TC:kc * TC + w], start=True, stop=not last)
                    if last:
                        mm = nc.tensor.matmul(p_1[x % R1B][:, w - P:w], identb[:], mask1[:], start=False, stop=True)
                    mm.then_inc(s1_mm, 1)

                def second_pass(h, buf, b, x):
                    Q, g = QUADS[b]
                    t, k = 4 * g + x, 4 * b + x
                    over = (t - 4 * Q) * P if t > 4 * Q else 0
                    off = over if Q else 0
                    pe.wait_ge(exp_ready, count(h, 4 * NQ, k + 1))
                    p = p_2[k % R2B]
                    mm = nc.tensor.matmul(p[:, off:TC], ks[buf][0:SR + 3, t * P:(t + 1) * P],
                                          qs[buf][0:SR + 3, Q * TC + off:(Q + 1) * TC], start=True, stop=t < 4 * Q)
                    if t >= 4 * Q:
                        lead = 0 if Q else over
                        mm = nc.tensor.matmul(p[:, off:off + lead + P], identb[:], mask2[:, TC - P - lead:TC],
                                              start=False, stop=True)
                    mm.then_inc(s2_mm, 1)

                def values(h, buf, b):
                    Q, g = QUADS[b]
                    if g == 0:
                        pe.wait_ge(oT_taken, count(h, NC, Q + 1))
                    for x in range(4):
                        t, k = 4 * g + x, 4 * b + x
                        off = (t - 4 * Q) * P if Q and t > 4 * Q else 0
                        pe.wait_ge(exp_ready, count(h, 4 * NQ, R2B + k + 1))
                        mm = nc.tensor.matmul(p_oT[x * VW:(x + 1) * VW, off:TC], vh[buf][:, t, :],
                                              pt[k % RPT][:, off:TC], start=g == 0, stop=g == Q)
                    mm.then_inc(pv_done, 1)

                def combine(h, Q, use):
                    pe.wait_ge(oT_taken, count(h, NC, Q + 2))
                    pe.wait_ge(misc_taken, count(h, MISC, use))
                    for j in range(JT):
                        mm = nc.tensor.matmul(p_c[:, j, 0:DH + 1], oT[Q % 2][:, j * P:(j + 1) * P],
                                              comb[:, 0:DH + 1], start=True, stop=True)
                    mm.then_inc(misc_mm, 1)

                def turn_maxima(h, use):
                    pe.wait_ge(s1_taken, count(h, S1, R1B + S1))
                    pe.wait_ge(misc_taken, use)
                    nc.tensor.transpose(p_mT, negm[:], ident[:]).then_inc(misc_mm, 1)

                def head(h, ahead):
                    after, buf, nxt = (h[0], h[1] + 1), h[1], (h[1] + 1) % NB
                    pe.wait_ge(m_in[buf], turns(h, MAX_IN))
                    pe.wait_ge(v_ready, count(h, 1, 1))
                    if ahead:
                        pe.wait_ge(stack_in[nxt], turns(after, STACK_IN))
                    x1, use = 0, 1
                    for b in range(NQ):
                        n1 = share[b] if ahead else 0
                        for x in range(4):
                            if x == 3 and b:
                                values(h, buf, b - 1)
                            for _ in range(n1 // 4 + (x < n1 % 4)):
                                first_pass(after, nxt, x1)
                                x1 += 1
                            second_pass(h, buf, b, x)
                        if comb_of(b) is not None:
                            combine(h, comb_of(b), use)
                            use += 1
                        if b == TURN_AT and ahead:
                            turn_maxima(after, count(h, MISC, use))
                            use += 1
                    values(h, buf, NQ - 1)
                    combine(h, NC - 1, use)

                pe.wait_ge(buf_set, 1)
                pe.wait_ge(const_step, 9 + P // VW)
                pe.wait_ge(stack_in[0], STACK_IN)
                for x in range(N1):
                    first_pass((0, 0), 0, x)
                turn_maxima((0, 0), 0)
                with pe.Fori(0, NH - NB, NB) as r:
                    for i in range(NB):
                        head((r, i), True)
                head((NH - 1, 0), False)

            @block.scalar
            def _(act):
                def head(h):
                    for b, (Q, g) in enumerate(QUADS):
                        for x in range(4):
                            k = 4 * b + x
                            off = (4 * g + x - 4 * Q) * P if Q and g == Q else 0
                            act.wait_ge(s2_mm, count(h, 4 * NQ, k + 1))
                            if x == 0:
                                act.wait_ge(pv_done, PRIMED + count(h, NQ, max(b - 1, 0)))
                            nc.scalar.activation(pt[k % RPT][:, off:TC], p_2[k % R2B][:, off:TC], ACT.Exp,
                                                 scale=DH ** -0.5).then_inc(exp_ready, 1)
                        done = Q - 1 if g == 0 and Q else (NC - 1 if b == NQ - 1 else None)
                        if done is not None:
                            act.wait_ge(pv_done, PRIMED + count(h, NQ, LAST[done] + 1))
                            act.wait_ge(misc_mm, PRIMED + count(h, MISC, done))
                            nc.scalar.copy(oT[done % 2][:], p_oT[:]).then_inc(oT_taken, 1)

                act.sem_inc(exp_ready, R2B)
                act.sem_inc(oT_taken, 1)
                with act.Fori(0, NH) as r:
                    head((r, 0))

            @block.vector
            def _(dve):
                def row_max(h, x):
                    i, kc = TILES1[x]
                    w = (i % 4 + 1) * P if kc == i // 4 else TC
                    dve.wait_ge(s1_mm, count(h, N1, x + 1))
                    nc.vector.reduce_max(mx[:, i, kc:kc + 1], p_1[x % R1B][:, 0:w], AXX).then_inc(s1_taken, 1)

                def negate(h):
                    dve.wait_ge(s1_taken, count(h, S1, R1B + N1))
                    nc.vector.tensor_reduce(negm[:], mx[:], AXX, ALU.max, negate=True).then_inc(s1_taken, 1)

                def split_maxima(h, use):
                    dve.wait_ge(misc_mm, PRIMED + use + 1)
                    nc.vector.tensor_copy(m_parts[:, 0, :], p_mT).then_inc(mstep, 1)
                    dve.wait_ge(mstep, count(h, 2, 1))
                    nc.vector.tensor_tensor(m_rest[:], p_mT, m_parts[:, 0, :], ALU.subtract).then_inc(misc_taken, 1)
                    dve.wait_ge(misc_taken, use + 1)
                    nc.vector.tensor_copy(m_parts[:, 1, :], m_rest[:]).then_inc(mstep, 1)
                    dve.wait_ge(mstep, count(h, 2, 2))
                    nc.vector.tensor_tensor(m_parts[:, 2, :], m_rest[:], m_parts[:, 1, :],
                                            ALU.subtract).then_inc(mp_ready, 1)

                def divide(h, Q, use):
                    dve.wait_ge(misc_mm, PRIMED + count(h, MISC, use + 1))
                    dve.wait_ge(misc_taken, count(h, MISC, use))
                    nc.vector.reciprocal(rec[Q % 2][:], p_c[:, :, DH]).then_inc(rec_ready, 1)
                    dve.wait_ge(rec_ready, count(h, NC, Q + 1))
                    nc.vector.tensor_tensor(att[:, Q * JT:(Q + 1) * JT, bass.ds(count(h, DH), DH)], p_c[:, :, 0:DH],
                                            rec[Q % 2][:].unsqueeze(2).to_broadcast([P, JT, DH]),
                                            ALU.mult).then_inc(misc_taken, 1)

                def head(h, ahead):
                    after, x1, use = (h[0], h[1] + 1), 0, 1
                    for b in range(NQ):
                        for _ in range(share[b] if ahead else 0):
                            row_max(after, x1)
                            x1 += 1
                        if b == NQ - SLOW - 1 and ahead:
                            negate(after)
                        if comb_of(b) is not None:
                            divide(h, comb_of(b), use)
                            use += 1
                        if b == TURN_AT and ahead:
                            dve.wait_ge(m_in[h[1]], turns(h, MAX_IN))
                            split_maxima(after, count(h, MISC, use))
                            use += 1
                    divide(h, NC - 1, use)

                dve.sem_inc(s1_taken, R1B)
                for i in range(NB):
                    nc.vector.memset(vh[i][:], 0.0).then_inc(consts, 1)
                    nc.vector.memset(ks[i][SR:SR + 3, :], 1.0).then_inc(consts, 1)
                nc.vector.memset(mx[:], NEG).then_inc(consts, 1)
                dve.wait_ge(consts, 2 * NB + 1)
                for i in range(NB):
                    st = nc.vector.memset(vh[i][:, :, DH:DH + 1], 1.0)
                st.then_inc(buf_set, 1)
                for x in range(N1):
                    row_max((0, 0), x)
                negate((0, 0))
                split_maxima((0, 0), 0)
                with dve.Fori(0, NH - NB, NB) as r:
                    for i in range(NB):
                        head((r, i), True)
                head((NH - 1, 0), False)


E1 = 8
DF = 1024
KF = DF // P
BLOCKS = TT + E1 - 1


def attention_out(nc, S, D, keep):
    xn, att, aff = keep["xn"], keep["att"], keep["aff"]
    with Mem(nc) as m:
        w_o = m.sb("s7_w_o", [P, KD, DM])
        cent = m.sb("s7_cent", [P, KD, E1])
        zeros = m.sb("s7_zeros", [P, DM])
        ident = m.sb("s7_ident", [P, P])
        ya = [m.sb(f"s7_ya{i}", [P, JT, DM]) for i in range(2)]
        yT = [m.sb(f"s7_yT{i}", [P, KD, TC]) for i in range(2)]
        p_u = [m.ps(f"s7_p_u{i}", [P, TC]) for i in range(KD)]
        p_t = [m.ps(f"s7_p_t{i}", [P, TC]) for i in range(KD)]
        p_o = [m.ps(f"s7_p_o{i}", [P, 2, DM]) for i in range(JT // 2)]
        p_a = m.ps("s7_p_a", [P, JT, E1])
        R = NormRing(m, S, "s7a")
        R2 = NormRing(m, S, "s7b", of=R)
        x3T = [m.sb(f"s7_x3T{i}", [P, KD, TC]) for i in range(2)]
        w_loaded, cleared, ident_ready = S("w_loaded"), S("cleared"), S("ident_ready")
        zeros_ready, zero_out = S("zeros_ready"), S("zero_out")
        gate = S("gate")
        att_taken, att_turned, yT_ready, out_ready = S("att_taken"), S("att_turned"), S("yT_ready"), S("out_ready")
        kept, turned, x3T_ready, aff_mm, aff_taken, kept2 = (
            S("kept"), S("turned"), S("x3T_ready"), S("aff_mm"), S("aff_taken"), S("kept2"))

        with nc.Block() as block:
            @block.sync
            def _(sp):
                prime(sp, [yT_ready, x3T_ready, aff_taken])
                sp.dma_start(w_o[:], D["w_o"].rearrange("(k p) n -> p k n", p=P)).then_inc(w_loaded, 16)
                sp.dma_start(cent[:], D["cent"].rearrange("(k p) n -> p k n", p=P)).then_inc(w_loaded, 16)
                sp.wait_ge(zeros_ready, 1)
                sp.dma_start(D["sorted_in"].rearrange("(b p) n -> p b n", p=P),
                             zeros[:].unsqueeze(1).to_broadcast([P, BLOCKS, DM])).then_inc(zero_out, 16)
                for e in range(E1):
                    sp.dma_start(keep["w1"][:, e * KD:(e + 1) * KD, :],
                                 D["w1"][e].rearrange("(k p) n -> p k n", p=P)).then_inc(keep["w1_in"], 16)
                sp.wait_ge(zero_out, 16)

            @block.gpsimd
            def _(pool):
                pool.memset(zeros[:], 0.0).then_inc(zeros_ready, 1)
                set_identity(pool, ident, cleared, ident_ready)
                pool.sem_inc(kept, FREE)
                pool.sem_inc(kept2, FREE)

                def take_att(c, n):
                    pool.tensor_copy(ya[n % 2][:], att[:, bass.ds((c + n) * JT, JT), :]).then_inc(att_taken, 1)

                def keep_x3(c, n):
                    at = bass.ds((c + n) * JT, JT)
                    R.wait_normed(pool, c, n)
                    pool.tensor_tensor(xn[:, at, :], R.y[n][:], R.y[n][:], ALU.add).then_inc(kept, 1)

                def keep_input(c, n):
                    at = bass.ds((c + n) * JT, JT)
                    R2.wait_normed(pool, c, n)
                    pool.wait_ge(att_taken, c + (n + 1))
                    pool.sem_inc(gate, 1)
                    pool.tensor_copy(att[:, at, :], R2.y[n][:]).then_inc(kept2, 1)

                take_att(0, 0)
                take_att(0, 1)
                with pool.Fori(0, NC - 3, 2) as c:
                    pool.wait_ge(att_turned, c + 1)
                    take_att(c, 2)
                    keep_x3(c, 0)
                    pool.wait_ge(att_turned, c + 2)
                    take_att(c, 3)
                    keep_input(c, 0)
                    keep_x3(c, 1)
                    keep_input(c, 1)
                for n in range(2):
                    keep_x3(NC - 2, n)
                    keep_input(NC - 2, n)

            @block.tensor
            def _(pe):
                def turn_att(c, n):
                    pe.wait_ge(att_taken, c + (n + 1))
                    pe.wait_ge(yT_ready, c + (PRIMED + n))
                    for k in range(KD):
                        for j in range(JT):
                            tr = nc.tensor.transpose(p_u[k][:, j * P:(j + 1) * P],
                                                     ya[n % 2][:, j, k * P:(k + 1) * P], ident[:])
                    tr.then_inc(att_turned, 1)

                def project(c, n):
                    pe.wait_ge(yT_ready, c + (PRIMED + n + 1))
                    for i in range(JT // 2):
                        if n:
                            pe.wait_ge(R.sum_ready, c * JT + (PRIMED + (n - 1) * JT + 2 * i + 2))
                        for j in range(2):
                            at = (2 * i + j) * P
                            for k in range(KD):
                                mm = nc.tensor.matmul(p_o[i][:, j, :], yT[n % 2][:, k, at:at + P], w_o[:, k, :],
                                                      start=k == 0, stop=k == KD - 1)
                        mm.then_inc(out_ready, 1)

                def turn_x3(c, n):
                    R.wait_normed(pe, c, n)
                    pe.wait_ge(x3T_ready, c + (PRIMED + n))
                    for k in range(KD):
                        for j in range(JT):
                            tr = nc.tensor.transpose(p_t[k][:, j * P:(j + 1) * P],
                                                     R.y[n % 2][:, j, k * P:(k + 1) * P], ident[:])
                    tr.then_inc(turned, 1)

                def affinity(c, n):
                    pe.wait_ge(x3T_ready, c + (PRIMED + n + 1))
                    pe.wait_ge(aff_taken, c + (PRIMED + n))
                    for j in range(JT):
                        for k in range(KD):
                            mm = nc.tensor.matmul(p_a[:, j, :], x3T[n % 2][:, k, j * P:(j + 1) * P],
                                                  cent[:, k, :], start=k == 0, stop=k == KD - 1)
                    mm.then_inc(aff_mm, 1)

                pe.wait_ge(w_loaded, 32)
                pe.wait_ge(ident_ready, 1)
                turn_att(0, 0)
                turn_att(0, 1)
                project(0, 0)
                project(0, 1)
                with pe.Fori(0, NC - 3, 2) as c:
                    for n in range(2):
                        turn_att(c, n + 2)
                        turn_x3(c, n)
                        project(c, n + 2)
                        affinity(c, n)
                for n in range(2):
                    turn_x3(NC - 2, n)
                    affinity(NC - 2, n)

            @block.scalar
            def _(act):
                def take_yT(c, n):
                    act.wait_ge(att_turned, c + (n + 1))
                    if n > 1:
                        act.wait_ge(out_ready, c * 2 + (n - 1) * 2)
                    for k in range(KD):
                        cp = nc.scalar.copy(yT[n % 2][:, k, :], p_u[k][:])
                    cp.then_inc(yT_ready, 1)

                def take_x3T(c, n):
                    act.wait_ge(turned, c + (n + 1))
                    for k in range(KD):
                        cp = nc.scalar.copy(x3T[n % 2][:, k, :], p_t[k][:])
                    cp.then_inc(x3T_ready, 1)

                def take_affinity(c, n):
                    act.wait_ge(aff_mm, c + (n + 1))
                    nc.scalar.copy(aff[:, bass.ds((c + n) * JT, JT), :], p_a[:]).then_inc(aff_taken, 1)

                act.wait_ge(R.eps_ready, 1)
                act.wait_ge(R2.eps_ready, 1)
                take_yT(0, 0)
                take_yT(0, 1)
                R.scalar_std(act, 0, 0)
                with act.Fori(0, NC - 3, 2) as c:
                    for n in range(2):
                        take_yT(c, n + 2)
                        R.scalar_std(act, c, n + 1)
                        take_x3T(c, n)
                        R2.scalar_std(act, c, n)
                        take_affinity(c, n)
                R.scalar_std(act, NC - 2, 1)
                for n in range(2):
                    take_x3T(NC - 2, n)
                    R2.scalar_std(act, NC - 2, n)
                    take_affinity(NC - 2, n)

            @block.vector
            def _(dve):
                def add(c, n):
                    if n:
                        R.wait_free(dve, c, n)
                    for i in range(JT // 2):
                        dve.wait_ge(out_ready, c * 2 + (2 * n + i + 1))
                        nc.vector.tensor_tensor(R.s[n % 2][:, 2 * i:2 * i + 2, :], p_o[i][:],
                                                xn[:, bass.ds(c * JT + (n * JT + 2 * i), 2), :],
                                                ALU.add).then_inc(R.sum_ready, 2)
                    R.vector_stats(dve, c, n)

                def norm(c, n):
                    dve.wait_ge(kept, c + (n + 1))
                    R2.wait_free(dve, c, n)
                    R.vector_norm(dve, c, n)
                    R2.vector_stats(dve, c, n)

                def norm_again(c, n):
                    dve.wait_ge(kept2, c + (n + 1))
                    R2.vector_norm(dve, c, n)

                R.vector_setup(dve)
                R2.vector_setup(dve)
                add(0, 0)
                with dve.Fori(0, NC - 3, 2) as c:
                    add(c, 1)
                    norm(c, 0)
                    add(c, 2)
                    norm_again(c, 0)
                    norm(c, 1)
                    norm_again(c, 1)
                add(NC - 2, 1)
                norm(NC - 2, 0)
                norm(NC - 2, 1)
                norm_again(NC - 2, 0)
                norm_again(NC - 2, 1)


def route(nc, S, D, keep):
    att, aff, alpha, slot, expert_of = (keep[n] for n in ("att", "aff", "alpha", "slot", "expert_of"))
    with Mem(nc) as m:
        top = m.sb("s8_top", [P, TT])
        order = m.sb("s8_order", [P, 1, E1])
        hit = m.sb("s8_hit", [P, TT, E1])
        first = m.sb("s8_first", [P, TT])
        onehot = m.sb("s8_onehot", [P, TT, E1])
        onehot_b = m.sb("s8_onehot_b", [P, TT, E1], BF16)
        triangle = m.sb("s8_triangle", [P, P], BF16)
        ones = m.sb("s8_ones", [P, P], BF16)
        ex = m.sb("s8_ex", [P, TT])
        count = m.sb("s8_count", [P, E1, TT])
        carry = m.sb("s8_carry", [P, E1, TT])
        upto = m.sb("s8_upto", [P, E1, TT])
        before = m.sb("s8_before", [P, E1, TT])
        steps = m.sb("s8_steps", [P, 1, BLOCKS])
        starts = m.sb("s8_starts", [P, 1, TT])
        over = m.sb("s8_over", [P, E1, TT])
        need = m.sb("s8_need", [P, E1])
        ones8 = m.sb("s8_ones8", [P, E1])
        ends = m.sb("s8_ends", [P, E1])
        base = m.sb("s8_base", [P, E1])
        place = m.sb("s8_place", [P, TT, E1])
        slot_f = m.sb("s8_slot_f", [P, TT])
        past = m.sb("s8_past", [1, BLOCKS, E1])
        number = m.sb("s8_number", [1, BLOCKS])
        p_rank = m.ps("s8_p_rank", [P, TT, E1])
        p_count = m.ps("s8_p_count", [P, TT, E1])
        consts, tri_step, onehot_ready, rank_mm = S("consts"), S("tri_step"), S("onehot_ready"), S("rank_mm")
        step, top_ready, exp_ready, slots_ready, scattered = (
            S("step"), S("top_ready"), S("exp_ready"), S("slots_ready"), S("scattered"))
        NCONST = 6 + E1

        with nc.Block() as block:
            @block.sync
            def _(sp):
                for e in range(E1):
                    sp.dma_start(keep["w2"][:, e * KF:(e + 1) * KF, :],
                                 D["w2"][e].rearrange("(k p) n -> p k n", p=P)).then_inc(keep["w2_in"], 16)

            @block.gpsimd
            def _(pool):
                for e in range(E1):
                    pool.memset(order[:, :, e:e + 1], float(E1 - e)).then_inc(consts, 1)
                pool.iota(steps[:, 0, :], pattern=[[1, BLOCKS]], base=0, channel_multiplier=0,
                          allow_small_or_imprecise_dtypes=True).then_inc(consts, 1)
                pool.iota(starts[:, 0, :], pattern=[[P, TT]], base=0, channel_multiplier=0,
                          allow_small_or_imprecise_dtypes=True).then_inc(consts, 1)
                pool.memset(ones[:], 1.0).then_inc(consts, 1)
                pool.memset(ones8[:], 1.0).then_inc(consts, 1)
                pool.memset(carry[:], 1.0).then_inc(tri_step, 1)
                pool.memset(triangle[:], 1.0).then_inc(tri_step, 1)
                pool.wait_ge(tri_step, 2)
                pool.memset(carry[:, :, 0:1], 0.0).then_inc(consts, 1)
                pool.affine_select(out=triangle[:], in_=triangle[:], compare_op=ALU.is_gt, fill=0.0, base=0,
                                   pattern=[[1, P]], channel_multiplier=-1).then_inc(consts, 1)
                pool.wait_ge(slots_ready, 1)
                for t in range(TT):
                    pool.indirect_dma_start(D["sorted_in"][:], bass.IndirectOffsetOnAxis(ap=slot[:, t:t + 1], axis=0),
                                            att[:, t, :], None).then_inc(scattered, 16)
                pool.wait_ge(scattered, 16 * TT)

            @block.tensor
            def _(pe):
                pe.wait_ge(consts, NCONST)
                pe.wait_ge(onehot_ready, 1)
                nc.tensor.matmul(p_rank[:], triangle[:], onehot_b[:], start=True, stop=True)
                nc.tensor.matmul(p_count[:], ones[:], onehot_b[:], start=True, stop=True).then_inc(rank_mm, 1)

            @block.scalar
            def _(act):
                act.wait_ge(top_ready, 1)
                nc.scalar.activation(ex[:], top[:], ACT.Exp, scale=-1.0).then_inc(exp_ready, 1)

            @block.vector
            def _(dve):
                dve.wait_ge(consts, NCONST)
                nc.vector.tensor_reduce(top[:], aff[:], AXX, ALU.max).then_inc(top_ready, 1)
                dve.wait_ge(top_ready, 1)
                nc.vector.tensor_tensor(hit[:], aff[:], top[:].unsqueeze(2).to_broadcast([P, TT, E1]),
                                        ALU.is_equal).then_inc(step, 1)
                dve.wait_ge(step, 1)
                nc.vector.tensor_tensor(hit[:], hit[:], order[:].to_broadcast([P, TT, E1]), ALU.mult).then_inc(step, 1)
                dve.wait_ge(step, 2)
                nc.vector.tensor_reduce(first[:], hit[:], AXX, ALU.max).then_inc(step, 1)
                dve.wait_ge(step, 3)
                nc.vector.tensor_tensor(onehot[:], hit[:], first[:].unsqueeze(2).to_broadcast([P, TT, E1]),
                                        ALU.is_equal).then_inc(step, 1)
                dve.wait_ge(step, 4)
                nc.vector.tensor_copy(onehot_b[:], onehot[:]).then_inc(onehot_ready, 1)
                dve.wait_ge(exp_ready, 1)
                nc.vector.tensor_scalar(ex[:], ex[:], 1.0, None, ALU.add).then_inc(step, 1)
                dve.wait_ge(step, 5)
                nc.vector.reciprocal(alpha[:], ex[:]).then_inc(step, 1)
                dve.wait_ge(step, 6)
                dve.wait_ge(rank_mm, 1)
                nc.vector.tensor_copy(count[:], p_count[:].rearrange("p t e -> p e t")).then_inc(step, 1)
                dve.wait_ge(step, 7)
                nc.vector.tensor_tensor_scan(upto[:].rearrange("p e t -> p (e t)"),
                                             carry[:].rearrange("p e t -> p (e t)"),
                                             count[:].rearrange("p e t -> p (e t)"), 0.0, ALU.mult, ALU.add).then_inc(step, 1)
                dve.wait_ge(step, 8)
                nc.vector.tensor_tensor(before[:], upto[:], count[:], ALU.subtract).then_inc(step, 1)
                dve.wait_ge(step, 9)
                nc.vector.tensor_tensor(over[:], upto[:, :, TT - 1:TT].to_broadcast([P, E1, TT]),
                                        starts[:].to_broadcast([P, E1, TT]), ALU.is_gt).then_inc(step, 1)
                dve.wait_ge(step, 10)
                nc.vector.tensor_reduce(need[:], over[:], AXX, ALU.add).then_inc(step, 1)
                dve.wait_ge(step, 11)
                nc.vector.tensor_tensor_scan(ends[:], ones8[:], need[:], 0.0, ALU.mult, ALU.add).then_inc(step, 1)
                dve.wait_ge(step, 12)
                nc.vector.tensor_tensor(base[:], ends[:], need[:], ALU.subtract).then_inc(step, 1)
                dve.wait_ge(step, 13)
                nc.vector.tensor_scalar(base[:], base[:], float(P), None, ALU.mult).then_inc(step, 1)
                dve.wait_ge(step, 14)
                nc.vector.tensor_tensor(before[:], before[:], base[:].unsqueeze(2).to_broadcast([P, E1, TT]),
                                        ALU.add).then_inc(step, 1)
                dve.wait_ge(step, 15)
                nc.vector.tensor_tensor(place[:], p_rank[:], before[:].rearrange("p e t -> p t e"), ALU.add).then_inc(step, 1)
                dve.wait_ge(step, 16)
                nc.vector.tensor_tensor(place[:], place[:], onehot[:], ALU.mult).then_inc(step, 1)
                dve.wait_ge(step, 17)
                nc.vector.tensor_reduce(slot_f[:], place[:], AXX, ALU.add).then_inc(step, 1)
                dve.wait_ge(step, 18)
                nc.vector.tensor_copy(slot[:], slot_f[:]).then_inc(slots_ready, 1)
                nc.vector.tensor_tensor(past[:], ends[0:1, :].unsqueeze(1).to_broadcast([1, BLOCKS, E1]),
                                        steps[0:1, 0, :].unsqueeze(2).to_broadcast([1, BLOCKS, E1]), ALU.is_le).then_inc(step, 1)
                dve.wait_ge(step, 19)
                nc.vector.tensor_reduce(number[:], past[:], AXX, ALU.add).then_inc(step, 1)
                dve.wait_ge(step, 20)
                nc.vector.tensor_scalar(number[:], number[:], float(E1 - 1), None, ALU.min).then_inc(step, 1)
                dve.wait_ge(step, 21)
                nc.vector.tensor_copy(expert_of[:], number[:]).then_inc(step, 1)
                dve.wait_ge(step, 22)


def experts(nc, S, D, keep):
    w1, w2, expert_of = keep["w1"], keep["w2"], keep["expert_of"]
    N3 = 3
    TURNS = BLOCKS // N3
    with Mem(nc) as m:
        ln = m.sb("s9_ln", [P, E1, KD, 2])
        b1 = m.sb("s9_b1", [P, E1 * KF])
        b2 = m.sb("s9_b2", [P, E1, DM])
        ident = m.sb("s9_ident", [P, P])
        area = keep["att"][:].rearrange("p (n k) d -> p n (k d)", k=KF // KD)
        h = [area[:, i, :] for i in range(N3)]
        hT = [area[:, N3 + i, :].rearrange("p (k t) -> p k t", t=P) for i in range(N3)]
        xb = [area[:, 2 * N3, i * DM:(i + 1) * DM] for i in range(N3)]
        xT = [area[:, 2 * N3 + 1, i * DM:(i + 1) * DM].rearrange("p (k t) -> p k t", t=P) for i in range(N3)]
        y = [m.sb(f"s9_y{i}", [P, DM]) for i in range(N3)]
        p_x = m.ps("s9_p_x", [P, KD, P])
        p_h = [m.ps(f"s9_p_h{i}", [P, TC]) for i in range(2)]
        p_t = [m.ps(f"s9_p_t{i}", [P, KF // 2, P]) for i in range(2)]
        p_y = m.ps("s9_p_y", [P, DM])
        vec_in, cleared, ident_ready = S("vec_in"), S("cleared"), S("ident_ready")
        x_in = [S(f"x_in{i}") for i in range(N3)]
        y_out = [S(f"y_out{i}") for i in range(N3)]
        x_turned, xT_ready, h_mm, h_taken = S("x_turned"), S("xT_ready"), S("h_mm"), [S("h0_taken"), S("h1_taken")]
        h_turned, hT_ready = S("h_turned"), [S("hT0_ready"), S("hT1_ready")]
        y_mm, y_ready = S("y_mm"), S("y_ready")

        def n(q, i, per, more):
            return q * (N3 * per) + (i * per + more)

        def expert(eng, q, i):
            return eng.value_load(expert_of[0:1, bass.ds(q * N3 + i, 1)], min_val=0, max_val=E1 - 1)

        with nc.Block() as block:
            @block.sync
            def _(sp):
                prime(sp, [*hT_ready, y_ready, *y_out])
                def load(q, i):
                    sp.dma_start(xb[i % N3][:], D["sorted_in"][bass.ds(q * (N3 * P) + i * P, P), :]
                                 ).then_inc(x_in[i % N3], 16)

                def store(q, i):
                    sp.wait_ge(y_ready, PRIMED + n(q, i, 1, 1))
                    sp.dma_start(D["sorted_out"][bass.ds(q * (N3 * P) + i * P, P), :], y[i][:]).then_inc(y_out[i], 16)

                for i in range(N3):
                    load(0, i)
                sp.dma_start(ln[:], D["ln"]).then_inc(vec_in, 16)
                sp.dma_start(b1[:], D["b1"]).then_inc(vec_in, 16)
                sp.dma_start(b2[:], D["b2"]).then_inc(vec_in, 16)
                with sp.Fori(0, TURNS - 1) as q:
                    for i in range(N3):
                        sp.wait_ge(x_turned, n(q, i, 1, 1))
                        load(q, i + N3)
                        store(q, i)
                for i in range(N3):
                    store(TURNS - 1, i)
                for i in range(N3):
                    sp.wait_ge(y_out[i], PRIMED + 16 * TURNS)

            @block.gpsimd
            def _(pool):
                set_identity(pool, ident, cleared, ident_ready)

            @block.tensor
            def _(pe):
                def turn_x(q, i):
                    pe.wait_ge(x_in[i % N3], q * 16 + (i // N3 + 1) * 16)
                    pe.wait_ge(xT_ready, n(q, i, 1, 0))
                    for k in range(KD):
                        tr = nc.tensor.transpose(p_x[:, k, :], xb[i % N3][:, k * P:(k + 1) * P], ident[:])
                    tr.then_inc(x_turned, 1)

                def hidden(q, i, e, half):
                    pe.wait_ge(xT_ready, n(q, i, 1, 1))
                    pe.wait_ge(h_taken[half], n(q, i, 1, 0))
                    for k in range(KD):
                        mm = nc.tensor.matmul(p_h[half][:], xT[i % N3][:, k, :],
                                              w1[:, e * KD + k, half * TC:(half + 1) * TC],
                                              start=k == 0, stop=k == KD - 1)
                    mm.then_inc(h_mm, 1)

                def turn_hidden(q, i, half):
                    pe.wait_ge(h_taken[half], n(q, i, 1, 1))
                    pe.wait_ge(hT_ready[half], PRIMED + n(q, i, 1, 0))
                    for k in range(KF // 2):
                        at = (half * (KF // 2) + k) * P
                        tr = nc.tensor.transpose(p_t[half][:, k, :], h[i][:, at:at + P], ident[:])
                    tr.then_inc(h_turned, 1)

                def down(q, i, e):
                    pe.wait_ge(y_ready, PRIMED + n(q, i, 1, 0))
                    for k in range(KF):
                        if k % (KF // 2) == 0:
                            pe.wait_ge(hT_ready[k // (KF // 2)], PRIMED + n(q, i, 1, 1))
                        mm = nc.tensor.matmul(p_y[:], hT[i][:, k, :], w2[:, e * KF + k, :],
                                              start=k == 0, stop=k == KF - 1)
                    mm.then_inc(y_mm, 1)

                def block_step(q, i, last):
                    ahead = not last or i + 1 < N3
                    if ahead:
                        e_next = expert(pe, q, i + 1)
                    for half in range(2):
                        if ahead:
                            hidden(q, i + 1, e_next, half)
                        turn_hidden(q, i, half)
                    if not last or i + 2 < N3:
                        turn_x(q, i + 2)
                    down(q, i, expert(pe, q, i))

                pe.wait_ge(ident_ready, 1)
                pe.wait_ge(keep["w1_in"], 16 * E1)
                turn_x(0, 0)
                turn_x(0, 1)
                e = expert(pe, 0, 0)
                hidden(0, 0, e, 0)
                hidden(0, 0, e, 1)
                pe.wait_ge(keep["w2_in"], 16 * E1)
                with pe.Fori(0, TURNS - 1) as q:
                    for i in range(N3):
                        block_step(q, i, False)
                for i in range(N3):
                    block_step(TURNS - 1, i, True)

            @block.scalar
            def _(act):
                def take_hidden(q, i):
                    act.wait_ge(h_mm, n(q, i, 2, 1))
                    nc.scalar.copy(h[i % N3][:, 0:TC], p_h[0][:]).then_inc(h_taken[0], 1)

                def block_step(q, i, last):
                    if not last or i + 1 < N3:
                        take_hidden(q, i + 1)
                    e = expert(act, q, i)
                    act.wait_ge(h_turned, n(q, i, 2, 1))
                    for k in range(KF // 2):
                        rl = nc.scalar.activation(hT[i][:, k, :], p_t[0][:, k, :], ACT.Relu,
                                                  bias=b1[:, bass.ds(e * KF + k, 1)])
                    rl.then_inc(hT_ready[0], 1)

                act.wait_ge(vec_in, 48)
                take_hidden(0, 0)
                with act.Fori(0, TURNS - 1) as q:
                    for i in range(N3):
                        block_step(q, i, False)
                for i in range(N3):
                    block_step(TURNS - 1, i, True)

            @block.vector
            def _(dve):
                def take_x(q, i):
                    e = expert(dve, q, i)
                    dve.wait_ge(x_turned, n(q, i, 1, 1))
                    for k in range(KD):
                        ts = nc.vector.tensor_scalar(xT[i % N3][:, k, :], p_x[:, k, :], ln[:, e, k, 0:1],
                                                     ln[:, e, k, 1:2], ALU.mult, ALU.add)
                    ts.then_inc(xT_ready, 1)

                def take_hidden(q, i):
                    dve.wait_ge(h_mm, n(q, i, 2, 2))
                    nc.vector.tensor_copy(h[i % N3][:, TC:2 * TC], p_h[1][:]).then_inc(h_taken[1], 1)

                def block_step(q, i, last):
                    if not last or i + 1 < N3:
                        take_hidden(q, i + 1)
                    e = expert(dve, q, i)
                    dve.wait_ge(h_turned, n(q, i, 2, 2))
                    for k in range(KF // 2):
                        rl = nc.vector.tensor_scalar(hT[i][:, KF // 2 + k, :], p_t[1][:, k, :],
                                                     b1[:, bass.ds(e * KF + KF // 2 + k, 1)], 0.0, ALU.add, ALU.max)
                    rl.then_inc(hT_ready[1], 1)
                    if not last or i + 2 < N3:
                        take_x(q, i + 2)
                    dve.wait_ge(y_mm, n(q, i, 1, 1))
                    dve.wait_ge(y_out[i], PRIMED + q * 16)
                    nc.vector.tensor_tensor(y[i][:], p_y[:], b2[:, e, :], ALU.add).then_inc(y_ready, 1)

                dve.wait_ge(vec_in, 48)
                take_x(0, 0)
                take_x(0, 1)
                take_hidden(0, 0)
                with dve.Fori(0, TURNS - 1) as q:
                    for i in range(N3):
                        block_step(q, i, False)
                for i in range(N3):
                    block_step(TURNS - 1, i, True)


def finish(nc, S, D, keep):
    xn, alpha, slot = keep["xn"], keep["alpha"], keep["slot"]
    with Mem(nc) as m:
        f = [m.sb(f"s10_f{i}", [P, JT, DM]) for i in range(2)]
        R = NormRing(m, S, "s10")
        gathered = [S(f"gathered{i}") for i in range(2)]
        out_done = [S(f"out_done{i}") for i in range(2)]

        with nc.Block() as block:
            @block.sync
            def _(sp):
                prime(sp, [*out_done])
                with sp.Fori(0, NC - 1, 2) as c:
                    for par in range(2):
                        R.wait_normed(sp, c, par)
                        sp.dma_start(D["out"][0, bass.ds((c + par) * TC, TC), :].rearrange("(j p) n -> p j n", p=P),
                                     R.y[par][:]).then_inc(out_done[par], 16)
                for par in range(2):
                    sp.wait_ge(out_done[par], PRIMED + 16 * NC // 2)

            @block.gpsimd
            def _(pool):
                for t in range(TT):
                    par = t // JT % 2
                    if t >= 2 * JT:
                        pool.wait_ge(R.sum_ready, PRIMED + t - 2 * JT + 1)
                    pool.indirect_dma_start(f[par][:, t % JT, :], None, D["sorted_out"][:],
                                            bass.IndirectOffsetOnAxis(ap=slot[:, t:t + 1], axis=0)
                                            ).then_inc(gathered[par], 16)

            @block.scalar
            def _(act):
                act.wait_ge(R.eps_ready, 1)
                with act.Fori(0, NC - 1, 2) as c:
                    R.scalar_std(act, c, 0)
                    R.scalar_std(act, c, 1)

            @block.vector
            def _(dve):
                def add(c, n):
                    if n:
                        R.wait_free(dve, c, n)
                    dve.wait_ge(gathered[n % 2], c * (8 * JT) + (n // 2 + 1) * (16 * JT))
                    for j in range(JT):
                        t = c * JT + (n * JT + j)
                        nc.vector.scalar_tensor_tensor(
                            out=R.s[n % 2][:, j, :], in0=f[n % 2][:, j, :], scalar=alpha[:, bass.ds(t, 1)],
                            in1=xn[:, t, :], op0=ALU.mult, op1=ALU.add).then_inc(R.sum_ready, 1)
                    R.vector_stats(dve, c, n)

                def norm(c, n):
                    dve.wait_ge(out_done[n], PRIMED + c * 8)
                    R.vector_norm(dve, c, n)

                R.vector_setup(dve)
                add(0, 0)
                with dve.Fori(0, NC - 3, 2) as c:
                    add(c, 1)
                    norm(c, 0)
                    add(c, 2)
                    norm(c, 1)
                add(NC - 2, 1)
                norm(NC - 2, 0)
                norm(NC - 2, 1)


SCRATCH = {
    "sz": ((DI, L), F32), "u": ((DI, L), F32), "delta": ((DI, L), F32), "yz": ((DI, L), F32),
    "qk": ((2 * 3 * DM, L), BF16),
    "sorted_in": ((BLOCKS * P, DM), F32), "sorted_out": ((BLOCKS * P, DM), F32),
}


def build(nc, D, out):
    D = dict(D)
    D["out"] = out
    for name, (shape, dt) in SCRATCH.items():
        D[name] = nc.dram_tensor(name, shape, dt, kind="Internal").ap()
    with Mem(nc) as top:
        keep = {}
        with Mem(nc) as m:
            keep["bc_parts"] = m.sb("bc_parts", [3 * 2 * NS, L], BF16)
            with Mem(nc) as st:
                mixer_front(nc, st.sem, D, keep)
                st.clear_sems()
            with Mem(nc) as st:
                mixer_scan(nc, st.sem, D, keep)
                st.clear_sems()
        keep["xn"] = top.sb("xn", [P, TT, DM])
        keep["aff"] = top.sb("aff", [P, TT, E1])
        keep["alpha"] = top.sb("alpha", [P, TT])
        keep["slot"] = top.sb("slot", [P, TT], U32)
        keep["expert_of"] = top.sb("expert_of", [1, BLOCKS], I32)
        keep["w1_in"], keep["w2_in"] = top.sem("w1_in"), top.sem("w2_in")
        with Mem(nc) as ex:
            keep["att"] = ex.sb("att", [P, TT, DM])
            with Mem(nc) as v:
                keep["v_all"] = v.sb("v_all", [P, NH, TT, DH])
                with Mem(nc) as m:
                    keep["xt"] = m.sb("xt", [P, KD, L])
                    for n, stage in ((3, mixer_out), (4, adapter), (5, qkv)):
                        with Mem(nc) as st:
                            stage(nc, st.sem, D, keep)
                with Mem(nc) as st:
                    attention(nc, st.sem, D, keep)
            keep["w1"] = ex.sb("w1", [P, E1 * KD, DF])
            with Mem(nc) as st:
                attention_out(nc, st.sem, D, keep)
            keep["w2"] = ex.sb("w2", [P, E1 * KF, DM])
            with Mem(nc) as st:
                route(nc, st.sem, D, keep)
            with Mem(nc) as st:
                experts(nc, st.sem, D, keep)
        with Mem(nc) as st:
            finish(nc, st.sem, D, keep)


def lay_out(x):
    import numpy as np

    def T(a):
        return np.ascontiguousarray(a.T)
    X = x["L0_attn_x"][0]
    w_x = x["L0_attn_W_x"]
    a = {
        "xT": T(X), "x": np.ascontiguousarray(X),
        "w_in": T(x["L0_attn_W_in"]),
        "w_x": T(np.concatenate([w_x[RK:], w_x[:RK]])),
        "w_dt": T(x["L0_attn_W_dt"]),
        "mixer_vecs": np.concatenate([x["L0_attn_conv_w"][:, 0, :], x["L0_attn_conv_b"][:, None],
                                      x["L0_attn_b_dt"][:, None]], 1),
        "scan_vecs": np.concatenate([x["L0_attn_A_log"], x["L0_attn_D_param"][:, None]], 1),
        "w_out": T(x["L0_attn_W_out"]),
        "disc": np.concatenate([T(x["L0_ffn_disc_mu"]), T(x["L0_ffn_disc_sigma"])], 1),
        "base": T(x["L0_ffn_base_W"]), "base_b": x["L0_ffn_base_b"][None],
        "down": x["L0_ffn_down_W"], "down_b": x["L0_ffn_down_b"].reshape(-1, 1),
        "up": np.concatenate([x["L0_ffn_up_W"].transpose(0, 2, 1), x["L0_ffn_up_b"][:, :, None]], 2),
        "w_qk": np.concatenate([T(x["L1_attn_W_Q"]), T(x["L1_attn_W_K"])], 1), "w_v": T(x["L1_attn_W_V"]),
        "outm": x["L0_ffn_conv_W"].transpose(0, 2, 1), "outm_b": x["L0_ffn_conv_b"],
        "w_o": T(x["L1_attn_W_O"]), "cent": T(x["L1_ffn_centroids"]),
        "ln": np.stack([x["L1_ffn_ln_g"], x["L1_ffn_ln_b"]], -1).reshape(E1, KD, P, 2).transpose(2, 0, 1, 3),
        "w1": x["L1_ffn_w1"].transpose(0, 2, 1), "w2": x["L1_ffn_w2"].transpose(0, 2, 1),
        "b1": T(x["L1_ffn_b1"].reshape(E1 * KF, P)),
        "b2": np.broadcast_to(x["L1_ffn_b2"][None], (P, E1, DM)),
    }
    return {k: np.ascontiguousarray(v) for k, v in a.items()}


def kernel(**inputs):
    import numpy as np
    import concourse.bacc as _bacc
    from concourse.bass_utils import run_bass_kernel_spmd as _run

    arrays = lay_out({name: np.asarray(a) for name, a in inputs.items()})
    nc = _bacc.Bacc("TRN2", target_bir_lowering=False, num_devices=1)
    D = {n: nc.dram_tensor(f"in_{n}", a.shape, mybir.dt.from_np(a.dtype), kind="ExternalInput").ap()
         for n, a in arrays.items()}
    out = nc.dram_tensor("out", (1, L, DM), F32, kind="ExternalOutput").ap()
    build(nc, D, out)
    r = _run(nc, [{f"in_{n}": a for n, a in arrays.items()}], core_ids=[0])
    return r.results[0]["out"]
```
